# Optimizing a Trainium2 kernel written in Bass

```python
import numpy as np
import jax
import jax.numpy as jnp

def _softmax(x, axis=-1):
    return jax.nn.softmax(x, axis=axis)

def _gelu(x):
    return jax.nn.gelu(x, approximate=True)

def _silu(x):
    return jax.nn.silu(x)

def _sigmoid(x):
    return jax.nn.sigmoid(x)

def _layernorm(x, axis=-1, eps=1e-05):
    m = jnp.mean(x, axis=axis, keepdims=True)
    v = jnp.var(x, axis=axis, keepdims=True)
    return (x - m) / jnp.sqrt(v + eps)

def _scatter_add(tgt, idx, src, axis=0):
    return tgt.at[idx].add(src)

def _segment_sum(src, seg, n):
    return jax.ops.segment_sum(src, seg, n)
kernel_name = 'mk_vit_tower_cls_d1_tok_img768_r4_e47f2f'

def setup_inputs(seed: int=0):
    np.random.seed(seed)
    _w = jnp.asarray

    def _rec_inputs():
        import jax
        import jax.numpy as jnp
        _rk = jax.random.key(seed)
        x = -0.000596345 + 1.00056 * jax.random.normal(jax.random.fold_in(_rk, 1), (8, 3, 64, 64), jnp.float32)
        cls_tok = 0.02 * jax.random.normal(jax.random.fold_in(_rk, 5), (1, 1, 192), jnp.float32)
        return (x, cls_tok)
    x, cls_tok = _rec_inputs()

    def _L0_tok_setup():
        import jax, jax.numpy as jnp
        import numpy as np
        B = 16
        IMG = 64
        CH = 3
        EMBED = 64
        GP = 16
        PRE = [1, 2, 4]
        N_LEVELS = 3
        FUSED = EMBED * N_LEVELS

        def hilbert_flat_indices(n):
            t = np.arange(n * n, dtype=np.int64)
            x = np.zeros(n * n, dtype=np.int64)
            y = np.zeros(n * n, dtype=np.int64)
            s = 1
            while s < n:
                rx = 1 & t // 2
                ry = 1 & (t ^ rx)
                swap = ry == 0
                flip = swap & (rx == 1)
                x = np.where(flip, s - 1 - x, x)
                y = np.where(flip, s - 1 - y, y)
                x2 = np.where(swap, y, x)
                y2 = np.where(swap, x, y)
                x, y = (x2, y2)
                x = x + s * rx
                y = y + s * ry
                t = t // 4
                s *= 2
            return y * n + x

        def _level(x, idx, W, b, p, gp):
            Bsz, C, H, _ = x.shape
            h = H // p
            t = x.reshape(Bsz, C, h, p, h, p).transpose(0, 2, 4, 3, 5, 1).reshape(Bsz, h * h, p * p * C)
            t = t[:, idx]
            t = t.reshape(Bsz, h * h // gp, gp * p * p * C)
            return t @ W.T + b

        def _interp_linear(x, n_out):
            L = x.shape[1]
            pos = (jnp.arange(n_out, dtype=jnp.float32) + 0.5) * (L / n_out) - 0.5
            pos = jnp.clip(pos, 0.0, L - 1)
            i0 = jnp.floor(pos).astype(jnp.int32)
            i1 = jnp.minimum(i0 + 1, L - 1)
            w = (pos - i0).astype(x.dtype)
            return x[:, i0] * (1.0 - w)[None, :, None] + x[:, i1] * w[None, :, None]
        key = jax.random.key(seed)
        ks = jax.random.split(key, 9)
        inp = {'x': jax.random.normal(ks[0], (B, CH, IMG, IMG), jnp.float32)}
        for i, p in enumerate(PRE):
            din = CH * p * p * GP
            inp[f'W{i}'] = jax.random.normal(ks[1 + 2 * i], (EMBED, din), jnp.float32) * din ** (-0.5)
            inp[f'b{i}'] = jax.random.normal(ks[2 + 2 * i], (EMBED,), jnp.float32) * 0.02
        inp['Wf'] = jax.random.normal(ks[7], (FUSED, FUSED), jnp.float32) * FUSED ** (-0.5)
        inp['bf'] = jax.random.normal(ks[8], (FUSED,), jnp.float32) * 0.02
        for i, p in enumerate(PRE):
            inp[f'idx{i}'] = jnp.asarray(hilbert_flat_indices(IMG // p), jnp.int32)
        return inp
    _L0_tok_all = _L0_tok_setup()
    _L0_tok_in = {k: v for k, v in _L0_tok_all.items() if k in ('W0', 'b0', 'W1', 'b1', 'W2', 'b2', 'Wf', 'bf', 'idx0', 'idx1', 'idx2')}
    del _L0_tok_all

    def _L0_attn_setup():
        import jax, jax.numpy as jnp
        import numpy as np
        key = jax.random.key(seed)
        k0, k1, k2, k3, k4 = jax.random.split(key, 5)
        B, L, D, N = (4, 512, 192, 64)
        u = jax.random.normal(k0, (B, L, D), dtype=jnp.float32)
        A_real = -0.5 - 0.5 * jax.random.uniform(k1, (D, N), dtype=jnp.float32)
        A_imag = jax.random.normal(k2, (D, N), dtype=jnp.float32)
        B_mat = jax.random.normal(k3, (D, N), dtype=jnp.float32)
        C_mat = jax.random.normal(k4, (D, N), dtype=jnp.float32)
        log_delta = jnp.full((D,), np.log(0.1), dtype=jnp.float32)
        return {'u': u, 'A_real': A_real, 'A_imag': A_imag, 'B_mat': B_mat, 'C_mat': C_mat, 'log_delta': log_delta}
    _L0_attn_all = _L0_attn_setup()
    _L0_attn_in = {k: v for k, v in _L0_attn_all.items() if k in ('A_real', 'A_imag', 'B_mat', 'C_mat', 'log_delta')}
    del _L0_attn_all

    def _L0_ffn_setup():
        import jax, jax.numpy as jnp
        import numpy as np
        B, T, C = (2, 256, 192)
        H, NE, K = (768, 8, 2)
        key = jax.random.key(seed)
        k1, k2, k3, k4 = jax.random.split(key, 4)
        x = jax.random.normal(k1, (B, T, C), dtype=jnp.float32)
        w_fc = jax.random.normal(k2, (C, H * NE), dtype=jnp.float32) * 0.02
        w_proj = jax.random.normal(k3, (H * NE, C), dtype=jnp.float32) * (0.02 * (2 * 12) ** (-0.5))
        w_gate = jax.random.normal(k4, (C, NE), dtype=jnp.float32) * 0.02
        return {'x': x, 'w_fc': w_fc, 'w_proj': w_proj, 'w_gate': w_gate}
    _L0_ffn_all = _L0_ffn_setup()
    _L0_ffn_in = {k: v for k, v in _L0_ffn_all.items() if k in ('w_fc', 'w_proj', 'w_gate')}
    del _L0_ffn_all
    return {'x': x, 'cls_tok': cls_tok, 'L0_tok_W0': _L0_tok_in['W0'], 'L0_tok_b0': _L0_tok_in['b0'], 'L0_tok_W1': _L0_tok_in['W1'], 'L0_tok_b1': _L0_tok_in['b1'], 'L0_tok_W2': _L0_tok_in['W2'], 'L0_tok_b2': _L0_tok_in['b2'], 'L0_tok_Wf': _L0_tok_in['Wf'], 'L0_tok_bf': _L0_tok_in['bf'], 'L0_tok_idx0': _L0_tok_in['idx0'], 'L0_tok_idx1': _L0_tok_in['idx1'], 'L0_tok_idx2': _L0_tok_in['idx2'], 'L0_attn_A_real': _L0_attn_in['A_real'], 'L0_attn_A_imag': _L0_attn_in['A_imag'], 'L0_attn_B_mat': _L0_attn_in['B_mat'], 'L0_attn_C_mat': _L0_attn_in['C_mat'], 'L0_attn_log_delta': _L0_attn_in['log_delta'], 'L0_ffn_w_fc': _L0_ffn_in['w_fc'], 'L0_ffn_w_proj': _L0_ffn_in['w_proj'], 'L0_ffn_w_gate': _L0_ffn_in['w_gate']}

def reference(x, cls_tok, L0_tok_W0, L0_tok_b0, L0_tok_W1, L0_tok_b1, L0_tok_W2, L0_tok_b2, L0_tok_Wf, L0_tok_bf, L0_tok_idx0, L0_tok_idx1, L0_tok_idx2, L0_attn_A_real, L0_attn_A_imag, L0_attn_B_mat, L0_attn_C_mat, L0_attn_log_delta, L0_ffn_w_fc, L0_ffn_w_proj, L0_ffn_w_gate):
    import jax
    import jax.numpy as jnp

    def _L0_tok_ref(x, W0, b0, W1, b1, W2, b2, Wf, bf, idx0, idx1, idx2):
        import jax, jax.numpy as jnp
        import numpy as np
        B = 16
        IMG = 64
        CH = 3
        EMBED = 64
        GP = 16
        PRE = [1, 2, 4]
        N_LEVELS = 3
        FUSED = EMBED * N_LEVELS

        def hilbert_flat_indices(n):
            t = np.arange(n * n, dtype=np.int64)
            x = np.zeros(n * n, dtype=np.int64)
            y = np.zeros(n * n, dtype=np.int64)
            s = 1
            while s < n:
                rx = 1 & t // 2
                ry = 1 & (t ^ rx)
                swap = ry == 0
                flip = swap & (rx == 1)
                x = np.where(flip, s - 1 - x, x)
                y = np.where(flip, s - 1 - y, y)
                x2 = np.where(swap, y, x)
                y2 = np.where(swap, x, y)
                x, y = (x2, y2)
                x = x + s * rx
                y = y + s * ry
                t = t // 4
                s *= 2
            return y * n + x

        def _level(x, idx, W, b, p, gp):
            Bsz, C, H, _ = x.shape
            h = H // p
            t = x.reshape(Bsz, C, h, p, h, p).transpose(0, 2, 4, 3, 5, 1).reshape(Bsz, h * h, p * p * C)
            t = t[:, idx]
            t = t.reshape(Bsz, h * h // gp, gp * p * p * C)
            return t @ W.T + b

        def _interp_linear(x, n_out):
            L = x.shape[1]
            pos = (jnp.arange(n_out, dtype=jnp.float32) + 0.5) * (L / n_out) - 0.5
            pos = jnp.clip(pos, 0.0, L - 1)
            i0 = jnp.floor(pos).astype(jnp.int32)
            i1 = jnp.minimum(i0 + 1, L - 1)
            w = (pos - i0).astype(x.dtype)
            return x[:, i0] * (1.0 - w)[None, :, None] + x[:, i1] * w[None, :, None]
        Ws = [(idx0, W0, b0, PRE[0]), (idx1, W1, b1, PRE[1]), (idx2, W2, b2, PRE[2])]
        outs = [_level(x, idx, W, b, p, GP) for idx, W, b, p in Ws]
        n_tokens = outs[0].shape[1]
        outs = [outs[0]] + [_interp_linear(o, n_tokens) for o in outs[1:]]
        y = jnp.concatenate(outs, axis=-1)
        return y @ Wf.T + bf

    def _L0_attn_ref(u, A_real, A_imag, B_mat, C_mat, log_delta):
        import jax, jax.numpy as jnp
        import numpy as np
        Bsz, L, D = u.shape
        delta = jax.nn.softplus(log_delta)
        A = A_real + 1j * A_imag
        dA = delta[:, None] * A
        A_bar = jnp.exp(dA)
        B_bar = (A_bar - 1.0) / A * B_mat
        CB = C_mat.astype(B_bar.dtype) * B_bar
        ell = jnp.arange(L, dtype=jnp.float32)
        P = jnp.exp(dA[:, :, None] * ell[None, None, :])
        K = jnp.einsum('dn,dnl->dl', CB, P).real
        n_fft = 2 * L
        Uf = jnp.fft.rfft(u, n=n_fft, axis=1)
        Kf = jnp.fft.rfft(K, n=n_fft, axis=1)
        y = jnp.fft.irfft(Uf * Kf.T[None, :, :], n=n_fft, axis=1)[:, :L, :]
        return y.astype(u.dtype)

    def _L0_ffn_ref(x, w_fc, w_proj, w_gate):
        import jax, jax.numpy as jnp
        import numpy as np
        B, T, C = (2, 256, 192)
        H, NE, K = (768, 8, 2)
        router_logits = jnp.einsum('btc,ce->bte', x, w_gate)
        router_probs = jax.nn.softmax(router_logits, axis=-1)
        top_p, top_i = jax.lax.top_k(router_probs, K)
        top_p = top_p / jnp.sum(top_p, axis=-1, keepdims=True)
        wf = w_fc.reshape(C, H, NE)
        h_all = jnp.einsum('btc,che->bthe', x, wf)
        h = jnp.take_along_axis(h_all, top_i[:, :, None, :], axis=-1)
        h = jax.nn.gelu(h, approximate=True)
        wp = w_proj.reshape(H, C, NE)
        o_all = jnp.einsum('bthk,hce->btcke', h, wp)
        o = jnp.take_along_axis(o_all, top_i[:, :, None, :, None], axis=-1)[..., 0]
        o = jnp.einsum('btck,btk->btc', o, top_p)
        return o
    h = _L0_tok_ref(x, L0_tok_W0, L0_tok_b0, L0_tok_W1, L0_tok_b1, L0_tok_W2, L0_tok_b2, L0_tok_Wf, L0_tok_bf, L0_tok_idx0, L0_tok_idx1, L0_tok_idx2)
    h = jnp.concatenate([jnp.broadcast_to(cls_tok, (h.shape[0], 1, h.shape[2])), h], axis=1)
    h = h + _L0_attn_ref(_layernorm(h, axis=-1), L0_attn_A_real, L0_attn_A_imag, L0_attn_B_mat, L0_attn_C_mat, L0_attn_log_delta)
    h = h + _L0_ffn_ref(_layernorm(h, axis=-1), L0_ffn_w_fc, L0_ffn_w_proj, L0_ffn_w_gate)
    return h

_drawn_inputs = setup_inputs


def setup_inputs(seed=0):
    import zlib

    import numpy as np

    out = dict(_drawn_inputs(seed))
    spreads = {'L0_attn_log_delta': (-2.3025851249694824, 0.2)}
    factors = {'L0_tok_b0': 2.699,
     'L0_tok_b1': 2.833,
     'L0_ffn_w_fc': 8.0,
     'L0_ffn_w_proj': 8.0,
     'L0_ffn_w_gate': 8.0}
    for name, (base, spread) in spreads.items():
        noise = np.random.default_rng([zlib.crc32(name.encode()), seed]).standard_normal(out[name].shape)
        drawn = base * np.exp(spread * noise) if base else spread * noise
        out[name] = jnp.asarray(drawn.astype(out[name].dtype))
    for name, factor in factors.items():
        out[name] = (out[name] * factor).astype(out[name].dtype)
    return out
```

```python
import numpy as np
from contextlib import ExitStack

import concourse.bass as bass
from concourse import mybir

F32 = mybir.dt.float32
BF16 = mybir.dt.bfloat16
I32 = mybir.dt.int32
U32 = mybir.dt.uint32
ALU = mybir.AluOpType
ACT = mybir.ActivationFunctionType
AX = mybir.AxisListType

P = 128
B, CH, IMG = 8, 3, 64
D = 192
EMB = 64
GP = 16
NT = 256
L = NT + 1
D2 = D - P
NS = 64
TA, TB = 33, 8
NF = 256
NFFT = 2 * NF
KT = 4
H, NE = 768, 8
HT = H // P
TILES = 2 * B + 1
ROWS = B * L
NBLK = (2 * ROWS + NE * (P - 1)) // P
XW = D + NE
EPS = 1e-5
MAGIC = 1.5 * 2.0 ** 23
TWO_PI = 6.2831845
LOWEST = -3.0e38
assert NBLK == 40 and NBLK % 2 == 0

_WIDTHS = [("ident", P), ("ltri", P), ("iota_s", P), ("iota_b", NBLK), ("off", 5), ("ids", 2 * TILES * 3),
           ("valid", TILES), ("ew", NE), ("eidx", NE), ("sgn", B * B), ("w4", 4), ("w16", 16), ("row0", B)]
COL = {}
_at = 0
for _name, _w in _WIDTHS:
    COL[_name] = (_at, _at + _w)
    _at += _w
NCONST = _at


def shape_constants():
    c = np.zeros((P, NCONST), np.float32)

    def put(name, a):
        c[:, COL[name][0]:COL[name][1]] = a

    p = np.arange(P)
    put("ident", np.eye(P))
    put("ltri", p[:, None] < p[None, :])
    put("iota_s", p[None, :])
    put("iota_b", np.arange(NBLK)[None, :])
    low = (p < NS)[:, None]
    put("off", np.where(low, [[0.25, 0.25, 0.5, 0.25, 0.0]], [[0.0, 0.5, 0.75, 0.25, 0.0]]))
    rows = np.zeros((P, TILES), np.int64)
    valid = np.ones((P, TILES))
    for j in range(2 * B):
        rows[:, j] = (j % B) * L + P * (j // B) + p
    rows[:B, 2 * B] = p[:B] * L + NT
    valid[B:, 2 * B] = 0
    ids = np.stack([rows % 256, rows // 256, valid], -1) * valid[:, :, None]
    put("ids", np.concatenate([ids, ids], 1).reshape(P, -1))
    put("valid", valid)
    put("ew", NE - np.arange(NE)[None, :])
    put("eidx", np.arange(NE)[None, :])
    sgn = np.zeros((P, B, B))
    for b in range(B):
        sgn[:, b, b] = -(2.0 / NFFT) * (-1.0) ** p
    put("sgn", sgn.reshape(P, -1))
    put("w4", (np.arange(4) + 0.5)[None, :] / 4)
    put("w16", (np.arange(16) + 0.5)[None, :] / 16)
    put("row0", (p == 0)[:, None] * np.ones((1, B)))

    k = np.arange(NF)

    def angle(l):
        return np.pi * (((2 * k[None, :] + 1) * l[:, None]) % (2 * NFFT)) / NFFT

    def forward(l):
        return np.concatenate([np.cos(angle(l)), -np.sin(angle(l))], 1)

    fwd = forward(np.arange(NT)).reshape(2, P, NFFT).transpose(1, 0, 2)
    lk = TB * np.arange(TA)[:, None] + np.arange(TB)[None, :]
    fk = forward(lk.reshape(-1)).reshape(TA, TB, NFFT) * (lk < L)[:, :, None]
    inv = (2.0 / NFFT) * forward(np.arange(NT)).T.reshape(KT, P, NT).transpose(1, 0, 2)
    ones = np.zeros((2, B, L))
    ones[0, :, 1:] = 1
    ones[1, :, 0] = 1
    f = lambda a: np.ascontiguousarray(a, np.float32)
    return {"consts": c, "fwd": f(fwd), "fwd_k": f(fk), "inv": f(inv), "ones_rows": f(ones.reshape(2, -1))}


class Chain:

    def __init__(self, eng, s):
        self.eng, self.s, self.n = eng, s, 0

    def inc(self, ins):
        ins.then_inc(self.s, 1)
        self.n += 1

    def sync(self):
        self.eng.wait_ge(self.s, self.n)

    def link(self, ins):
        self.inc(ins)
        self.sync()


def bc(ap, axis, n):
    v = ap.unsqueeze(axis)
    shape = list(v.shape)
    shape[axis] = n
    return v.broadcast_to(shape)


def vit_layer(nc, t, out):
    with ExitStack() as ctx:
        def sb(name, shape, dt=F32):
            return ctx.enter_context(nc.sbuf_tensor(name, shape, dt))

        def sem(name):
            return ctx.enter_context(nc.semaphore(name))

        x_rows = nc.dram_tensor("x_rows", [ROWS, XW], F32, kind="Internal").ap()
        out_rows = out.rearrange("b l d -> (b l) d")

        cst = sb("cst", [P, NCONST])
        C = {n: cst[:, a:b] for n, (a, b) in COL.items()}
        ident = C["ident"]
        fwd = sb("fwd_sb", [P, 2, NFFT])
        inv = sb("inv_sb", [P, KT, NT])
        id0 = sb("id0_sb", [P, 2 * GP], I32)
        id1 = sb("id1_sb", [P, 8], I32)
        id2 = sb("id2_sb", [P, 2], I32)
        w0 = sb("w0_sb", [48, EMB])
        w1 = sb("w1_sb", [96, 2, EMB])
        tb = sb("tb_sb", [EMB, 3])
        wfa = sb("wfa", [P, D])
        wfb = sb("wfb", [D2 + 2, D])
        wga = sb("wga", [P, NE])
        wgb = sb("wgb", [D2, NE])
        khat = sb("khat", [P, KT, D])
        k0 = sb("k0", [B, D])
        hroom = sb("hroom", [P, 2 * B * D])
        h_last = sb("h_last", [B, D])
        uroom = sb("uroom", [P, 2 * B * D])
        u_last = sb("u_last", [B, D])
        stats = sb("stats", [P, TILES, 6])
        mv = sb("mv", [P, TILES, 2])
        rstd = sb("rstd", [P, TILES])
        veps = sb("veps", [P, TILES])
        mhalf = sb("mhalf", [P, TILES])
        lg = sb("lg", [P, TILES, NE])
        oh1 = sb("oh1", [P, TILES, NE])
        oh2 = sb("oh2", [P, TILES, NE])
        rt = sb("rt", [P, 3, TILES, NE])
        rs = sb("rs", [P, 12, TILES])
        ohb16 = sb("ohb16", [P, TILES + 1, NE], BF16)
        ltri16 = sb("ltri16", [P, P], BF16)
        ones16 = sb("ones16", [P, P], BF16)
        cnt = sb("cnt", [P, 6, NE])
        cnt_i = sb("cnt_i", [P, NE], I32)
        pos = sb("pos", [P, 2, TILES])
        pos_i = sb("pos_i", [P, 2, TILES], I32)
        blk_i = sb("blk_i", [P, 2, TILES], I32)
        slt_i = sb("slt_i", [P, 2, TILES], I32)
        blk_f = sb("blk_f", [P, 2 * TILES])
        slt_f = sb("slt_f", [P, 2 * TILES])
        blk_e = sb("blk_e", [P, NBLK])
        blk_ei = sb("blk_ei", [P, NBLK], I32)
        idx_f = sb("idx_f", [P, NBLK])
        idx = sb("idx", [P, NBLK], I32)
        gcol = sb("gcol", [P, 4], I32)
        scol = sb("scol", [P, 4], I32)
        slotv = sb("slotv", [P, 3 * NBLK])
        gsel = sb("gsel", [P, 2, NE])
        gate = sb("gate", [P, 2])

        def view(base, at, shape):
            n = int(np.prod(shape[1:]))
            v = base[0:shape[0], at:at + n]
            names = "abcd"[:len(shape) - 1]
            if len(names) > 1:
                v = v.rearrange(f"p ({' '.join(names)}) -> p {' '.join(names)}",
                                **{c: s for c, s in zip(names[1:], shape[2:])})
            return v, at + n

        u, _ = view(uroom, 0, [P, 2, B, D])
        h, _ = view(hroom, 0, [P, 2, B, D])
        byb1, at = view(hroom, 0, [P, B, 8, 12])
        byb0, at = view(hroom, at, [P, 2, B, GP * CH])
        assert at <= 2 * B * D
        w2, _ = view(uroom, 0, [48, GP, EMB])
        n_fc = NE * H
        wroom = sb("wroom", [P, 2 * n_fc + NE * HT * D])
        wfc_a = wroom[:, 0:n_fc]
        wfc_b = wroom[0:D2, n_fc:2 * n_fc]
        wpj = wroom[:, 2 * n_fc:]
        ytab, at = view(wroom, 0, [P, 2, TB, D])
        ye, at = view(wroom, at, [P, TB, D])
        ksb, at = view(wroom, at, [TA, D, TB])
        assert at <= n_fc
        fwd_k, at = view(wroom, n_fc, [TA, TB, NFFT])
        t2, at = view(wroom, at, [48, 2, B, P])
        assert at <= 2 * n_fc
        xtab, at = view(wroom, 2 * n_fc, [P, TA, D])
        xe, at = view(wroom, at, [P, TA // 3, D])
        assert at <= 2 * n_fc + NE * HT * D

        SROOM = 18700
        sroom = sb("sroom", [P, SROOM])
        sm, at = view(sroom, 0, [P, 12, D])
        ssm, at = view(sroom, at, [P, 5, D])
        trig1, at = view(sroom, at, [P, 2, D])
        scr, at = view(sroom, at, [P, TA // 3, D])
        raw2, at = view(sroom, at, [P, 2, B * 48])
        raw1, at = view(sroom, at, [P, 8, B * 12])
        raw0, at = view(sroom, at, [P, 2, GP * B * 3])
        t1, at = view(sroom, at, [96, B, P])
        t0, at = view(sroom, at, [48, 2, B, P])
        p1, at = view(sroom, at, [EMB, B, 66])
        p2, at = view(sroom, at, [EMB, B, 18])
        d1, at = view(sroom, at, [EMB, B, 65])
        d2, at = view(sroom, at, [EMB, B, 17])
        itmp, at = view(sroom, at, [EMB, B, 252])
        ya, at = view(sroom, at, [P, B, L])
        yb, at = view(sroom, at, [D2 + 2, B, L])
        assert at <= SROOM, at
        yhat, at = view(sroom, 0, [P, KT, B, D])
        prod_at = at
        prod, at = view(sroom, at, [P, 2, KT, 4 * D])
        xg, at = view(sroom, at, [P, TILES, XW])
        k0u, at = view(sroom, at, [B, D])
        assert at <= SROOM, at
        ohs_f, at = view(sroom, prod_at, [P, TILES * P])
        ohs = ohs_f.bitcast(BF16).rearrange("p (k s) -> p k s", s=P)
        ohb_f, at = view(sroom, at, [P, TILES * NBLK])
        ohb = ohb_f.bitcast(BF16).rearrange("p (k s) -> p k s", s=NBLK)
        mvb_f, at = view(sroom, at, [P, 3 * TILES * NBLK])
        mvb = mvb_f.bitcast(BF16).rearrange("p (k c s) -> p k c s", c=3, s=NBLK)
        assert at <= prod_at + 2 * KT * 4 * D
        xta, at = view(sroom, 0, [P, TILES, P])
        xtb, at = view(sroom, at, [D2, TILES, P])
        assert at <= prod_at
        gsel_e, at = view(sroom, 0, [P, NBLK, NE])
        ge_t, at = view(sroom, at, [P, NBLK, NE])
        xs, at = view(sroom, at, [P, 4, XW])
        bta, at = view(sroom, at, [P, 2, P])
        btb, at = view(sroom, at, [D2, 2, P])
        hs, at = view(sroom, at, [P, 2, H])
        hT, at = view(sroom, at, [P, 2, H])
        o_sb, at = view(sroom, at, [P, 2, D])
        assert at <= prod_at

        delta, rate, turn = sm[:, 9], sm[:, 10], sm[:, 11]
        T0_BANK = (5, 0)
        Y0_BANK = ((7, 5), (2, 6))
        ps = ctx.enter_context(nc.psum_tensor("ps", [P, 8, 512], F32))
        pf = ps[:, :, :].rearrange("p k n -> p (k n)")

        idx_in, ssm_in, const_in, tokw_in = sem("idx_in"), sem("ssm_in"), sem("const_in"), sem("tokw_in")
        four_in, yrows_in, exp_in = sem("four_in"), sem("yrows_in"), sem("exp_in")
        raw2_in, raw1_in = sem("raw2_in"), sem("raw1_in")
        byb1_ready, byb0_ready = sem("byb1_ready"), sem("byb0_ready")
        raw0_in = [sem("raw0a_in"), sem("raw0b_in")]
        vec_own = sem("vec_own")
        edge_zero = sem("edge_zero")
        abs_ready, e_ready, w_ready, ln_ready = sem("abs_ready"), sem("e_ready"), sem("w_ready"), sem("ln_ready")
        rate_ready = sem("rate_ready")
        env1_ready, turn1_ready, frac1_ready, sin1_ready = (sem("env1_ready"), sem("turn1_ready"),
                                                            sem("frac1_ready"), sem("sin1_ready"))
        yenv_ready, yturn_ready, yfrac_ready, ysin_ready, ytab_ready = (
            sem("yenv_ready"), sem("yturn_ready"), sem("yfrac_ready"), sem("ysin_ready"), sem("ytab_ready"))
        xenv_ready, xturn_ready, xfrac_ready, xsin_ready, xtab_ready = (
            sem("xenv_ready"), sem("xturn_ready"), sem("xfrac_ready"), sem("xsin_ready"), sem("xtab_ready"))
        kps_ready, ksb_ready, khat_ps, khat_ready = (sem("kps_ready"), sem("ksb_ready"), sem("khat_ps"),
                                                     sem("khat_ready"))
        t2_ps, t2_sb, t1_ps, t1_sb = sem("t2_ps"), sem("t2_sb"), sem("t1_ps"), sem("t1_sb")
        y2_ps, y2_sb, y1_ps, y1_sb, y12_done = (sem("y2_ps"), sem("y2_sb"), sem("y1_ps"), sem("y1_sb"),
                                                sem("y12_done"))
        t0_ps, t0_sb, y0_ps, y0_sb = sem("t0_ps"), sem("t0_sb"), sem("y0_ps"), sem("y0_sb")
        h_ps, h_sb, u_ready = sem("h_ps"), sem("h_sb"), sem("u_ready")
        uhat_ps, prod_ready, yhat_ready = sem("uhat_ps"), sem("prod_ready"), sem("yhat_ready")
        y_ps, h2_ready, x_ready = sem("y_ps"), sem("h2_ready"), sem("x_ready")
        xt_ps, xt_sb, logit_ps = sem("xt_ps"), sem("xt_sb"), sem("logit_ps")
        gap_ready, gexp_ready, gates_ready = sem("gap_ready"), sem("gexp_ready"), sem("gates_ready")
        cast_ready, oh_ready, rank_ps, pick_ready, slot_ps = (sem("cast_ready"), sem("oh_ready"), sem("rank_ps"),
                                                              sem("pick_ready"), sem("slot_ps"))
        expert_ready, idx_ready = sem("expert_ready"), sem("idx_ready")
        base_out, x_out = sem("base_out"), sem("x_out")
        added, xs_clear = sem("added"), sem("xs_clear")
        xs_in = [sem(f"xs_in{i}") for i in range(4)]
        bt_ps, bt_sb, fc_ps, gelu_ready = sem("bt_ps"), sem("bt_sb"), sem("fc_ps"), sem("gelu_ready")
        ht_ps, ht_sb, pj_ps, o_ready = sem("ht_ps"), sem("ht_sb"), sem("pj_ps"), sem("o_ready")
        gate_seen = sem("gate_seen")

        veps_ready, rstd_ready = sem("veps_ready"), sem("rstd_ready")
        ROOTS = ([(P, ((0, 8),)), (P, ((8, 16),)), (B, ((16, 17),))]
                 + [(P, ((2 * c, 2 * c + 2), (8 + 2 * c, 10 + 2 * c))) for c in range(B // 2)] + [(B, ((16, 17),))])

        block = ctx.enter_context(nc.Block())

        @block.sync
        def _(sp):
            sp.dma_start(id2[:, :], t["id2"]).then_inc(idx_in, 16)
            sp.dma_start(id1[:, :], t["id1"]).then_inc(idx_in, 16)
            sp.dma_start(id0[:, :], t["id0"]).then_inc(idx_in, 16)
            for n, name in enumerate(("a_real", "a_imag", "b_mat", "c_mat")):
                for half in range(2):
                    sp.dma_start(ssm[NS * half:NS * half + NS, n, :], t[name]).then_inc(ssm_in, 16)
            sp.dma_start(w2[:, :, :], t["w2"]).then_inc(tokw_in, 16)
            sp.dma_start(w1[:, :, :], t["w1"]).then_inc(tokw_in, 16)
            sp.dma_start(w0[:, :], t["w0"]).then_inc(tokw_in, 16)
            sp.dma_start(tb[:, :], t["tb"]).then_inc(tokw_in, 16)
            sp.dma_start(wfa[:, :], t["wf"][0:P, :]).then_inc(tokw_in, 16)
            sp.dma_start(wfb[0:D2, :], t["wf"][P:D, :]).then_inc(tokw_in, 16)
            sp.dma_start(wfb[D2:D2 + 1, :], t["bf"]).then_inc(tokw_in, 16)
            sp.dma_start(wfb[D2 + 1:D2 + 2, :], t["cls"]).then_inc(tokw_in, 16)
            sp.dma_start(yb[D2:D2 + 2, :, :], t["ones_rows"].rearrange("r (b l) -> r b l", b=B)).then_inc(tokw_in, 16)
            sp.dma_start(fwd_k[:, :, :], t["fwd_k"]).then_inc(four_in, 16)
            sp.dma_start(fwd[:, :, :], t["fwd"]).then_inc(four_in, 16)
            sp.dma_start(inv[:, :, :], t["inv"]).then_inc(four_in, 16)
            sp.dma_start(wga[:, :], t["w_gate"][0:P, :]).then_inc(four_in, 16)
            sp.dma_start(wgb[:, :], t["w_gate"][P:D, :]).then_inc(four_in, 16)
            sp.wait_ge(khat_ps, 1)
            sp.dma_start(wfc_a, t["w_fc"][0:P, :]).then_inc(exp_in, 16)
            sp.dma_start(wfc_b, t["w_fc"][P:D, :]).then_inc(exp_in, 16)
            sp.dma_start(wpj, t["w_proj"]).then_inc(exp_in, 16)
            sp.wait_ge(h2_ready, 2 * B + 1)
            for lt in range(2):
                sp.dma_start(out[:, P * lt:P * lt + P, :].rearrange("b l d -> l b d"), h[:, lt]).then_inc(base_out, 16)
            sp.dma_start(out[:, NT, :], h_last[:, :]).then_inc(base_out, 16)
            rows = x_rows.rearrange("(b l) w -> l b w", b=B)
            sp.wait_ge(gates_ready, 1)
            for lt in range(2):
                sp.dma_start(rows[P * lt:P * lt + P], xg[:, B * lt:B * lt + B, :]).then_inc(x_out, 16)
            sp.dma_start(rows[NT], xg[0:B, 2 * B, :]).then_inc(x_out, 16)
            sp.wait_ge(base_out, 48)
            sp.wait_ge(x_out, 48)

        @block.gpsimd
        def _(pool):
            nc.gpsimd.memset(ya[:, :, 0:1], 0.0).then_inc(edge_zero, 1)
            nc.gpsimd.memset(yb[0:D2, :, 0:1], 0.0).then_inc(edge_zero, 1)
            nc.gpsimd.memset(mhalf[:, :], -0.5).then_inc(edge_zero, 1)
            pool.wait_ge(idx_in, 48)
            for q in range(2):
                nc.gpsimd.indirect_dma_start(raw2[:, q, :], None, t["px2"], bass.IndirectOffsetOnAxis(
                    ap=id2[:, q:q + 1].bitcast(U32), axis=0)).then_inc(raw2_in, 16)
            for g in range(8):
                nc.gpsimd.indirect_dma_start(raw1[:, g, :], None, t["px1"], bass.IndirectOffsetOnAxis(
                    ap=id1[:, g:g + 1].bitcast(U32), axis=0)).then_inc(raw1_in, 16)
            for half in range(2):
                for g in range(GP):
                    nc.gpsimd.indirect_dma_start(
                        raw0[:, half, g * B * 3:(g + 1) * B * 3], None, t["px0"], bass.IndirectOffsetOnAxis(
                            ap=id0[:, half * GP + g:half * GP + g + 1].bitcast(U32), axis=0)).then_inc(raw0_in[half], 16)
            def root(n):
                np_, tiles = ROOTS[n]
                pool.wait_ge(veps_ready, n + 1)
                for j0, j1 in tiles:
                    ins = nc.gpsimd.tensor_tensor(rstd[0:np_, j0:j1], veps[0:np_, j0:j1], mhalf[0:np_, j0:j1], ALU.pow)
                ins.then_inc(rstd_ready, 1)

            pool.wait_ge(edge_zero, 3)
            for n in range(3):
                root(n)
            for c in range(B // 2):
                pool.wait_ge(prod_ready, c + 1)
                pr = prod[:, c % 2].rearrange("p k (f n) -> p k f n", f=2)
                for part, op in ((0, ALU.subtract), (1, ALU.add)):
                    dst = yhat[:, 2 * part:2 * part + 2, 2 * c:2 * c + 2, :].rearrange("p f b d -> p f (b d)")
                    last = nc.gpsimd.tensor_tensor(dst, pr[:, 2 * part], pr[:, 2 * part + 1], op)
                last.then_inc(yhat_ready, 1)
            for n in range(3, 8):
                root(n)

            def gather(q, r):
                nc.gpsimd.indirect_dma_start(xs[:, r, :], None, x_rows, bass.IndirectOffsetOnAxis(
                    ap=gcol[:, r:r + 1].bitcast(U32), axis=0), bounds_check=ROWS - 1,
                    oob_is_err=False).then_inc(xs_in[r], 16)

            def step(q, r, more=True, first=False):
                i = 4 * q + r + 1
                if not isinstance(i, int):
                    i, blocks_out, rows_added = pool.to_reg(i), pool.to_reg(i + 1), pool.to_reg(16 * i)
                else:
                    blocks_out, rows_added = i + 1, 16 * i
                if more:
                    pool.wait_ge(idx_ready, 1)
                    pool.wait_ge(o_ready, i)
                    gather(q + 1, r)
                pool.wait_ge(idx_ready, 1)
                pool.wait_ge(o_ready, blocks_out)
                pool.wait_ge(added, rows_added)
                scatter((r + 1) % 4, (r + 1) % 2)

            def scatter(r, par):
                nc.gpsimd.indirect_dma_start(out_rows, bass.IndirectOffsetOnAxis(
                    ap=scol[:, r:r + 1].bitcast(U32), axis=0), o_sb[:, par, :], None, bounds_check=ROWS - 1,
                    oob_is_err=False, compute_op=ALU.add).then_inc(added, 16)

            pool.wait_ge(idx_ready, 1)
            pool.wait_ge(xs_clear, 1)
            pool.wait_ge(x_out, 48)
            for r in range(4):
                gather(0, r)
            pool.wait_ge(base_out, 48)
            pool.wait_ge(o_ready, 1)
            scatter(0, 0)
            with pool.Fori(0, NBLK // 4 - 1) as q:
                for r in range(4):
                    step(q, r)
            for r in range(3):
                step(NBLK // 4 - 1, r, more=False)
            pool.wait_ge(added, 16 * NBLK)

        @block.scalar
        def _(act):
            act.dma_start(ssm[:, 4, :], t["log_delta"].partition_broadcast(P)).then_inc(ssm_in, 16)
            act.dma_start(cst[:, :], t["consts"]).then_inc(const_in, 16)

            act.wait_ge(abs_ready, 1)
            nc.scalar.activation(sm[:, 1], sm[:, 0], ACT.Exp, scale=-1.0).then_inc(e_ready, 1)
            act.wait_ge(w_ready, 1)
            nc.scalar.activation(sm[:, 3], sm[:, 2], ACT.Ln).then_inc(ln_ready, 1)
            act.wait_ge(rate_ready, 1)
            nc.scalar.activation(sm[:, 8], rate, ACT.Exp).then_inc(env1_ready, 1)
            for b in range(TB):
                ins = nc.scalar.activation(ye[:, b], rate, ACT.Exp, scale=float(b))
            ins.then_inc(yenv_ready, 1)
            for a in range(TA):
                ins = nc.scalar.activation(xtab[:, a], rate, ACT.Exp, scale=float(TB * a))
            ins.then_inc(xenv_ready, 1)

            act.wait_ge(const_in, 16)
            for v in range(2):
                ins = nc.scalar.activation(trig1[:, v], turn, ACT.Identity, bias=C["off"][:, 3 + v:4 + v])
            ins.then_inc(turn1_ready, 1)
            for v in range(2):
                for b in range(TB):
                    ins = nc.scalar.activation(ytab[:, v, b], turn, ACT.Identity, scale=float(b),
                                               bias=C["off"][:, 1 + v:2 + v])
                ins.then_inc(yturn_ready, 1)
            for k in range(3):
                if k:
                    act.wait_ge(xtab_ready, k)
                for a in range(TA // 3):
                    ins = nc.scalar.activation(xe[:, a], turn, ACT.Identity, scale=float(TB * (k * TA // 3 + a)),
                                               bias=C["off"][:, 0:1])
                ins.then_inc(xturn_ready, 1)
                if k == 0:
                    act.wait_ge(raw1_in, 16 * 8)
                    nc.scalar.activation(byb1, raw1.rearrange("p g (b c) -> p b g c", b=B),
                                         ACT.Copy).then_inc(byb1_ready, 1)
                    act.wait_ge(frac1_ready, 1)
                    nc.scalar.activation(trig1[:, :], trig1[:, :], ACT.Sin, scale=TWO_PI).then_inc(sin1_ready, 1)
                    for v in range(2):
                        act.wait_ge(yfrac_ready, v + 1)
                        nc.scalar.activation(ytab[:, v], ytab[:, v], ACT.Sin, scale=TWO_PI).then_inc(ysin_ready, 1)
                act.wait_ge(xfrac_ready, k + 1)
                nc.scalar.activation(xe[:, :], xe[:, :], ACT.Sin, scale=TWO_PI).then_inc(xsin_ready, 1)
                if k == 0:
                    act.wait_ge(tokw_in, 16 * 9)
                    act.wait_ge(y2_ps, 1)
                    nc.scalar.activation(p2[:, :, 1:17], ps[0:EMB, 7, 0:B * 16].rearrange("p (b s) -> p b s", b=B),
                                         ACT.Identity, bias=tb[:, 2:3]).then_inc(y2_sb, 1)
                    act.wait_ge(y1_ps, 1)
                    nc.scalar.activation(p1[:, :, 1:65], ps[0:EMB, 6, 0:512].rearrange("p (b s) -> p b s", b=B),
                                         ACT.Identity, bias=tb[:, 1:2]).then_inc(y1_sb, 1)

            def level0(half):
                act.wait_ge(raw0_in[half], 16 * GP)
                nc.scalar.activation(byb0[:, half].rearrange("p b (g c) -> p b g c", g=GP),
                                     raw0[:, half].rearrange("p (g b c) -> p b g c", g=GP, b=B),
                                     ACT.Copy).then_inc(byb0_ready, 1)
                act.wait_ge(t0_ps, half + 1)
                k = T0_BANK[half] * 512
                nc.scalar.activation(t0[:, half].rearrange("p b s -> p (b s)"), pf[0:48, k:k + 1024],
                                     ACT.Copy).then_inc(t0_sb, 1)
                for c in range(2):
                    act.wait_ge(y0_ps, 2 * half + c + 1)
                    nc.scalar.activation(
                        ya[0:EMB, 4 * c:4 * c + 4, 1 + P * half:1 + P * half + P],
                        ps[0:EMB, Y0_BANK[half][c], :].rearrange("p (b s) -> p b s", b=4),
                        ACT.Identity, bias=tb[:, 0:1]).then_inc(y0_sb, 1)

            level0(0)
            act.wait_ge(kps_ready, 1)
            nc.scalar.activation(ksb.rearrange("p d b -> p (d b)"), pf[0:TA, 0:D * TB], ACT.Copy).then_inc(ksb_ready, 1)
            act.wait_ge(khat_ps, 1)
            nc.scalar.activation(khat[:, :, :].rearrange("p (x y) d -> p x (y d)", x=2), ps[:, 3:5, 0:2 * D], ACT.Copy)
            nc.scalar.activation(k0[:, :], ps[0:B, 2, 0:D], ACT.Copy).then_inc(khat_ready, 1)
            level0(1)
            for g in range(B):
                act.wait_ge(h_ps, g + 1)
                half, b = g // 4, 2 * (g % 4)
                nc.scalar.activation(h[:, half, b:b + 2, :].rearrange("p b d -> p (b d)"), ps[:, g, 0:2 * D],
                                     ACT.Copy).then_inc(h_sb, 1)
            act.wait_ge(h_ps, B + 1)
            nc.scalar.activation(h_last[:, :], ps[0:B, 0, 0:D], ACT.Copy).then_inc(h_sb, 1)

            for g in range(5):
                act.wait_ge(xt_ps, g + 1)
                n = 4 if g < 4 else 1
                w = P if g < 4 else B
                for dst, bank, rows in ((xta, g % 3, P), (xtb, 3 + g % 3, D2)):
                    ins = nc.scalar.activation(
                        dst[0:rows, 4 * g:4 * g + n, 0:w],
                        ps[0:rows, bank, 0:n * P].rearrange("p (k s) -> p k s", k=n)[:, :, 0:w], ACT.Copy)
                ins.then_inc(xt_sb, 1)
            act.wait_ge(gap_ready, 1)
            nc.scalar.activation(rs[:, 5], rs[:, 4], ACT.Exp).then_inc(gexp_ready, 1)

            def gelu(i, par):
                act.wait_ge(fc_ps, i + 1)
                nc.scalar.activation(hs[:, par].rearrange("p (k n) -> p k n", k=2), ps[:, 0:2, 0:H // 2],
                                     ACT.Gelu_apprx_tanh).then_inc(gelu_ready, 1)

            with act.Fori(0, NBLK // 2) as q:
                for par in range(2):
                    gelu(2 * q + par, par)

        @block.vector
        def _(dve):
            own = Chain(dve, vec_own)
            v = nc.vector
            AR, AI, BM, CM, LD = (ssm[:, n] for n in range(5))

            dve.wait_ge(const_in, 16)
            dve.wait_ge(ssm_in, 16 * 9)
            v.scalar_tensor_tensor(out=sm[:, 0], in0=LD, scalar=-1.0, in1=LD, op0=ALU.mult,
                                   op1=ALU.max).then_inc(abs_ready, 1)
            dve.wait_ge(e_ready, 1)
            v.tensor_scalar(sm[:, 2], sm[:, 1], 1.0, None, ALU.add).then_inc(w_ready, 1)
            dve.wait_ge(w_ready, 1)
            own.inc(v.scalar_tensor_tensor(out=sm[:, 4], in0=sm[:, 2], scalar=-1.0, in1=sm[:, 1], op0=ALU.add,
                                           op1=ALU.subtract))
            own.link(v.reciprocal(sm[:, 5], sm[:, 2]))
            own.link(v.tensor_tensor(sm[:, 4], sm[:, 4], sm[:, 5], ALU.mult))
            dve.wait_ge(ln_ready, 1)
            own.link(v.scalar_tensor_tensor(out=sm[:, 5], in0=LD, scalar=0.0, in1=sm[:, 3], op0=ALU.max, op1=ALU.add))
            own.link(v.tensor_tensor(delta, sm[:, 5], sm[:, 4], ALU.subtract))
            v.tensor_tensor(rate, AR, delta, ALU.mult)
            v.scalar_tensor_tensor(out=turn, in0=AI, scalar=1.0 / (2.0 * np.pi), in1=delta, op0=ALU.mult,
                                   op1=ALU.mult).then_inc(rate_ready, 1)
            dve.wait_ge(rate_ready, 1)
            own.inc(v.tensor_tensor(sm[:, 0], AR, AR, ALU.mult))
            own.link(v.tensor_tensor(sm[:, 1], AI, AI, ALU.mult))
            own.link(v.tensor_tensor(sm[:, 0], sm[:, 0], sm[:, 1], ALU.add))
            own.link(v.reciprocal(sm[:, 1], sm[:, 0]))
            own.link(v.tensor_tensor(sm[:, 2], BM, CM, ALU.mult))
            own.link(v.tensor_tensor(sm[:, 0], sm[:, 1], sm[:, 2], ALU.mult))

            def fraction(dst, tmp, done, n):
                own.link(v.tensor_scalar(tmp, dst, MAGIC, -MAGIC, ALU.add, ALU.add))
                v.tensor_tensor(dst, dst, tmp, ALU.subtract).then_inc(done, 1)
                dve.wait_ge(done, n)

            dve.wait_ge(turn1_ready, 1)
            fraction(trig1, scr[:, 0:2], frac1_ready, 1)
            for k in range(2):
                dve.wait_ge(yturn_ready, k + 1)
                fraction(ytab[:, k], scr[:, 0:TB], yfrac_ready, k + 1)
            dve.wait_ge(sin1_ready, 1)
            dve.wait_ge(env1_ready, 1)
            own.inc(v.tensor_tensor(sm[:, 1], sm[:, 8], trig1[:, 0], ALU.mult))
            own.link(v.tensor_tensor(sm[:, 2], sm[:, 8], trig1[:, 1], ALU.mult))
            own.link(v.tensor_scalar(sm[:, 1], sm[:, 1], -1.0, None, ALU.add))
            for n, (x, y) in enumerate(((sm[:, 1], AR), (sm[:, 2], AI), (sm[:, 2], AR), (sm[:, 1], AI))):
                own.inc(v.tensor_tensor(scr[:, n], x, y, ALU.mult))
            own.sync()
            own.inc(v.tensor_tensor(sm[:, 3], scr[:, 0], scr[:, 1], ALU.add))
            own.link(v.tensor_tensor(sm[:, 4], scr[:, 2], scr[:, 3], ALU.subtract))
            own.inc(v.tensor_tensor(sm[:, 3], sm[:, 3], sm[:, 0], ALU.mult))
            own.link(v.tensor_tensor(sm[:, 4], sm[:, 4], sm[:, 0], ALU.mult))
            dve.wait_ge(ysin_ready, 2)
            dve.wait_ge(yenv_ready, 1)
            for k in range(2):
                own.inc(v.tensor_tensor(ytab[:, k], ytab[:, k], bc(sm[:, 3 + k], 1, TB), ALU.mult))
            own.sync()
            own.link(v.tensor_tensor(ytab[:, 0], ytab[:, 0], ytab[:, 1], ALU.add))
            v.tensor_tensor(ytab[:, 0], ytab[:, 0], ye, ALU.mult).then_inc(ytab_ready, 1)

            def level12():
                dve.wait_ge(t2_ps, 1)
                v.tensor_copy(t2.rearrange("p q b s -> p (q b s)"), pf[0:48, 0:2048]).then_inc(t2_sb, 1)
                dve.wait_ge(t1_ps, 1)
                v.tensor_copy(t1.rearrange("p b s -> p (b s)"), pf[0:96, 2048:3072]).then_inc(t1_sb, 1)

            def interpolate():
                for pad, dif, n, f, w, ready, dst in ((p2, d2, 16, 16, C["w16"], y2_sb, yb[0:EMB]),
                                                      (p1, d1, 64, 4, C["w4"], y1_sb, ya[EMB:P])):
                    dve.wait_ge(ready, 1)
                    own.inc(v.tensor_copy(pad[:, :, 0:1], pad[:, :, 1:2]))
                    own.link(v.tensor_copy(pad[:, :, n + 1:n + 2], pad[:, :, n:n + 1]))
                    own.link(v.tensor_tensor(dif[:, :, :], pad[:, :, 1:n + 2], pad[:, :, 0:n + 1], ALU.subtract))
                    cells = itmp[:, :, 0:(n - 1) * f].rearrange("p b (j r) -> p b j r", r=f)
                    wb = bc(w[0:EMB], 1, n - 1)
                    for b in range(B):
                        own.inc(v.tensor_tensor(cells[:, b], bc(dif[:, b, 1:n], 2, f), wb, ALU.mult))
                    own.sync()
                    lead = 1 + f // 2
                    for b in range(B):
                        ins = v.tensor_tensor(dst[:, b, lead:lead + (n - 1) * f].rearrange("p (j r) -> p j r", r=f),
                                              cells[:, b], bc(pad[:, b, 1:n], 2, f), ALU.add)
                    own.link(ins)
                    v.tensor_copy(dst[:, :, 1:lead], pad[:, :, 0:1].broadcast_to([EMB, B, f // 2]))
                    v.tensor_copy(dst[:, :, L - f // 2:L],
                                  pad[:, :, n:n + 1].broadcast_to([EMB, B, f // 2])).then_inc(y12_done, 1)

            n3 = TA // 3
            for k in range(3):
                dve.wait_ge(xturn_ready, k + 1)
                fraction(xe, scr, xfrac_ready, k + 1)
                if k == 0:
                    level12()
                if k == 1:
                    interpolate()
                dve.wait_ge(xsin_ready, k + 1)
                if k == 0:
                    dve.wait_ge(xenv_ready, 1)
                v.tensor_tensor(xtab[:, k * n3:(k + 1) * n3], xtab[:, k * n3:(k + 1) * n3], xe,
                                ALU.mult).then_inc(xtab_ready, 1)

            def norm(j, np_, src, dst):
                return v.tensor_scalar(dst, src, mv[0:np_, j, 0:1], rstd[0:np_, j:j + 1], ALU.subtract, ALU.mult)

            roots = [0]

            def root(np_, *tiles):
                assert (np_, tiles) == ROOTS[roots[0]]
                for j0, j1 in tiles:
                    ins = v.tensor_scalar(veps[0:np_, j0:j1], mv[0:np_, j0:j1, 1], EPS, None, ALU.add)
                roots[0] += 1
                ins.then_inc(veps_ready, 1)
                dve.wait_ge(rstd_ready, roots[0])

            for half in range(2):
                for g in range(4):
                    dve.wait_ge(h_sb, 4 * half + g + 1)
                    for m in range(2):
                        own.inc(v.bn_stats(stats[:, 8 * half + 2 * g + m], h[:, half, 2 * g + m]))
                own.sync()
                for j in range(8 * half, 8 * half + 8):
                    own.inc(v.bn_aggr(mv[:, j], stats[:, j]))
                own.sync()
                root(P, (8 * half, 8 * half + 8))
                for b in range(B):
                    ins = norm(8 * half + b, P, h[:, half, b], u[:, half, b])
                ins.then_inc(u_ready, 1)
            dve.wait_ge(h_sb, 9)
            own.link(v.bn_stats(stats[0:B, 16], h_last[:, :]))
            own.link(v.bn_aggr(mv[0:B, 16], stats[0:B, 16]))
            root(B, (16, 17))
            own.link(norm(16, B, h_last[:, :], u_last[:, :]))
            dve.wait_ge(khat_ready, 1)
            own.inc(v.tensor_tensor(k0u, u_last[:, :], k0[:, :], ALU.mult))

            for c in range(B // 2):
                dve.wait_ge(uhat_ps, c + 1)
                if c >= 2:
                    dve.wait_ge(yhat_ready, c - 1)
                base = 4 * (c % 2)
                for n, (x, y) in enumerate(((0, 0), (1, 1), (0, 1), (1, 0))):
                    src = ps[:, base + 2 * x:base + 2 * x + 2, 0:2 * D].rearrange("p f (b d) -> p f b d", b=2)
                    dst = prod[:, c % 2, n].rearrange("p (f b d) -> p f b d", f=2, b=2)
                    ins = v.tensor_tensor(dst, src, bc(khat[:, 2 * y:2 * y + 2, :], 2, 2), ALU.mult)
                ins.then_inc(prod_ready, 1)

            own.inc(v.memset(lg[:, 2 * B], 0.0))
            for c in range(B // 2):
                dve.wait_ge(y_ps, 2 * c + 2)
                for lt in range(2):
                    hv = h[:, lt, 2 * c:2 * c + 2, :].rearrange("p b d -> p (b d)")
                    v.tensor_tensor(hv, hv, ps[:, 2 * c + lt, 0:2 * D], ALU.add).then_inc(h2_ready, 1)
                dve.wait_ge(h2_ready, 2 * c + 2)
                for lt in range(2):
                    for b in (2 * c, 2 * c + 1):
                        own.inc(v.bn_stats(stats[:, 8 * lt + b], h[:, lt, b]))
                own.sync()
                for lt in range(2):
                    for b in (2 * c, 2 * c + 1):
                        own.inc(v.bn_aggr(mv[:, 8 * lt + b], stats[:, 8 * lt + b]))
                own.sync()
                root(P, (2 * c, 2 * c + 2), (8 + 2 * c, 10 + 2 * c))
                for lt in range(2):
                    for b in (2 * c, 2 * c + 1):
                        norm(8 * lt + b, P, h[:, lt, b], xg[:, 8 * lt + b, 0:D]).then_inc(x_ready, 1)
            dve.wait_ge(y_ps, 9)
            own.link(v.tensor_tensor(h_last[:, :], h_last[:, :], k0u, ALU.add))
            v.tensor_tensor(h_last[:, :], h_last[:, :], ps[0:B, 0, 0:D], ALU.add).then_inc(h2_ready, 9)
            dve.wait_ge(h2_ready, 17)
            own.link(v.bn_stats(stats[0:B, 16], h_last[:, :]))
            own.link(v.bn_aggr(mv[0:B, 16], stats[0:B, 16]))
            root(B, (16, 17))
            norm(16, B, h_last[:, :], xg[0:B, 16, 0:D]).then_inc(x_ready, 1)

            own.inc(v.tensor_copy(ltri16[:, :], C["ltri"]))
            own.inc(v.memset(ones16[:, :], 1.0))
            own.inc(v.memset(ohb16[:, TILES], 0.0))
            dve.wait_ge(logit_ps, 1)
            own.inc(v.tensor_copy(lg[:, 0:2 * B].rearrange("p k e -> p (k e)"), ps[:, 6, 0:2 * B * NE]))
            own.link(v.tensor_copy(lg[0:B, 2 * B], ps[0:B, 6, 2 * B * NE:TILES * NE]))
            ew = bc(C["ew"], 1, TILES)

            def pick(src, top, oh):
                own.link(v.tensor_reduce(top, src, AX.X, ALU.max))
                own.link(v.tensor_tensor(rt[:, 0], src, bc(top, 2, NE), ALU.is_equal))
                own.link(v.tensor_tensor(rt[:, 0], rt[:, 0], ew, ALU.mult))
                own.link(v.tensor_reduce(rs[:, 3], rt[:, 0], AX.X, ALU.max))
                own.link(v.tensor_tensor(oh, ew, bc(rs[:, 3], 2, NE), ALU.is_equal))

            pick(lg[:, :, :], rs[:, 0], oh1[:, :, :])
            own.link(v.scalar_tensor_tensor(out=rt[:, 1], in0=oh1[:, :, :], scalar=LOWEST, in1=lg[:, :, :],
                                            op0=ALU.mult, op1=ALU.add))
            pick(rt[:, 1], rs[:, 1], oh2[:, :, :])
            v.tensor_tensor(rs[:, 4], rs[:, 1], rs[:, 0], ALU.subtract).then_inc(gap_ready, 1)
            own.link(v.tensor_tensor(rt[:, 0], oh1[:, :, :], oh2[:, :, :], ALU.add))
            v.tensor_tensor(ohb16[:, 0:TILES], rt[:, 0], bc(C["valid"], 2, NE), ALU.mult).then_inc(oh_ready, 1)
            dve.wait_ge(gexp_ready, 1)
            own.link(v.tensor_scalar(rs[:, 6], rs[:, 5], 1.0, None, ALU.add))
            own.link(v.reciprocal(rs[:, 7], rs[:, 6]))
            own.link(v.tensor_tensor(rs[:, 8], rs[:, 5], rs[:, 7], ALU.mult))
            own.inc(v.tensor_tensor(rt[:, 1], oh1[:, :, :], bc(rs[:, 7], 2, NE), ALU.mult))
            own.link(v.tensor_tensor(rt[:, 2], oh2[:, :, :], bc(rs[:, 8], 2, NE), ALU.mult))
            v.tensor_tensor(xg[:, :, D:XW], rt[:, 1], rt[:, 2], ALU.add).then_inc(gates_ready, 1)
            dve.wait_ge(rank_ps, 1)
            rank = ps[:, 7, 0:(TILES + 1) * NE].rearrange("p (k e) -> p k e", e=NE)
            own.link(v.tensor_scalar(cnt_i[:, :], rank[:, TILES], float(P - 1), None, ALU.add))
            own.link(v.tensor_scalar(cnt_i[:, :], cnt_i[:, :], 7, None, ALU.arith_shift_right))
            own.inc(v.memset(cnt[:, 0], 1.0))
            own.link(v.tensor_copy(cnt[:, 1], cnt_i[:, :]))
            own.link(v.tensor_tensor_scan(cnt[:, 2], cnt[:, 0], cnt[:, 1], 0.0, ALU.mult, ALU.add))
            own.link(v.tensor_tensor(cnt[:, 3], cnt[:, 2], cnt[:, 1], ALU.subtract))
            own.link(v.tensor_scalar(cnt[:, 3], cnt[:, 3], float(P), None, ALU.mult))
            own.link(v.tensor_tensor(rt[:, 0], rank[:, 0:TILES], bc(cnt[:, 3], 1, TILES), ALU.add))
            own.inc(v.tensor_tensor(rt[:, 1], rt[:, 0], oh1[:, :, :], ALU.mult))
            own.link(v.tensor_tensor(rt[:, 2], rt[:, 0], oh2[:, :, :], ALU.mult))
            for n in range(2):
                own.inc(v.tensor_reduce(pos[:, n], rt[:, 1 + n], AX.X, ALU.add))
            own.sync()
            own.link(v.tensor_copy(pos_i[:, :, :], pos[:, :, :]))
            own.inc(v.tensor_scalar(blk_i[:, :, :], pos_i[:, :, :], 7, None, ALU.arith_shift_right))
            own.link(v.tensor_scalar(slt_i[:, :, :], pos_i[:, :, :], P - 1, None, ALU.bitwise_and))
            own.inc(v.tensor_copy(blk_f[:, :], blk_i[:, :, :].rearrange("p k j -> p (k j)")))
            own.link(v.tensor_copy(slt_f[:, :], slt_i[:, :, :].rearrange("p k j -> p (k j)")))
            own.inc(v.tensor_tensor(ohs, bc(C["iota_s"], 1, 2 * TILES), bc(slt_f[:, :], 2, P), ALU.is_equal))
            own.link(v.tensor_tensor(ohb, bc(C["iota_b"], 1, 2 * TILES), bc(blk_f[:, :], 2, NBLK), ALU.is_equal))
            v.tensor_tensor(mvb, bc(ohb, 2, 3),
                            bc(C["ids"].rearrange("p (k c) -> p k c", c=3), 3, NBLK), ALU.mult).then_inc(pick_ready, 1)
            own.link(v.tensor_tensor(ge_t, bc(C["iota_b"], 2, NE), bc(cnt[:, 2], 1, NBLK), ALU.is_ge))
            own.link(v.tensor_reduce(blk_e[:, :], ge_t, AX.X, ALU.add))
            own.link(v.tensor_scalar(blk_e[:, :], blk_e[:, :], float(NE - 1), None, ALU.min))
            v.tensor_copy(blk_ei[:, :], blk_e[:, :]).then_inc(expert_ready, 1)
            own.inc(v.tensor_tensor(gsel_e, bc(C["eidx"], 1, NBLK), bc(blk_e[:, :], 2, NE), ALU.is_equal))
            v.memset(xs, 0.0).then_inc(xs_clear, 1)
            dve.wait_ge(slot_ps, 1)
            own.link(v.tensor_copy(slotv[:, :], ps[:, 0, 0:3 * NBLK]))
            sv = slotv[:, :].rearrange("p (c s) -> p c s", c=3)
            own.link(v.scalar_tensor_tensor(out=idx_f[:, :], in0=sv[:, 1], scalar=256.0, in1=sv[:, 0], op0=ALU.mult,
                                            op1=ALU.add))
            own.link(v.scalar_tensor_tensor(out=idx_f[:, :], in0=sv[:, 2], scalar=-1.0, in1=idx_f[:, :], op0=ALU.add,
                                            op1=ALU.add))
            own.link(v.tensor_copy(idx[:, :], idx_f[:, :]))
            v.tensor_copy(gcol[:, :], idx[:, 0:4]).then_inc(idx_ready, 1)

            def turned(i, par):
                dve.wait_ge(bt_ps, i + 1)
                v.tensor_copy(bta[:, par], ps[:, 4, 0:P])
                v.tensor_copy(btb[:, par], ps[0:D2, 4, P:2 * P]).then_inc(bt_sb, 1)

            def output(i, r, first, more=True):
                v.tensor_tensor(gsel[:, r % 2], xs[:, r, D:XW], gsel_e[:, bass.ds(i, 1), :].rearrange("p o e -> p (o e)"),
                                ALU.mult).then_inc(gate_seen, 1)
                dve.wait_ge(gate_seen, 2 * i + 1)
                v.tensor_reduce(gate[:, r % 2:r % 2 + 1], gsel[:, r % 2], AX.X, ALU.add).then_inc(gate_seen, 1)
                dve.wait_ge(gate_seen, 2 * i + 2)
                dve.wait_ge(pj_ps, i + 1)
                if not first:
                    dve.wait_ge(added, 16 * (i - 1))
                v.tensor_copy(scol[:, r:r + 1], idx[:, bass.ds(i, 1)])
                if more:
                    v.tensor_copy(gcol[:, r:r + 1], idx[:, bass.ds(i + 4, 1)])
                v.tensor_scalar(o_sb[:, r % 2], ps[:, 5 + r % 2, 0:D], gate[:, r % 2:r % 2 + 1], None,
                                ALU.mult).then_inc(o_ready, 1)

            def hidden(i, par):
                dve.wait_ge(ht_ps, i + 1)
                v.tensor_copy(hT[:, par].rearrange("p (k n) -> p k n", k=2), ps[:, 2:4, 0:H // 2]).then_inc(ht_sb, 1)

            def vstep(q, r, more=True, first=False, gather_more=True):
                i = 4 * q + r + 1
                if more:
                    turned(i + 1, r % 2)
                output(i - 1, r, first, gather_more)
                hidden(i, (r + 1) % 2)

            turned(0, 0)
            turned(1, 1)
            hidden(0, 0)
            for r in range(2):
                vstep(0, r, first=True)
            for r in range(2, 4):
                vstep(0, r)
            with dve.Fori(1, NBLK // 4 - 1) as q:
                for r in range(4):
                    vstep(q, r)
            for r in range(3):
                vstep(NBLK // 4 - 1, r, more=r < 2, gather_more=False)
            output(NBLK - 1, 3, False, False)

        @block.tensor
        def _(pe):
            mm = nc.tensor.matmul
            pe.wait_ge(const_in, 16)
            pe.wait_ge(raw2_in, 32)
            for q in range(2):
                for b in range(B):
                    k = (q * B + b) * P
                    ins = nc.tensor.transpose(pf[0:48, k:k + P], raw2[:, q, b * 48:(b + 1) * 48], ident)
            ins.then_inc(t2_ps, 1)
            pe.wait_ge(byb1_ready, 1)
            for b in range(B):
                k = 2048 + b * P
                ins = nc.tensor.transpose(pf[0:96, k:k + P], byb1[:, b].rearrange("p g c -> p (g c)"), ident)
            ins.then_inc(t1_ps, 1)
            pe.wait_ge(tokw_in, 16 * 9)
            pe.wait_ge(t2_sb, 1)
            for g in range(GP):
                q, gg = g // 8, g % 8
                ins = mm(ps[0:EMB, 7, 0:B * 16], lhsT=w2[:, g, :],
                         rhs=t2[:, q, :, gg * 16:(gg + 1) * 16], start=g == 0, stop=g == GP - 1)
            ins.then_inc(y2_ps, 1)
            pe.wait_ge(t1_sb, 1)
            for k in range(2):
                ins = mm(ps[0:EMB, 6, :], lhsT=w1[:, k, :], rhs=t1[:, :, k * 64:(k + 1) * 64], start=k == 0, stop=k == 1)
            ins.then_inc(y1_ps, 1)

            def level0(half):
                pe.wait_ge(byb0_ready, half + 1)
                for b in range(B):
                    k = T0_BANK[half] * 512 + b * P
                    ins = nc.tensor.transpose(pf[0:48, k:k + P], byb0[:, half, b], ident)
                ins.then_inc(t0_ps, 1)
                pe.wait_ge(t0_sb, half + 1)
                for c in range(2):
                    mm(ps[0:EMB, Y0_BANK[half][c], :], lhsT=w0[:, :], rhs=t0[:, half, 4 * c:4 * c + 4, :],
                       start=True, stop=True).then_inc(y0_ps, 1)

            pe.wait_ge(y1_sb, 1)
            pe.wait_ge(y2_sb, 1)
            level0(0)
            pe.wait_ge(ytab_ready, 1)
            pe.wait_ge(xtab_ready, 3)
            for d in range(D):
                ins = mm(pf[0:TA, d * TB:(d + 1) * TB], lhsT=xtab[:, :, d], rhs=ytab[:, 0, :, d], start=True, stop=True)
            ins.then_inc(kps_ready, 1)
            pe.wait_ge(ksb_ready, 1)
            pe.wait_ge(four_in, 16 * 5)
            for kt in range(KT):
                dst = ps[:, 3 + kt // 2, (kt % 2) * D:(kt % 2) * D + D]
                for b in range(TB):
                    mm(dst, lhsT=fwd_k[:, b, kt * P:(kt + 1) * P], rhs=ksb[:, :, b], start=b == 0, stop=b == TB - 1)
            mm(ps[0:B, 2, 0:D], lhsT=C["row0"][0:TA], rhs=ksb[:, :, 0], start=True, stop=True).then_inc(khat_ps, 1)
            pe.wait_ge(khat_ready, 1)
            level0(1)
            pe.wait_ge(y0_sb, 4)
            pe.wait_ge(y12_done, 2)
            pe.wait_ge(edge_zero, 2)
            for g in range(B):
                half = g // 4
                for m in range(2):
                    b = 2 * (g % 4) + m
                    dst = ps[:, g, m * D:(m + 1) * D]
                    mm(dst, lhsT=ya[:, b, P * half:P * half + P], rhs=wfa[:, :], start=True, stop=False)
                    ins = mm(dst, lhsT=yb[:, b, P * half:P * half + P], rhs=wfb[:, :], start=False, stop=True)
                ins.then_inc(h_ps, 1)
            pe.wait_ge(h_sb, 1)
            mm(ps[0:B, 0, 0:D], lhsT=ya[:, :, NT], rhs=wfa[:, :], start=True, stop=False)
            mm(ps[0:B, 0, 0:D], lhsT=yb[:, :, NT], rhs=wfb[:, :], start=False, stop=True).then_inc(h_ps, 1)
            pe.wait_ge(h_sb, 9)
            pe.wait_ge(u_ready, 2)
            for c in range(B // 2):
                if c >= 2:
                    pe.wait_ge(prod_ready, c - 1)
                for kt in range(KT):
                    for m in range(2):
                        ins = mm(ps[:, 4 * (c % 2) + kt, 0:2 * D], lhsT=fwd[:, m, kt * P:(kt + 1) * P],
                                 rhs=u[:, m, 2 * c:2 * c + 2, :], start=m == 0, stop=m == 1)
                ins.then_inc(uhat_ps, 1)
            for c in range(B // 2):
                pe.wait_ge(yhat_ready, c + 1)
                pe.wait_ge(prod_ready, 3 if c < 2 else 4)
                for lt in range(2):
                    for kt in range(KT):
                        ins = mm(ps[:, 2 * c + lt, 0:2 * D], lhsT=inv[:, kt, lt * P:(lt + 1) * P],
                                 rhs=yhat[:, kt, 2 * c:2 * c + 2, :], start=kt == 0, stop=kt == KT - 1)
                    ins.then_inc(y_ps, 1)
            pe.wait_ge(h2_ready, 1)
            sgn = C["sgn"].rearrange("p (b c) -> p b c", b=B)
            for b in range(B):
                for f in range(2):
                    ins = mm(ps[0:B, 0, 0:D], lhsT=sgn[:, b, :], rhs=yhat[:, 2 + f, b, :],
                             start=(b, f) == (0, 0), stop=(b, f) == (B - 1, 1))
            ins.then_inc(y_ps, 1)
            seen = [4 * (j % 8 // 2) + 2 * (j // 8) + j % 2 + 1 for j in range(2 * B)] + [TILES]
            pe.wait_ge(h2_ready, 17)
            for g in range(5):
                n = 4 if g < 4 else 1
                pe.wait_ge(x_ready, max(seen[4 * g:4 * g + n]))
                if g >= 3:
                    pe.wait_ge(xt_sb, g - 2)
                w = P if g < 4 else B
                for m in range(n):
                    j = 4 * g + m
                    nc.tensor.transpose(ps[:, g % 3, m * P:m * P + w], xg[0:w, j, 0:P], ident[0:w, 0:w])
                    ins = nc.tensor.transpose(ps[0:D2, 3 + g % 3, m * P:m * P + w], xg[0:w, j, P:D], ident[0:w, 0:w])
                ins.then_inc(xt_ps, 1)
            for j in range(TILES):
                w = P if j < 2 * B else B
                pe.wait_ge(xt_sb, j // 4 + 1)
                mm(ps[0:w, 6, j * NE:(j + 1) * NE], lhsT=xta[:, j, 0:w], rhs=wga[:, :], start=True, stop=False)
                ins = mm(ps[0:w, 6, j * NE:(j + 1) * NE], lhsT=xtb[:, j, 0:w], rhs=wgb[:, :], start=False, stop=True)
            ins.then_inc(logit_ps, 1)
            pe.wait_ge(oh_ready, 1)
            mm(ps[:, 7, 0:(TILES + 1) * NE], lhsT=ltri16[:, :], rhs=ohb16[:, :, :].rearrange("p k e -> p (k e)"),
               start=True, stop=False)
            for j in range(TILES):
                n = TILES - j
                ins = mm(ps[:, 7, (j + 1) * NE:(TILES + 1) * NE], lhsT=ones16[:, :], rhs=bc(ohb16[:, j], 1, n),
                         start=False, stop=j == TILES - 1)
            ins.then_inc(rank_ps, 1)
            pe.wait_ge(pick_ready, 1)
            for k in range(2 * TILES):
                ins = mm(ps[:, 0, 0:3 * NBLK], lhsT=ohs[:, k, :], rhs=mvb[:, k].rearrange("p c s -> p (c s)"),
                         start=k == 0, stop=k == 2 * TILES - 1)
            ins.then_inc(slot_ps, 1)

            def turn_rows(q, r):
                pe.wait_ge(xs_in[r], 16 * (q + 1))
                nc.tensor.transpose(ps[:, 4, 0:P], xs[:, r, 0:P], ident)
                nc.tensor.transpose(ps[0:D2, 4, P:2 * P], xs[:, r, P:D], ident).then_inc(bt_ps, 1)

            def up(i, e, par):
                pe.wait_ge(bt_sb, i + 1)
                for n in range(2):
                    dst = ps[:, n, 0:H // 2]
                    mm(dst, lhsT=bta[:, par], rhs=wfc_a[:, bass.ds(e * H + n * (H // 2), H // 2)], start=True, stop=False)
                    ins = mm(dst, lhsT=btb[:, par], rhs=wfc_b[:, bass.ds(e * H + n * (H // 2), H // 2)],
                             start=False, stop=True)
                ins.then_inc(fc_ps, 1)

            def down(i, e, par, first):
                pe.wait_ge(ht_sb, i + 1)
                if not first:
                    pe.wait_ge(o_ready, i - 1)
                for k in range(HT):
                    ins = mm(ps[:, 5 + par, 0:D], lhsT=hT[:, par, k * P:(k + 1) * P],
                             rhs=wpj[:, bass.ds(e * HT * D + k * D, D)], start=k == 0, stop=k == HT - 1)
                ins.then_inc(pj_ps, 1)

            def turn_hidden(i, par):
                pe.wait_ge(gelu_ready, i + 1)
                for k in range(HT):
                    ins = nc.tensor.transpose(ps[:, 2 + k // 3, (k % 3) * P:(k % 3 + 1) * P],
                                              hs[:, par, k * P:(k + 1) * P], ident)
                ins.then_inc(ht_ps, 1)

            def expert(i):
                return pe.value_load(blk_ei[0:1, bass.ds(i, 1)], min_val=0, max_val=NE - 1)

            def pstep(q, r, more=True, first=False):
                i = 4 * q + r + 1
                up(i, expert(i), (r + 1) % 2)
                if more:
                    turn_rows(q + (r + 2) // 4, (r + 2) % 4)
                down(i - 1, expert(i - 1), r % 2, first)
                turn_hidden(i, (r + 1) % 2)

            pe.wait_ge(expert_ready, 1)
            pe.wait_ge(idx_ready, 1)
            pe.wait_ge(exp_in, 48)
            turn_rows(0, 0)
            up(0, expert(0), 0)
            turn_rows(0, 1)
            turn_hidden(0, 0)
            for r in range(2):
                pstep(0, r, first=True)
            for r in range(2, 4):
                pstep(0, r)
            with pe.Fori(1, NBLK // 4 - 1) as q:
                for r in range(4):
                    pstep(q, r)
            for r in range(3):
                pstep(NBLK // 4 - 1, r, more=r < 2)
            down(NBLK - 1, expert(NBLK - 1), 1, False)


def kernel(**inputs):
    import concourse.bacc as bacc
    from concourse.bass_utils import run_bass_kernel_spmd

    a = {k: np.asarray(v) for k, v in inputs.items()}
    x = a["x"]

    def patches(p):
        n = IMG // p
        return x.reshape(B, CH, n, p, n, p).transpose(2, 4, 0, 3, 5, 1).reshape(n * n, B * p * p * CH)

    arrays = {
        "px0": patches(1), "px1": patches(2), "px2": patches(4),
        "id0": a["L0_tok_idx0"].reshape(2, P, GP).transpose(1, 0, 2).reshape(P, 2 * GP),
        "id1": a["L0_tok_idx1"].reshape(64, 2, 8).transpose(1, 0, 2).reshape(P, 8),
        "id2": a["L0_tok_idx2"].reshape(16, 2, 8).transpose(2, 0, 1).reshape(P, 2),
        "w0": a["L0_tok_W0"].T,
        "w1": a["L0_tok_W1"].T.reshape(2, 96, EMB).transpose(1, 0, 2),
        "w2": a["L0_tok_W2"].T.reshape(GP, 48, EMB).transpose(1, 0, 2),
        "tb": np.stack([a["L0_tok_b0"], a["L0_tok_b1"], a["L0_tok_b2"]], 1),
        "wf": a["L0_tok_Wf"].T,
        "bf": a["L0_tok_bf"].reshape(1, D),
        "cls": a["cls_tok"].reshape(1, D),
        "a_real": a["L0_attn_A_real"].T, "a_imag": a["L0_attn_A_imag"].T,
        "b_mat": a["L0_attn_B_mat"].T, "c_mat": a["L0_attn_C_mat"].T,
        "log_delta": a["L0_attn_log_delta"],
        "w_gate": a["L0_ffn_w_gate"],
        "w_fc": a["L0_ffn_w_fc"].reshape(D, H, NE).transpose(0, 2, 1).reshape(D, NE * H),
        "w_proj": a["L0_ffn_w_proj"].reshape(HT, P, D, NE).transpose(1, 3, 0, 2).reshape(P, NE * HT * D),
        **shape_constants(),
    }
    arrays = {k: np.ascontiguousarray(v) for k, v in arrays.items()}
    nc = bacc.Bacc("TRN2", target_bir_lowering=False, num_devices=1)
    t = {k: nc.dram_tensor(k, v.shape, mybir.dt.from_np(v.dtype), kind="ExternalInput").ap() for k, v in arrays.items()}
    out = nc.dram_tensor("out", (B, L, D), F32, kind="ExternalOutput").ap()
    vit_layer(nc, t, out)
    r = run_bass_kernel_spmd(nc, [arrays], core_ids=[0])
    return r.results[0]["out"]
```

```python
import numpy as np
from contextlib import ExitStack

import concourse.bass as bass
from concourse import mybir

F32 = mybir.dt.float32
BF16 = mybir.dt.bfloat16
F16 = mybir.dt.float16
I32 = mybir.dt.int32
U32 = mybir.dt.uint32
ALU = mybir.AluOpType
ACT = mybir.ActivationFunctionType
AX = mybir.AxisListType

P = 128
B, CH, IMG = 8, 3, 64
D = 192
EMB = 64
GP = 16
NT = 256
L = NT + 1
D2 = D - P
NS = 64
TA, TB = 32, 8
CG = P // TA
NG = D // CG
XP = 8
ZR = 82
NF = 256
NFFT = 2 * NF
KT = 4
H, NE = 768, 8
HT = H // P
TILES = 2 * B + 1
ROWS = B * L
NBLK = (2 * ROWS + NE * (P - 1)) // P
XW = D + NE
WC = 1024
N_FC, N_PJ = NE * H, NE * HT * D
FC_PIECES, PIECES = 2 * N_FC // WC, (2 * N_FC + N_PJ) // WC
STAT_PIECES = D * N_FC // P // WC
N_BUF = 5
VEC_PIECES = [0, 1, 2, 3, 6, 7, 9, 10, 12, 13]
POOL_PIECES = [n for n in range(PIECES) if n not in VEC_PIECES]
assert N_FC % WC == 0 and N_PJ % WC == 0 and D * N_FC // P == N_PJ == STAT_PIECES * WC
EPS = 1e-5
MAGIC = 1.5 * 2.0 ** 23
TWO_PI = 6.2831845
LOWEST = -3.0e38
assert NBLK == 40 and NBLK % 2 == 0

_WIDTHS = [("ident", P), ("ltri", P), ("iota_s", P), ("iota_b", NBLK), ("off", 6), ("ids", 2 * TILES * 2),
           ("valid", TILES), ("ew", NE), ("eidx", NE), ("sgn", B * B), ("cmask", CG), ("row0", B), ("half0", B), ("ones", B)]
COL = {}
_at = 0
for _name, _w in _WIDTHS:
    COL[_name] = (_at, _at + _w)
    _at += _w
NCONST = _at


def shape_constants():
    c = np.zeros((P, NCONST), np.float32)

    def put(name, a):
        c[:, COL[name][0]:COL[name][1]] = a

    p = np.arange(P)
    put("ident", np.eye(P))
    put("ltri", p[:, None] < p[None, :])
    put("iota_s", p[None, :])
    put("iota_b", np.arange(NBLK)[None, :])
    low = (p < NS)[:, None]
    put("off", np.where(low, [[0.25, 0.25, 0.5, 0.25, 0.0, 0.25]], [[0.0, 0.5, 0.75, 0.25, 0.0, 0.0]]))
    rows = np.zeros((P, TILES), np.int64)
    valid = np.ones((P, TILES))
    for j in range(2 * B):
        rows[:, j] = (j % B) * L + P * (j // B) + p
    rows[:B, 2 * B] = p[:B] * L + NT
    valid[B:, 2 * B] = 0
    ids = np.stack([(rows + 1) % 256, (rows + 1) // 256], -1) * valid[:, :, None]
    put("ids", np.concatenate([ids, ids], 1).reshape(P, -1))
    put("valid", valid)
    put("ew", NE - np.arange(NE)[None, :])
    put("eidx", np.arange(NE)[None, :])
    sgn = np.zeros((P, B, B))
    for b in range(B):
        sgn[:, b, b] = -(2.0 / NFFT) * (-1.0) ** p
    put("sgn", sgn.reshape(P, -1))
    put("cmask", (p // TA)[:, None] == np.arange(CG)[None, :])
    put("row0", (p == 0)[:, None] * np.ones((1, B)))
    put("half0", (p < NS)[:, None] * np.ones((1, B)))
    put("ones", np.ones((1, B)))

    k = np.arange(NF)

    def angle(l):
        return np.pi * (((2 * k[None, :] + 1) * l[:, None]) % (2 * NFFT)) / NFFT

    def forward(l):
        return np.concatenate([np.cos(angle(l)), -np.sin(angle(l))], 1)

    fwd = forward(np.arange(NT)).reshape(2, P, NFFT).transpose(1, 0, 2)
    lk = TB * np.arange(TA)[:, None] + np.arange(TB)[None, :]
    fk = np.tile(forward(lk.reshape(-1)).reshape(TA, TB, NFFT), (CG, 1, 1))
    inv = (2.0 / NFFT) * forward(np.arange(NT)).T.reshape(KT, P, NT).transpose(1, 0, 2)
    interp = np.zeros((ZR, L))
    for at, n in ((0, 64), (64, 16)):
        where = np.clip((np.arange(NT) + 0.5) * (n / NT) - 0.5, 0.0, n - 1)
        i0 = np.floor(where).astype(int)
        i1 = np.minimum(i0 + 1, n - 1)
        np.add.at(interp, (at + i0, 1 + np.arange(NT)), 1.0 - (where - i0))
        np.add.at(interp, (at + i1, 1 + np.arange(NT)), where - i0)
    interp[80, 1:] = 1
    interp[81, 0] = 1
    f = lambda a: np.ascontiguousarray(a, np.float32)
    return {"consts": c, "fwd": f(fwd), "fwd_k": f(fk), "inv": f(inv), "interp": f(interp),
            "last_interp": f(interp[:, L - 1, None, None] * np.eye(B)[None])}


class Chain:

    def __init__(self, eng, s):
        self.eng, self.s, self.n = eng, s, 0

    def inc(self, ins):
        ins.then_inc(self.s, 1)
        self.n += 1

    def sync(self):
        self.eng.wait_ge(self.s, self.n)

    def link(self, ins):
        self.inc(ins)
        self.sync()


def bc(ap, axis, n):
    v = ap.unsqueeze(axis)
    shape = list(v.shape)
    shape[axis] = n
    return v.broadcast_to(shape)


def vit_layer(nc, t, out):
    with ExitStack() as ctx:
        def sb(name, shape, dt=F32):
            return ctx.enter_context(nc.sbuf_tensor(name, shape, dt))

        def sem(name):
            return ctx.enter_context(nc.semaphore(name))

        x_rows = nc.dram_tensor("x_rows", [ROWS, XW], F32, kind="Internal").ap()
        out_rows = out.rearrange("b l d -> (b l) d")

        cst = sb("cst", [P, NCONST])
        C = {n: cst[:, a:b] for n, (a, b) in COL.items()}
        ident = C["ident"]
        fwd = sb("fwd_sb", [P, 2, NFFT])
        inv = sb("inv_sb", [P, KT, NT])
        id0 = sb("id0_sb", [P, 2 * GP], I32)
        id1 = sb("id1_sb", [P, 8], I32)
        id2 = sb("id2_sb", [P, 2], I32)
        w0 = sb("w0_sb", [48, EMB])
        w1 = sb("w1_sb", [96, 2, EMB])
        tb = sb("tb_sb", [EMB, 3])
        wf = sb("wf_sb", [EMB, 3, D])
        interp = sb("interp_sb", [ZR, L])
        last_interp = sb("last_interp_sb", [ZR, B, B])
        wga = sb("wga", [P, NE])
        wgb = sb("wgb", [D2, NE])
        khat = sb("khat", [P, KT, D])
        k0 = sb("k0", [B, 2, D])
        hroom = sb("hroom", [P, 2 * B * D])
        h_last = sb("h_last", [B, D])
        uroom = sb("uroom", [P, 2 * B * D])
        u_last = sb("u_last", [B, D])
        stats = sb("stats", [P, TILES, 6])
        mv = sb("mv", [P, TILES, 2])
        rstd = sb("rstd", [P, TILES])
        veps = sb("veps", [P, TILES])
        mhalf = sb("mhalf", [P, TILES])
        lg = sb("lg", [P, TILES, NE])
        oh1 = sb("oh1", [P, TILES, NE])
        oh2 = sb("oh2", [P, TILES, NE])
        rt = sb("rt", [P, 3, TILES, NE])
        rs = sb("rs", [P, 9, TILES])
        wmax = sb("wmax", [P, 2 * STAT_PIECES + 2])
        wmax_all = sb("wmax_all", [2, 4])
        wsc = sb("wsc", [P, 16])
        stage = sb("stage", [P, 2, WC])
        ident16 = sb("ident16", [P, P], F16)
        ohb16 = sb("ohb16", [P, TILES + 1, NE], BF16)
        ltri16 = sb("ltri16", [P, P], BF16)
        ones16 = sb("ones16", [P, P], BF16)
        cnt = sb("cnt", [P, 6, NE])
        cnt_i = sb("cnt_i", [P, NE], I32)
        pos = sb("pos", [P, 2, TILES])
        pos_i = sb("pos_i", [P, 2, TILES], I32)
        blk_i = sb("blk_i", [P, 2, TILES], I32)
        slt_i = sb("slt_i", [P, 2, TILES], I32)
        blk_f = sb("blk_f", [P, 2 * TILES])
        slt_f = sb("slt_f", [P, 2 * TILES])
        blk_e = sb("blk_e", [P, NBLK])
        blk_ei = sb("blk_ei", [P, NBLK], I32)
        idx_f = sb("idx_f", [P, NBLK])
        idx = sb("idx", [P, NBLK], I32)
        gcol = sb("gcol", [P, 4], I32)
        scol = sb("scol", [P, 4], I32)
        slotv = sb("slotv", [P, 2 * NBLK])
        gsel = sb("gsel", [P, 2, NE])
        gate = sb("gate", [P, 2])
        wsc_i = wsc[:, :].bitcast(I32)
        w_scale, fc_back, h_scale, out_back = wsc[:, 9:11], wsc[:, 11:12], wsc[:, 12:13], wsc[:, 13:14]

        def view(base, at, shape):
            n = int(np.prod(shape[1:]))
            v = base[0:shape[0], at:at + n]
            names = "abcd"[:len(shape) - 1]
            if len(names) > 1:
                v = v.rearrange(f"p ({' '.join(names)}) -> p {' '.join(names)}",
                                **{c: s for c, s in zip(names[1:], shape[2:])})
            return v, at + n

        u, _ = view(uroom, 0, [P, 2, B, D])
        h, _ = view(hroom, 0, [P, 2, B, D])
        byb1, at = view(hroom, B * D, [P, B, 8, 12])
        byb0, at = view(hroom, at, [P, 2, B, GP * CH])
        assert at <= 2 * B * D
        w2, _ = view(uroom, 0, [48, GP, EMB])
        n_fc = N_FC
        wroom = sb("wroom", [P, 2 * n_fc + NE * HT * D])
        fc16 = wroom[:, 0:2 * n_fc].bitcast(F16)
        pj16 = wroom[:, 2 * n_fc:].bitcast(F16)
        ytab, at = view(wroom, 0, [P, 2, D, TB])
        ye, at = view(wroom, at, [P, D, TB])
        kmask, at = view(wroom, at, [P, D, TB])
        assert at <= n_fc
        fwd_k, at = view(wroom, n_fc, [P, TB, NFFT])
        t2, at = view(wroom, at, [48, 2, B, P])
        assert at <= 2 * n_fc
        xtab, at = view(wroom, 2 * n_fc, [P, D, TA])
        xe, at = view(wroom, at, [P, 2, D, XP])
        assert at <= 2 * n_fc + NE * HT * D

        SROOM = 15936
        sroom = sb("sroom", [P, SROOM])
        sm, at = view(sroom, 0, [P, 14, D])
        ssm, at = view(sroom, at, [P, 5, D])
        trig1, at = view(sroom, at, [P, 3, D])
        scr, at = view(sroom, at, [P, D, XP])
        raw2, at = view(sroom, at, [P, 2, B * 48])
        raw1, at = view(sroom, at, [P, 8, B * 12])
        raw0, at = view(sroom, at, [P, 2, GP * B * 3])
        t1, at = view(sroom, at, [96, B, P])
        t0, at = view(sroom, at, [48, 2, B, P])
        y1t, at = view(sroom, at, [EMB, B, 64])
        y2t, at = view(sroom, at, [EMB, B, 16])
        zt, at = view(sroom, at, [ZR, B, D])
        y0t, at = view(sroom, at, [EMB, B, L])
        assert at <= SROOM, at
        yhat, at = view(sroom, 0, [P, KT, B, D])
        prod_at = at
        prod, at = view(sroom, at, [P, 2, KT, 4 * D])
        xg, at = view(sroom, at, [P, TILES, D])
        k0u, at = view(sroom, at, [B, 2, D])
        assert at <= SROOM, at
        xr_f, at = view(sroom, prod_at, [P, TILES * XW])
        xr = xr_f.rearrange("p (k w) -> p k w", w=XW)
        xr16 = xr_f.bitcast(F16).rearrange("p (k w) -> p k w", w=2 * XW)
        assert at <= prod_at + 2 * KT * 4 * D
        ohs_f, at = view(sroom, 0, [P, TILES * P])
        ohs = ohs_f.bitcast(BF16).rearrange("p (k s) -> p k s", s=P)
        ohb_f, at = view(sroom, at, [P, TILES * NBLK])
        ohb = ohb_f.bitcast(BF16).rearrange("p (k s) -> p k s", s=NBLK)
        mvb_f, at = view(sroom, at, [P, 2 * TILES * NBLK])
        mvb = mvb_f.bitcast(BF16).rearrange("p (k c s) -> p k c s", c=2, s=NBLK)
        picks_end = at
        xt, at = view(sroom, 0, [P, TILES, 2, P])
        assert 4 * 2 * P <= 6 * D and 8 * 2 * P <= 2 * B * D
        assert at <= prod_at
        gsel_e, at = view(sroom, picks_end, [P, NBLK, NE])
        ge_t, at = view(sroom, at, [P, NBLK, NE])
        xs_f, at = view(sroom, at, [P, 4 * XW])
        xs = xs_f.rearrange("p (k w) -> p k w", w=XW)
        xs16 = xs_f.bitcast(F16).rearrange("p (k w) -> p k w", w=2 * XW)
        assert at <= prod_at
        hs, at = view(sroom, 0, [P, 2, H])
        x3_f, at = view(sroom, at, [P, 3 * P])
        x3 = x3_f.bitcast(F16).rearrange("p (k w) -> p k w", k=2)
        hh_f, at = view(sroom, at, [P, H])
        hh = hh_f.bitcast(F16).rearrange("p (k w) -> p k w", k=2)
        hl_f, at = view(sroom, at, [P, H])
        hl = hl_f.bitcast(F16).rearrange("p (k w) -> p k w", k=2)
        o_sb, at = view(sroom, at, [P, 2, D])
        assert at <= picks_end

        def piece_buffer(n):
            k = n % N_BUF
            return stage[:, k, :] if k < 2 else uroom[:, (k - 2) * WC:(k - 1) * WC]

        def piece_parts(n):
            if n < FC_PIECES:
                at = (n // (FC_PIECES // 2)) * 2 * N_FC + (n % (FC_PIECES // 2)) * WC
                return fc16[:, at:at + WC], fc16[:, at + N_FC:at + N_FC + WC], w_scale[:, 0:1]
            at = (n - FC_PIECES) * WC
            return pj16[:, at:at + WC], pj16[:, at + N_PJ:at + N_PJ + WC], w_scale[:, 1:2]

        def piece_loads(n):
            return 16 * sum(2 if FC_PIECES // 2 <= m < FC_PIECES else 1 for m in range(n % N_BUF, n + 1, N_BUF))

        def x_tiles(c):
            if c == B // 2:
                return xg[0:B, 2 * B, :], xr16[0:B, 2 * B, :]
            return tuple(a[:, 0:2 * B, :].rearrange("p (l b) w -> p l b w", l=2)[:, :, 2 * c:2 * c + 2, :] for a in (xg, xr16))

        ones_row = rt[0:2, :, :, :].rearrange("p a k e -> p (a k e)")[:, 0:P]
        delta, rate, turn = sm[:, 9], sm[:, 10], sm[:, 11]
        T0_BANK, Y0_BANK = 0, 2
        TILE_ORDER = [8 * lt + b for c in range(B // 2) for lt in range(2) for b in (2 * c, 2 * c + 1)] + [2 * B]
        ps = ctx.enter_context(nc.psum_tensor("ps", [P, 8, 512], F32))
        pf = ps[:, :, :].rearrange("p k n -> p (k n)")
        x3_ps = ps[:, 4, 0:3 * P // 2].bitcast(F16)

        idx_in, ssm_in, const_in, tokw_in = sem("idx_in"), sem("ssm_in"), sem("const_in"), sem("tokw_in")
        four_in, wmax_taken, wmax_ready = sem("four_in"), sem("wmax_taken"), sem("wmax_ready")
        stat_in = [sem(f"stat_in{i}") for i in range(2)]
        piece_in = [sem(f"piece_in{i}") for i in range(N_BUF)]
        wmax_ps, diag_ready, scale_ps, scale_ready = sem("wmax_ps"), sem("diag_ready"), sem("scale_ps"), sem("scale_ready")
        piece_scaled, piece_high, low_vec, low_pool = sem("piece_scaled"), sem("piece_high"), sem("low_vec"), sem("low_pool")
        xhigh_ready, xlow_ready = sem("xhigh_ready"), sem("xlow_ready")
        raw2_in, raw1_in = sem("raw2_in"), sem("raw1_in")
        byb1_ready, byb0_ready = sem("byb1_ready"), sem("byb0_ready")
        raw0_in = [sem("raw0a_in"), sem("raw0b_in")]
        vec_own = sem("vec_own")
        edge_zero = sem("edge_zero")
        abs_ready, e_ready, w_ready, ln_ready = sem("abs_ready"), sem("e_ready"), sem("w_ready"), sem("ln_ready")
        rate_ready = sem("rate_ready")
        env1_ready, turn1_ready, frac1_ready, sin1_ready = (sem("env1_ready"), sem("turn1_ready"),
                                                            sem("frac1_ready"), sem("sin1_ready"))
        yenv_ready, yturn_ready, yfrac_ready, ysin_ready, ytab_ready = (
            sem("yenv_ready"), sem("yturn_ready"), sem("yfrac_ready"), sem("ysin_ready"), sem("ytab_ready"))
        xenv_ready, xturn_ready, xfrac_ready, xsin_ready, xtab_ready = (
            sem("xenv_ready"), sem("xturn_ready"), sem("xfrac_ready"), sem("xsin_ready"), sem("xtab_ready"))
        kps_ready, ksb_ready, khat_ps, khat_ready = (sem("kps_ready"), sem("ksb_ready"), sem("khat_ps"),
                                                     sem("khat_ready"))
        t2_ps, t2_sb, t1_ps, t1_sb = sem("t2_ps"), sem("t2_sb"), sem("t1_ps"), sem("t1_sb")
        y2_ps, y2_sb, y1_ps, y1_sb = sem("y2_ps"), sem("y2_sb"), sem("y1_ps"), sem("y1_sb")
        z_ps, z_sb = sem("z_ps"), sem("z_sb")
        t0_ps, t0_sb, y0_ps, y0_sb = sem("t0_ps"), sem("t0_sb"), sem("y0_ps"), sem("y0_sb")
        h_ps, h_sb, u_ready = sem("h_ps"), sem("h_sb"), sem("u_ready")
        uhat_ps, prod_ready, yhat_ready = sem("uhat_ps"), sem("prod_ready"), sem("yhat_ready")
        y_ps, h2_ready, x_ready = sem("y_ps"), sem("h2_ready"), sem("x_ready")
        xt_ps, xt_sb, logit_ps = sem("xt_ps"), sem("xt_sb"), sem("logit_ps")
        gap_ready, gexp_ready, gates_ready = sem("gap_ready"), sem("gexp_ready"), sem("gates_ready")
        cast_ready, oh_ready, rank_ps, pick_ready, slot_ps = (sem("cast_ready"), sem("oh_ready"), sem("rank_ps"),
                                                              sem("pick_ready"), sem("slot_ps"))
        expert_ready, idx_ready = sem("expert_ready"), sem("idx_ready")
        base_out, x_out = sem("base_out"), sem("x_out")
        added, xs_clear = sem("added"), sem("xs_clear")
        xs_in = [sem(f"xs_in{i}") for i in range(4)]
        bt_ps, bt_sb, fc_ps = sem("bt_ps"), sem("bt_sb"), sem("fc_ps")
        ht_ps = sem("ht_ps")
        hs_ready, hh_ready, hl_ready = sem("hs_ready"), sem("hh_ready"), sem("hl_ready")
        pj_ps, o_ready = sem("pj_ps"), sem("o_ready")
        gate_seen = sem("gate_seen")

        veps_ready, rstd_ready = sem("veps_ready"), sem("rstd_ready")
        ROOTS = 2 * ([(P, ((2 * c, 2 * c + 2), (8 + 2 * c, 10 + 2 * c))) for c in range(B // 2)] + [(B, ((16, 17),))])

        block = ctx.enter_context(nc.Block())

        @block.sync
        def _(sp):
            sp.dma_start(id2[:, :], t["id2"]).then_inc(idx_in, 16)
            sp.dma_start(id1[:, :], t["id1"]).then_inc(idx_in, 16)
            sp.dma_start(id0[:, :], t["id0"]).then_inc(idx_in, 16)
            for n, name in enumerate(("a_real", "a_imag", "b_mat", "c_mat")):
                for half in range(2):
                    sp.dma_start(ssm[NS * half:NS * half + NS, n, :], t[name]).then_inc(ssm_in, 16)
            sp.dma_start(w2[:, :, :], t["w2"]).then_inc(tokw_in, 16)
            sp.dma_start(w1[:, :, :], t["w1"]).then_inc(tokw_in, 16)
            sp.dma_start(w0[:, :], t["w0"]).then_inc(tokw_in, 16)
            sp.dma_start(tb[:, :], t["tb"]).then_inc(tokw_in, 16)
            sp.dma_start(wf[:, :, :], t["wf"]).then_inc(tokw_in, 16)
            sp.dma_start(zt[80:81, :, :], t["bf"].unsqueeze(1).broadcast_to([1, B, D])).then_inc(tokw_in, 16)
            sp.dma_start(zt[81:82, :, :], t["cls"].unsqueeze(1).broadcast_to([1, B, D])).then_inc(tokw_in, 16)
            sp.dma_start(interp[:, :], t["interp"]).then_inc(tokw_in, 16)
            sp.dma_start(last_interp[:, :, :], t["last_interp"]).then_inc(tokw_in, 16)
            sp.dma_start(fwd_k[:, :, :], t["fwd_k"]).then_inc(four_in, 16)
            sp.dma_start(fwd[:, :, :], t["fwd"]).then_inc(four_in, 16)
            sp.dma_start(inv[:, :, :], t["inv"]).then_inc(four_in, 16)
            sp.dma_start(wga[:, :], t["w_gate"][0:P, :]).then_inc(four_in, 16)
            sp.dma_start(wgb[:, :], t["w_gate"][P:D, :]).then_inc(four_in, 16)
            for n in range(2 * STAT_PIECES):
                if n >= 2:
                    sp.wait_ge(wmax_taken, n - 1)
                w = t["w_fc"] if n < STAT_PIECES else t["w_proj"]
                flat = w.rearrange("a b -> (a b)").rearrange("(p n) -> p n", p=P)
                at = (n % STAT_PIECES) * WC
                sp.dma_start(stage[:, n % 2, :], flat[:, at:at + WC]).then_inc(stat_in[n % 2], 16)
            sp.wait_ge(wmax_taken, 2 * STAT_PIECES)
            sp.wait_ge(khat_ps, 1)
            for n in range(PIECES):
                if n == 2:
                    sp.wait_ge(uhat_ps, B // 2)
                if n >= N_BUF:
                    m = n - N_BUF
                    if m in VEC_PIECES:
                        sp.wait_ge(low_vec, VEC_PIECES.index(m) + 1)
                    else:
                        sp.wait_ge(low_pool, POOL_PIECES.index(m) + 1)
                at = (n % (FC_PIECES // 2)) * WC
                if n < FC_PIECES // 2:
                    sp.dma_start(piece_buffer(n), t["w_fc"][0:P, at:at + WC]).then_inc(piece_in[n % N_BUF], 16)
                elif n < FC_PIECES:
                    for k in range(2):
                        sp.dma_start(piece_buffer(n)[D2 * k:D2 * k + D2], t["w_fc"][P:D, at:at + WC]).then_inc(
                            piece_in[n % N_BUF], 16)
                else:
                    at = (n - FC_PIECES) * WC
                    sp.dma_start(piece_buffer(n), t["w_proj"][:, at:at + WC]).then_inc(piece_in[n % N_BUF], 16)
            sp.wait_ge(h2_ready, 2 * B + 1)
            for lt in range(2):
                sp.dma_start(out[:, P * lt:P * lt + P, :].rearrange("b l d -> l b d"), h[:, lt]).then_inc(base_out, 16)
            sp.dma_start(out[:, NT, :], h_last[:, :]).then_inc(base_out, 16)
            rows = x_rows.rearrange("(b l) w -> l b w", b=B)
            sp.wait_ge(gates_ready, 1)
            sp.wait_ge(xlow_ready, B // 2 + 1)
            for lt in range(2):
                sp.dma_start(rows[P * lt:P * lt + P], xr[:, B * lt:B * lt + B, :]).then_inc(x_out, 16)
            sp.dma_start(rows[NT], xr[0:B, 2 * B, :]).then_inc(x_out, 16)
            sp.wait_ge(base_out, 48)
            sp.wait_ge(x_out, 48)

        @block.gpsimd
        def _(pool):
            nc.gpsimd.memset(y0t[:, :, 0:1], 0.0).then_inc(edge_zero, 1)
            nc.gpsimd.memset(mhalf[:, :], -0.5).then_inc(edge_zero, 1)
            nc.gpsimd.memset(ones_row, 1.0).then_inc(edge_zero, 1)
            pool.wait_ge(idx_in, 48)
            for q in range(2):
                nc.gpsimd.indirect_dma_start(raw2[:, q, :], None, t["px2"], bass.IndirectOffsetOnAxis(
                    ap=id2[:, q:q + 1].bitcast(U32), axis=0)).then_inc(raw2_in, 16)
            for g in range(8):
                nc.gpsimd.indirect_dma_start(raw1[:, g, :], None, t["px1"], bass.IndirectOffsetOnAxis(
                    ap=id1[:, g:g + 1].bitcast(U32), axis=0)).then_inc(raw1_in, 16)
            for half in range(2):
                for g in range(GP):
                    nc.gpsimd.indirect_dma_start(
                        raw0[:, half, g * B * 3:(g + 1) * B * 3], None, t["px0"], bass.IndirectOffsetOnAxis(
                            ap=id0[:, half * GP + g:half * GP + g + 1].bitcast(U32), axis=0)).then_inc(raw0_in[half], 16)
            def root(n):
                np_, tiles = ROOTS[n]
                pool.wait_ge(veps_ready, n + 1)
                for j0, j1 in tiles:
                    ins = nc.gpsimd.tensor_tensor(rstd[0:np_, j0:j1], veps[0:np_, j0:j1], mhalf[0:np_, j0:j1], ALU.pow)
                ins.then_inc(rstd_ready, 1)

            pool.wait_ge(edge_zero, 3)
            for n in range(5):
                root(n)
            for c in range(B // 2):
                pool.wait_ge(prod_ready, c + 1)
                pr = prod[:, c % 2].rearrange("p k (f n) -> p k f n", f=2)
                for part, op in ((0, ALU.subtract), (1, ALU.add)):
                    dst = yhat[:, 2 * part:2 * part + 2, 2 * c:2 * c + 2, :].rearrange("p f b d -> p f (b d)")
                    last = nc.gpsimd.tensor_tensor(dst, pr[:, 2 * part], pr[:, 2 * part + 1], op)
                last.then_inc(yhat_ready, 1)

            def x_low(c):
                pool.wait_ge(xhigh_ready, c + 1)
                whole, parts = x_tiles(c)
                nc.gpsimd.tensor_tensor(parts[..., D:D + D2], whole[..., P:D], parts[..., P:D], ALU.subtract)
                nc.gpsimd.tensor_tensor(parts[..., D + D2:D + D2 + P], whole[..., 0:P], parts[..., 0:P],
                                        ALU.subtract).then_inc(xlow_ready, 1)

            def low_parts(*pieces):
                for n in pieces:
                    assert n in POOL_PIECES
                    pool.wait_ge(piece_high, n + 1)
                    high, low, _ = piece_parts(n)
                    nc.gpsimd.tensor_tensor(low, piece_buffer(n), high, ALU.subtract).then_inc(low_pool, 1)

            for c, pieces in enumerate((POOL_PIECES[0:2], POOL_PIECES[2:3], POOL_PIECES[3:4], (), ())):
                root(5 + c)
                x_low(c)
                low_parts(*pieces)
            low_parts(*POOL_PIECES[4:])

            def gather(q, r):
                nc.gpsimd.indirect_dma_start(xs[:, r, :], None, x_rows, bass.IndirectOffsetOnAxis(
                    ap=gcol[:, r:r + 1].bitcast(U32), axis=0), bounds_check=ROWS - 1,
                    oob_is_err=False).then_inc(xs_in[r], 16)

            def step(q, r, more=True, first=False):
                i = 4 * q + r + 1
                if not isinstance(i, int):
                    i, blocks_out, rows_added = pool.to_reg(i), pool.to_reg(i + 1), pool.to_reg(16 * i)
                else:
                    blocks_out, rows_added = i + 1, 16 * i
                if more:
                    pool.wait_ge(idx_ready, 1)
                    pool.wait_ge(o_ready, i)
                    gather(q + 1, r)
                pool.wait_ge(idx_ready, 1)
                pool.wait_ge(o_ready, blocks_out)
                pool.wait_ge(added, rows_added)
                scatter((r + 1) % 4, (r + 1) % 2)

            def scatter(r, par):
                nc.gpsimd.indirect_dma_start(out_rows, bass.IndirectOffsetOnAxis(
                    ap=scol[:, r:r + 1].bitcast(U32), axis=0), o_sb[:, par, :], None, bounds_check=ROWS - 1,
                    oob_is_err=False, compute_op=ALU.add).then_inc(added, 16)

            pool.wait_ge(idx_ready, 1)
            pool.wait_ge(xs_clear, 1)
            pool.wait_ge(x_out, 48)
            for r in range(4):
                gather(0, r)
            pool.wait_ge(base_out, 48)
            pool.wait_ge(o_ready, 1)
            scatter(0, 0)
            with pool.Fori(0, NBLK // 4 - 1) as q:
                for r in range(4):
                    step(q, r)
            for r in range(3):
                step(NBLK // 4 - 1, r, more=False)
            pool.wait_ge(added, 16 * NBLK)

        @block.scalar
        def _(act):
            act.dma_start(ssm[:, 4, :], t["log_delta"].partition_broadcast(P)).then_inc(ssm_in, 16)
            act.dma_start(cst[:, :], t["consts"]).then_inc(const_in, 16)

            act.wait_ge(abs_ready, 1)
            nc.scalar.activation(sm[:, 1], sm[:, 0], ACT.Exp, scale=-1.0).then_inc(e_ready, 1)
            act.wait_ge(w_ready, 1)
            nc.scalar.activation(sm[:, 3], sm[:, 2], ACT.Ln).then_inc(ln_ready, 1)
            act.wait_ge(rate_ready, 1)
            nc.scalar.activation(sm[:, 8], rate, ACT.Exp)
            nc.scalar.activation(sm[:, 12], rate, ACT.Exp, scale=float(NT)).then_inc(env1_ready, 1)
            for b in range(TB):
                ins = nc.scalar.activation(ye[:, :, b], rate, ACT.Exp, scale=float(b))
            ins.then_inc(yenv_ready, 1)
            for a in range(TA):
                ins = nc.scalar.activation(xtab[:, :, a], rate, ACT.Exp, scale=float(TB * a))
            ins.then_inc(xenv_ready, 1)

            act.wait_ge(const_in, 16)
            for k, steps in enumerate((1, 1, NT)):
                ins = nc.scalar.activation(trig1[:, k], turn, ACT.Identity, scale=float(steps),
                                           bias=C["off"][:, 3 + k:4 + k])
            ins.then_inc(turn1_ready, 1)
            for k in range(2):
                for b in range(TB):
                    ins = nc.scalar.activation(ytab[:, k, :, b], turn, ACT.Identity, scale=float(b),
                                               bias=C["off"][:, 1 + k:2 + k])
                ins.then_inc(yturn_ready, 1)

            def xturns(k):
                if k >= 2:
                    act.wait_ge(xtab_ready, k - 1)
                for a in range(XP):
                    ins = nc.scalar.activation(xe[:, k % 2, :, a], turn, ACT.Identity,
                                               scale=float(TB * (k * XP + a)), bias=C["off"][:, 0:1])
                ins.then_inc(xturn_ready, 1)

            def xsines(k):
                act.wait_ge(xfrac_ready, k + 1)
                nc.scalar.activation(xe[:, k % 2], xe[:, k % 2], ACT.Sin, scale=TWO_PI).then_inc(xsin_ready, 1)

            def level12():
                act.wait_ge(raw1_in, 16 * 8)
                nc.scalar.activation(byb1, raw1.rearrange("p g (b c) -> p b g c", b=B),
                                     ACT.Copy).then_inc(byb1_ready, 1)
                act.wait_ge(t1_ps, 1)
                nc.scalar.activation(t1.rearrange("p b s -> p (b s)"), pf[0:96, 2048:3072], ACT.Copy).then_inc(t1_sb, 1)
                act.wait_ge(tokw_in, 16 * 9)
                act.wait_ge(y2_ps, 1)
                nc.scalar.activation(y2t.rearrange("p b s -> p (b s)"), ps[0:EMB, 7, 0:B * 16],
                                     ACT.Identity, bias=tb[:, 2:3]).then_inc(y2_sb, 1)
                act.wait_ge(y1_ps, 1)
                nc.scalar.activation(y1t.rearrange("p b s -> p (b s)"), ps[0:EMB, 6, 0:512],
                                     ACT.Identity, bias=tb[:, 1:2]).then_inc(y1_sb, 1)

            def level12_fused():
                for k, rows, bank in ((0, 64, 0), (64, 16, 4)):
                    act.wait_ge(z_ps, 1 + k // 64)
                    nc.scalar.activation(zt[k:k + rows].rearrange("p (g b) d -> p g (b d)", b=2),
                                         ps[0:rows, bank:bank + 4, 0:2 * D], ACT.Copy).then_inc(z_sb, 1)

            def level0(half):
                act.wait_ge(raw0_in[half], 16 * GP)
                nc.scalar.activation(byb0[:, half].rearrange("p b (g c) -> p b g c", g=GP),
                                     raw0[:, half].rearrange("p (g b c) -> p b g c", g=GP, b=B),
                                     ACT.Copy).then_inc(byb0_ready, 1)
                act.wait_ge(t0_ps, half + 1)
                nc.scalar.activation(t0[:, half].rearrange("p b s -> p (b s)"),
                                     pf[0:48, T0_BANK * 512:T0_BANK * 512 + 1024], ACT.Copy).then_inc(t0_sb, 1)
                for c in range(2):
                    act.wait_ge(y0_ps, 2 * half + c + 1)
                    nc.scalar.activation(
                        y0t[:, 4 * c:4 * c + 4, 1 + P * half:1 + P * half + P],
                        ps[0:EMB, Y0_BANK + c, :].rearrange("p (b s) -> p b s", b=4),
                        ACT.Identity, bias=tb[:, 0:1]).then_inc(y0_sb, 1)

            def fused(half):
                for c in range(4):
                    act.wait_ge(h_ps, 4 * half + c + 1)
                    nc.scalar.activation(h[:, half, 2 * c:2 * c + 2, :].rearrange("p b d -> p (b d)"),
                                         ps[:, c, 0:2 * D], ACT.Copy).then_inc(h_sb, 1)

            xturns(0)
            act.wait_ge(frac1_ready, 1)
            nc.scalar.activation(trig1[:, :], trig1[:, :], ACT.Sin, scale=TWO_PI).then_inc(sin1_ready, 1)
            level12()
            for k in range(2):
                act.wait_ge(yfrac_ready, k + 1)
                nc.scalar.activation(ytab[:, k], ytab[:, k], ACT.Sin, scale=TWO_PI).then_inc(ysin_ready, 1)
            level12_fused()
            xturns(1)
            xsines(0)
            level0(0)
            xturns(2)
            xsines(1)
            fused(0)
            xturns(3)
            xsines(2)
            xsines(3)
            level0(1)
            fused(1)
            act.wait_ge(h_ps, B + 1)
            nc.scalar.activation(h_last[:, :], ps[0:B, 0, 0:D], ACT.Copy).then_inc(h_sb, 1)
            act.wait_ge(khat_ps, 1)
            nc.scalar.activation(khat[:, :, :].rearrange("p (x y) d -> p x (y d)", x=2), ps[:, 4:6, 0:2 * D], ACT.Copy)
            nc.scalar.activation(k0[:, :, :].rearrange("p k d -> p (k d)"), ps[0:B, 6, 0:2 * D],
                                 ACT.Copy)
            nc.scalar.activation(k0u[:, 1], ps[0:B, 7, 0:D], ACT.Copy).then_inc(khat_ready, 1)

            def high_parts(*pieces):
                for n in pieces:
                    act.wait_ge(piece_in[n % N_BUF], piece_loads(n))
                    high, _, scale = piece_parts(n)
                    if n in POOL_PIECES:
                        nc.scalar.activation(piece_buffer(n), piece_buffer(n), ACT.Copy, scale=scale).then_inc(
                            piece_scaled, 1)
                        act.wait_ge(piece_scaled, POOL_PIECES.index(n) + 1)
                        scale = 1.0
                    nc.scalar.activation(high, piece_buffer(n), ACT.Copy, scale=scale).then_inc(piece_high, 1)

            act.wait_ge(scale_ready, 1)
            high_parts(0, 1, 2, 3, 4, 5)
            act.wait_ge(yhat_ready, B // 2)
            for c, (before, after) in enumerate((((6,), (7, 8)), ((), (9, 10, 11)), ((), (12, 13)), ((), (14,)), ((), (15,)))):
                act.wait_ge(x_ready, 4 * c + 4 if c < B // 2 else TILES)
                whole, parts = x_tiles(c)
                nc.scalar.activation(parts[..., 0:D], whole, ACT.Copy).then_inc(xhigh_ready, 1)
                high_parts(*before)
                act.wait_ge(xt_ps, c + 1)
                for k, bank, rows in ((0, 4, P), (1, 5, D2)):
                    if c < B // 2:
                        ins = nc.scalar.activation(xt[0:rows, 4 * c:4 * c + 4, k, :],
                                                   ps[0:rows, bank, :].rearrange("p (k s) -> p k s", k=4), ACT.Copy)
                    else:
                        ins = nc.scalar.activation(xt[0:rows, 2 * B, k, 0:B], ps[0:rows, bank, 0:B], ACT.Copy)
                ins.then_inc(xt_sb, 1)
                high_parts(*after)
            act.wait_ge(gap_ready, 1)
            nc.scalar.activation(rs[:, 5], rs[:, 4], ACT.Exp).then_inc(gexp_ready, 1)

            high_parts(*range(16, PIECES))

            def gelu(i, par):
                act.wait_ge(fc_ps, i + 1)
                nc.scalar.activation(hs[:, par].rearrange("p (k n) -> p k n", k=2), ps[:, 0:2, 0:H // 2],
                                     ACT.Gelu_apprx_tanh, scale=fc_back).then_inc(hs_ready, 1)
                act.wait_ge(ht_ps, i + 1)
                nc.scalar.activation(hh[:, par].rearrange("p (k n) -> p k n", k=2), ps[:, 2:4, 0:H // 2], ACT.Copy, scale=h_scale).then_inc(hh_ready, 1)

            with act.Fori(0, NBLK // 2) as q:
                for par in range(2):
                    gelu(2 * q + par, par)

        @block.vector
        def _(dve):
            own = Chain(dve, vec_own)
            v = nc.vector
            AR, AI, BM, CM, LD = (ssm[:, n] for n in range(5))

            dve.wait_ge(const_in, 16)
            dve.wait_ge(ssm_in, 16 * 9)
            v.scalar_tensor_tensor(out=sm[:, 0], in0=LD, scalar=-1.0, in1=LD, op0=ALU.mult,
                                   op1=ALU.max).then_inc(abs_ready, 1)
            dve.wait_ge(e_ready, 1)
            v.tensor_scalar(sm[:, 2], sm[:, 1], 1.0, None, ALU.add).then_inc(w_ready, 1)
            dve.wait_ge(w_ready, 1)
            own.inc(v.scalar_tensor_tensor(out=sm[:, 4], in0=sm[:, 2], scalar=-1.0, in1=sm[:, 1], op0=ALU.add,
                                           op1=ALU.subtract))
            own.link(v.reciprocal(sm[:, 5], sm[:, 2]))
            own.link(v.tensor_tensor(sm[:, 4], sm[:, 4], sm[:, 5], ALU.mult))
            dve.wait_ge(ln_ready, 1)
            own.link(v.scalar_tensor_tensor(out=sm[:, 5], in0=LD, scalar=0.0, in1=sm[:, 3], op0=ALU.max, op1=ALU.add))
            own.link(v.tensor_tensor(delta, sm[:, 5], sm[:, 4], ALU.subtract))
            v.tensor_tensor(rate, AR, delta, ALU.mult)
            v.scalar_tensor_tensor(out=turn, in0=AI, scalar=1.0 / (2.0 * np.pi), in1=delta, op0=ALU.mult,
                                   op1=ALU.mult).then_inc(rate_ready, 1)
            dve.wait_ge(rate_ready, 1)
            own.inc(v.tensor_tensor(sm[:, 0], AR, AR, ALU.mult))
            own.link(v.tensor_tensor(sm[:, 1], AI, AI, ALU.mult))
            own.link(v.tensor_tensor(sm[:, 0], sm[:, 0], sm[:, 1], ALU.add))
            own.link(v.reciprocal(sm[:, 1], sm[:, 0]))
            own.link(v.tensor_tensor(sm[:, 2], BM, CM, ALU.mult))
            own.link(v.tensor_tensor(sm[:, 0], sm[:, 1], sm[:, 2], ALU.mult))

            def fraction(dst, tmp, done, n):
                own.link(v.tensor_scalar(tmp, dst, MAGIC, -MAGIC, ALU.add, ALU.add))
                v.tensor_tensor(dst, dst, tmp, ALU.subtract).then_inc(done, 1)
                dve.wait_ge(done, n)

            taken = [0]

            def weight_max(count):
                for n in range(taken[0], taken[0] + count):
                    dve.wait_ge(stat_in[n % 2], 16 * (n // 2 + 1))
                    v.tensor_reduce(wmax[:, n:n + 1], stage[:, n % 2, :], AX.X, ALU.max,
                                    apply_absolute_value=True).then_inc(wmax_taken, 1)
                taken[0] += count

            dve.wait_ge(turn1_ready, 1)
            fraction(trig1, scr.rearrange("p d b -> p (d b)")[:, 0:3 * D].rearrange("p (k d) -> p k d", k=3),
                     frac1_ready, 1)
            dve.wait_ge(t2_ps, 1)
            v.tensor_copy(t2.rearrange("p q b s -> p (q b s)"), pf[0:48, 0:2048]).then_inc(t2_sb, 1)
            for k in range(2):
                dve.wait_ge(yturn_ready, k + 1)
                fraction(ytab[:, k], scr, yfrac_ready, k + 1)
            weight_max(4)
            dve.wait_ge(sin1_ready, 1)
            dve.wait_ge(env1_ready, 1)
            own.inc(v.tensor_tensor(sm[:, 12], sm[:, 12], trig1[:, 2], ALU.mult))
            own.inc(v.tensor_tensor(sm[:, 1], sm[:, 8], trig1[:, 0], ALU.mult))
            own.link(v.tensor_tensor(sm[:, 2], sm[:, 8], trig1[:, 1], ALU.mult))
            own.link(v.tensor_scalar(sm[:, 1], sm[:, 1], -1.0, None, ALU.add))
            for n, (x, y) in enumerate(((sm[:, 1], AR), (sm[:, 2], AI), (sm[:, 2], AR), (sm[:, 1], AI))):
                own.inc(v.tensor_tensor(sm[:, 4 + n], x, y, ALU.mult))
            own.sync()
            own.inc(v.tensor_tensor(sm[:, 3], sm[:, 4], sm[:, 5], ALU.add))
            own.link(v.tensor_tensor(sm[:, 7], sm[:, 6], sm[:, 7], ALU.subtract))
            own.inc(v.tensor_tensor(sm[:, 3], sm[:, 3], sm[:, 0], ALU.mult))
            own.link(v.tensor_tensor(sm[:, 4], sm[:, 7], sm[:, 0], ALU.mult))
            weight_max(4)
            dve.wait_ge(ysin_ready, 2)
            dve.wait_ge(yenv_ready, 1)
            for k in range(2):
                own.inc(v.tensor_tensor(ytab[:, k], ytab[:, k], bc(sm[:, 3 + k], 2, TB), ALU.mult))
            own.sync()
            own.link(v.tensor_tensor(ytab[:, 0], ytab[:, 0], ytab[:, 1], ALU.add))
            own.link(v.tensor_tensor(ytab[:, 0], ytab[:, 0], ye, ALU.mult))
            v.tensor_tensor(sm[:, 13], sm[:, 12], ytab[:, 0, :, 0], ALU.mult).then_inc(ytab_ready, 1)

            def part(k):
                dve.wait_ge(xturn_ready, k + 1)
                fraction(xe[:, k % 2], scr, xfrac_ready, k + 1)

            def part_done(k):
                dve.wait_ge(xsin_ready, k + 1)
                if k == 0:
                    dve.wait_ge(xenv_ready, 1)
                v.tensor_tensor(xtab[:, :, k * XP:(k + 1) * XP], xtab[:, :, k * XP:(k + 1) * XP], xe[:, k % 2],
                                ALU.mult).then_inc(xtab_ready, 1)

            def norm(j, np_, src, dst):
                return v.tensor_scalar(dst, src, mv[0:np_, j, 0:1], rstd[0:np_, j:j + 1], ALU.subtract, ALU.mult)

            roots = [0]

            def root(np_, *tiles):
                assert (np_, tiles) == ROOTS[roots[0]]
                for j0, j1 in tiles:
                    ins = v.tensor_scalar(veps[0:np_, j0:j1], mv[0:np_, j0:j1, 1], EPS, None, ALU.add)
                roots[0] += 1
                ins.then_inc(veps_ready, 1)
                dve.wait_ge(rstd_ready, roots[0])

            part(0)
            weight_max(2)
            part(1)
            weight_max(1)
            part_done(0)
            part(2)
            weight_max(2)
            part_done(1)
            weight_max(1)
            for b in range(B):
                dve.wait_ge(h_sb, b // 2 + 1)
                own.inc(v.bn_stats(stats[:, b], h[:, 0, b]))
            own.sync()
            for b in range(B):
                own.inc(v.bn_aggr(mv[:, b], stats[:, b]))
            part(3)
            part_done(2)
            weight_max(2)
            part_done(3)
            weight_max(2)
            assert taken[0] == 2 * STAT_PIECES
            dve.wait_ge(wmax_taken, 2 * STAT_PIECES)
            v.tensor_reduce(wmax[:, 2 * STAT_PIECES:], wmax[:, 0:2 * STAT_PIECES].rearrange("p (w n) -> p w n", w=2), AX.X,
                            ALU.max).then_inc(wmax_ready, 1)
            for c in range(B // 2):
                dve.wait_ge(h_sb, 4 + c + 1)
                for b in (2 * c, 2 * c + 1):
                    own.inc(v.bn_stats(stats[:, 8 + b], h[:, 1, b]))
                own.sync()
                for b in (2 * c, 2 * c + 1):
                    own.inc(v.bn_aggr(mv[:, 8 + b], stats[:, 8 + b]))
                own.sync()
                root(P, (2 * c, 2 * c + 2), (8 + 2 * c, 10 + 2 * c))
                for half in range(2):
                    for b in (2 * c, 2 * c + 1):
                        ins = norm(8 * half + b, P, h[:, half, b], u[:, half, b])
                ins.then_inc(u_ready, 1)
            dve.wait_ge(h_sb, 9)
            own.link(v.bn_stats(stats[0:B, 16], h_last[:, :]))
            own.link(v.bn_aggr(mv[0:B, 16], stats[0:B, 16]))
            root(B, (16, 17))
            own.link(norm(16, B, h_last[:, :], u_last[:, :]))
            dve.wait_ge(wmax_ps, 1)
            own.link(v.tensor_reduce(wmax_all[:, 0:1], ps[0:2, 7, 0:P], AX.X, ALU.max))
            v.tensor_scalar(wmax_all[:, 2:4], ident[0:2, 0:2], wmax_all[:, 0:1], None, ALU.mult).then_inc(diag_ready, 1)
            dve.wait_ge(kps_ready, 1)
            v.tensor_tensor(kmask.rearrange("p (g c) b -> p g c b", c=CG),
                            pf[:, 2048:2048 + D * TB].rearrange("p (g c b) -> p g c b", c=CG, b=TB),
                            bc(bc(C["cmask"], 1, NG), 3, TB), ALU.mult).then_inc(ksb_ready, 1)
            dve.wait_ge(scale_ps, 1)
            own.link(v.tensor_copy(wsc[:, 0:2], ps[:, 7, 2 * P:2 * P + 2]))
            own.link(v.tensor_scalar(wsc_i[:, 0:2], wsc_i[:, 0:2], 23, None, ALU.arith_shift_right))
            own.link(v.tensor_scalar(wsc_i[:, 0:2], wsc_i[:, 0:2], 72, 198, ALU.max, ALU.min))
            own.inc(v.tensor_scalar(wsc_i[:, 2:4], wsc_i[:, 0:2], -1, 262, ALU.mult, ALU.add))
            own.inc(v.tensor_scalar(wsc_i[:, 4:5], wsc_i[:, 0:1], -8, None, ALU.add))
            own.inc(v.tensor_scalar(wsc_i[:, 5:6], wsc_i[:, 0:1], -1, 261, ALU.mult, ALU.add))
            own.inc(v.tensor_tensor(wsc_i[:, 6:7], wsc_i[:, 0:1], wsc_i[:, 1:2], ALU.add))
            own.sync()
            own.link(v.tensor_scalar(wsc_i[:, 6:7], wsc_i[:, 6:7], -142, None, ALU.add))
            v.tensor_scalar(wsc_i[:, 9:14], wsc_i[:, 2:7], 23, None, ALU.arith_shift_left).then_inc(scale_ready, 1)
            own.inc(v.tensor_copy(ident16[:, :], ident))
            dve.wait_ge(khat_ready, 1)
            own.inc(v.tensor_tensor(k0u[:, 1], k0u[:, 1], k0[:, 1], ALU.mult))
            own.inc(v.tensor_tensor(k0u[:, 0], u_last[:, :], k0[:, 0], ALU.mult))

            def low_parts(*pieces):
                for n in pieces:
                    assert n in VEC_PIECES
                    dve.wait_ge(piece_high, n + 1)
                    high, low, scale = piece_parts(n)
                    v.scalar_tensor_tensor(out=low, in0=piece_buffer(n), scalar=scale, in1=high, op0=ALU.mult,
                                           op1=ALU.subtract).then_inc(low_vec, 1)

            dve.wait_ge(scale_ready, 1)
            for c in range(B // 2):
                dve.wait_ge(uhat_ps, c + 1)
                if c >= 2:
                    dve.wait_ge(yhat_ready, c - 1)
                base = 4 * (c % 2)
                for n, (x, y) in enumerate(((0, 0), (1, 1), (0, 1), (1, 0))):
                    src = ps[:, base + 2 * x:base + 2 * x + 2, 0:2 * D].rearrange("p f (b d) -> p f b d", b=2)
                    dst = prod[:, c % 2, n].rearrange("p (f b d) -> p f b d", f=2, b=2)
                    ins = v.tensor_tensor(dst, src, bc(khat[:, 2 * y:2 * y + 2, :], 2, 2), ALU.mult)
                ins.then_inc(prod_ready, 1)
                if c in (1, 2):
                    low_parts(c - 1)

            own.inc(v.memset(lg[:, 2 * B], 0.0))
            for c in range(B // 2):
                dve.wait_ge(y_ps, 2 * c + 2)
                for lt in range(2):
                    hv = h[:, lt, 2 * c:2 * c + 2, :].rearrange("p b d -> p (b d)")
                    v.tensor_tensor(hv, hv, ps[:, 2 * (c % 2) + lt, 0:2 * D], ALU.add).then_inc(h2_ready, 1)
                dve.wait_ge(h2_ready, 2 * c + 2)
                for lt in range(2):
                    for b in (2 * c, 2 * c + 1):
                        own.inc(v.bn_stats(stats[:, 8 * lt + b], h[:, lt, b]))
                own.sync()
                for lt in range(2):
                    for b in (2 * c, 2 * c + 1):
                        own.inc(v.bn_aggr(mv[:, 8 * lt + b], stats[:, 8 * lt + b]))
                own.sync()
                root(P, (2 * c, 2 * c + 2), (8 + 2 * c, 10 + 2 * c))
                for lt in range(2):
                    for b in (2 * c, 2 * c + 1):
                        norm(8 * lt + b, P, h[:, lt, b], xg[:, 8 * lt + b, :]).then_inc(x_ready, 1)
                low_parts(*((2, 3), (6, 7), (9, 10), ())[c])
            dve.wait_ge(y_ps, 9)
            own.link(v.tensor_tensor(h_last[:, :], h_last[:, :], ps[0:B, 7, 0:D], ALU.add))
            own.link(v.tensor_tensor(k0u[:, 0], k0u[:, 0], k0u[:, 1], ALU.add))
            v.tensor_tensor(h_last[:, :], h_last[:, :], k0u[:, 0], ALU.add).then_inc(h2_ready, 9)
            dve.wait_ge(h2_ready, 17)
            own.link(v.bn_stats(stats[0:B, 16], h_last[:, :]))
            own.link(v.bn_aggr(mv[0:B, 16], stats[0:B, 16]))
            root(B, (16, 17))
            norm(16, B, h_last[:, :], xg[0:B, 16, :]).then_inc(x_ready, 1)
            low_parts(12, 13)

            own.inc(v.tensor_copy(ltri16[:, :], C["ltri"]))
            own.inc(v.memset(ones16[:, :], 1.0))
            own.inc(v.memset(ohb16[:, TILES], 0.0))
            dve.wait_ge(logit_ps, 1)
            own.inc(v.tensor_copy(lg[:, 0:2 * B].rearrange("p k e -> p (k e)"), ps[:, 6, 0:2 * B * NE]))
            own.link(v.tensor_copy(lg[0:B, 2 * B], ps[0:B, 6, 2 * B * NE:TILES * NE]))
            ew = bc(C["ew"], 1, TILES)

            def pick(src, top, oh):
                own.link(v.tensor_reduce(top, src, AX.X, ALU.max))
                own.link(v.tensor_tensor(rt[:, 0], src, bc(top, 2, NE), ALU.is_equal))
                own.link(v.tensor_tensor(rt[:, 0], rt[:, 0], ew, ALU.mult))
                own.link(v.tensor_reduce(rs[:, 3], rt[:, 0], AX.X, ALU.max))
                own.link(v.tensor_tensor(oh, ew, bc(rs[:, 3], 2, NE), ALU.is_equal))

            pick(lg[:, :, :], rs[:, 0], oh1[:, :, :])
            own.link(v.scalar_tensor_tensor(out=rt[:, 1], in0=oh1[:, :, :], scalar=LOWEST, in1=lg[:, :, :],
                                            op0=ALU.mult, op1=ALU.add))
            pick(rt[:, 1], rs[:, 1], oh2[:, :, :])
            v.tensor_tensor(rs[:, 4], rs[:, 1], rs[:, 0], ALU.subtract).then_inc(gap_ready, 1)
            own.link(v.tensor_tensor(rt[:, 0], oh1[:, :, :], oh2[:, :, :], ALU.add))
            v.tensor_tensor(ohb16[:, 0:TILES], rt[:, 0], bc(C["valid"], 2, NE), ALU.mult).then_inc(oh_ready, 1)
            dve.wait_ge(gexp_ready, 1)
            own.link(v.tensor_scalar(rs[:, 6], rs[:, 5], 1.0, None, ALU.add))
            own.link(v.reciprocal(rs[:, 7], rs[:, 6]))
            own.link(v.tensor_scalar(rs[:, 7], rs[:, 7], out_back, None, ALU.mult))
            own.link(v.tensor_tensor(rs[:, 8], rs[:, 5], rs[:, 7], ALU.mult))
            own.inc(v.tensor_tensor(rt[:, 1], oh1[:, :, :], bc(rs[:, 7], 2, NE), ALU.mult))
            own.link(v.tensor_tensor(rt[:, 2], oh2[:, :, :], bc(rs[:, 8], 2, NE), ALU.mult))
            v.tensor_tensor(xr[:, :, D:XW], rt[:, 1], rt[:, 2], ALU.add).then_inc(gates_ready, 1)
            dve.wait_ge(rank_ps, 1)
            rank = ps[:, 7, 0:(TILES + 1) * NE].rearrange("p (k e) -> p k e", e=NE)
            own.link(v.tensor_scalar(cnt_i[:, :], rank[:, TILES], float(P - 1), None, ALU.add))
            own.link(v.tensor_scalar(cnt_i[:, :], cnt_i[:, :], 7, None, ALU.arith_shift_right))
            own.inc(v.memset(cnt[:, 0], 1.0))
            own.link(v.tensor_copy(cnt[:, 1], cnt_i[:, :]))
            own.link(v.tensor_tensor_scan(cnt[:, 2], cnt[:, 0], cnt[:, 1], 0.0, ALU.mult, ALU.add))
            own.link(v.tensor_tensor(cnt[:, 3], cnt[:, 2], cnt[:, 1], ALU.subtract))
            own.link(v.tensor_scalar(cnt[:, 3], cnt[:, 3], float(P), None, ALU.mult))
            own.link(v.tensor_tensor(rt[:, 0], rank[:, 0:TILES], bc(cnt[:, 3], 1, TILES), ALU.add))
            own.inc(v.tensor_tensor(rt[:, 1], rt[:, 0], oh1[:, :, :], ALU.mult))
            own.link(v.tensor_tensor(rt[:, 2], rt[:, 0], oh2[:, :, :], ALU.mult))
            for n in range(2):
                own.inc(v.tensor_reduce(pos[:, n], rt[:, 1 + n], AX.X, ALU.add))
            own.sync()
            own.link(v.tensor_copy(pos_i[:, :, :], pos[:, :, :]))
            own.inc(v.tensor_scalar(blk_i[:, :, :], pos_i[:, :, :], 7, None, ALU.arith_shift_right))
            own.link(v.tensor_scalar(slt_i[:, :, :], pos_i[:, :, :], P - 1, None, ALU.bitwise_and))
            own.inc(v.tensor_copy(blk_f[:, :], blk_i[:, :, :].rearrange("p k j -> p (k j)")))
            own.link(v.tensor_copy(slt_f[:, :], slt_i[:, :, :].rearrange("p k j -> p (k j)")))
            own.inc(v.tensor_tensor(ohs, bc(C["iota_s"], 1, 2 * TILES), bc(slt_f[:, :], 2, P), ALU.is_equal))
            own.link(v.tensor_tensor(ohb, bc(C["iota_b"], 1, 2 * TILES), bc(blk_f[:, :], 2, NBLK), ALU.is_equal))
            v.tensor_tensor(mvb, bc(ohb, 2, 2),
                            bc(C["ids"].rearrange("p (k c) -> p k c", c=2), 3, NBLK), ALU.mult).then_inc(pick_ready, 1)
            own.link(v.tensor_tensor(ge_t, bc(C["iota_b"], 2, NE), bc(cnt[:, 2], 1, NBLK), ALU.is_ge))
            own.link(v.tensor_reduce(blk_e[:, :], ge_t, AX.X, ALU.add))
            own.link(v.tensor_scalar(blk_e[:, :], blk_e[:, :], float(NE - 1), None, ALU.min))
            v.tensor_copy(blk_ei[:, :], blk_e[:, :]).then_inc(expert_ready, 1)
            own.inc(v.tensor_tensor(gsel_e, bc(C["eidx"], 1, NBLK), bc(blk_e[:, :], 2, NE), ALU.is_equal))
            v.memset(xs, 0.0).then_inc(xs_clear, 1)
            dve.wait_ge(slot_ps, 1)
            own.link(v.tensor_copy(slotv[:, :], ps[:, 0, 0:2 * NBLK]))
            sv = slotv[:, :].rearrange("p (c s) -> p c s", c=2)
            own.link(v.scalar_tensor_tensor(out=idx_f[:, :], in0=sv[:, 1], scalar=256.0, in1=sv[:, 0], op0=ALU.mult,
                                            op1=ALU.add))
            own.link(v.tensor_scalar(idx_f[:, :], idx_f[:, :], -1.0, None, ALU.add))
            own.link(v.tensor_copy(idx[:, :], idx_f[:, :]))
            v.tensor_copy(gcol[:, :], idx[:, 0:4]).then_inc(idx_ready, 1)

            def turned(i, par):
                dve.wait_ge(bt_ps, i + 1)
                v.tensor_copy(x3[:, par], x3_ps).then_inc(bt_sb, 1)

            def output(i, r, first, more=True):
                v.tensor_tensor(gsel[:, r % 2], xs[:, r, D:XW], gsel_e[:, bass.ds(i, 1), :].rearrange("p o e -> p (o e)"),
                                ALU.mult).then_inc(gate_seen, 1)
                dve.wait_ge(gate_seen, 2 * i + 1)
                v.tensor_reduce(gate[:, r % 2:r % 2 + 1], gsel[:, r % 2], AX.X, ALU.add).then_inc(gate_seen, 1)
                dve.wait_ge(gate_seen, 2 * i + 2)
                dve.wait_ge(pj_ps, i + 1)
                if not first:
                    dve.wait_ge(added, 16 * (i - 1))
                v.tensor_copy(scol[:, r:r + 1], idx[:, bass.ds(i, 1)])
                if more:
                    v.tensor_copy(gcol[:, r:r + 1], idx[:, bass.ds(i + 4, 1)])
                v.tensor_scalar(o_sb[:, r % 2], ps[:, 5 + r % 2, 0:D], gate[:, r % 2:r % 2 + 1], None,
                                ALU.mult).then_inc(o_ready, 1)

            def hidden(i, par):
                dve.wait_ge(hh_ready, i + 1)
                v.scalar_tensor_tensor(out=hl[:, par].rearrange("p (k n) -> p k n", k=2), in0=ps[:, 2:4, 0:H // 2],
                                       scalar=h_scale, in1=hh[:, par].rearrange("p (k n) -> p k n", k=2),
                                       op0=ALU.mult, op1=ALU.subtract).then_inc(hl_ready, 1)

            def vstep(q, r, more=True, first=False, gather_more=True):
                i = 4 * q + r + 1
                if more:
                    turned(i + 1, r % 2)
                output(i - 1, r, first, gather_more)
                hidden(i, (r + 1) % 2)

            turned(0, 0)
            turned(1, 1)
            hidden(0, 0)
            for r in range(2):
                vstep(0, r, first=True)
            for r in range(2, 4):
                vstep(0, r)
            with dve.Fori(1, NBLK // 4 - 1) as q:
                for r in range(4):
                    vstep(q, r)
            for r in range(3):
                vstep(NBLK // 4 - 1, r, more=r < 2, gather_more=False)
            output(NBLK - 1, 3, False, False)

        @block.tensor
        def _(pe):
            mm = nc.tensor.matmul
            pe.wait_ge(const_in, 16)
            pe.wait_ge(raw2_in, 32)
            for q in range(2):
                for b in range(B):
                    k = (q * B + b) * P
                    ins = nc.tensor.transpose(pf[0:48, k:k + P], raw2[:, q, b * 48:(b + 1) * 48], ident)
            ins.then_inc(t2_ps, 1)
            pe.wait_ge(byb1_ready, 1)
            for b in range(B):
                k = 2048 + b * P
                ins = nc.tensor.transpose(pf[0:96, k:k + P], byb1[:, b].rearrange("p g c -> p (g c)"), ident)
            ins.then_inc(t1_ps, 1)
            pe.wait_ge(tokw_in, 16 * 9)
            pe.wait_ge(t2_sb, 1)
            for g in range(GP):
                q, gg = g // 8, g % 8
                ins = mm(ps[0:EMB, 7, 0:B * 16], lhsT=w2[:, g, :],
                         rhs=t2[:, q, :, gg * 16:(gg + 1) * 16], start=g == 0, stop=g == GP - 1)
            ins.then_inc(y2_ps, 1)
            pe.wait_ge(t1_sb, 1)
            for k in range(2):
                ins = mm(ps[0:EMB, 6, :], lhsT=w1[:, k, :], rhs=t1[:, :, k * 64:(k + 1) * 64], start=k == 0, stop=k == 1)
            ins.then_inc(y1_ps, 1)
            pe.wait_ge(y1_sb, 1)
            for b in range(B):
                ins = mm(ps[0:64, b // 2, (b % 2) * D:(b % 2) * D + D], lhsT=y1t[:, b, :], rhs=wf[:, 1, :],
                         start=True, stop=True)
            ins.then_inc(z_ps, 1)
            pe.wait_ge(y2_sb, 1)
            for b in range(B):
                ins = mm(ps[0:16, 4 + b // 2, (b % 2) * D:(b % 2) * D + D], lhsT=y2t[:, b, :], rhs=wf[:, 2, :],
                         start=True, stop=True)
            ins.then_inc(z_ps, 1)
            pe.wait_ge(z_sb, 2)

            def level0(half):
                pe.wait_ge(byb0_ready, half + 1)
                for b in range(B):
                    k = T0_BANK * 512 + b * P
                    ins = nc.tensor.transpose(pf[0:48, k:k + P], byb0[:, half, b], ident)
                ins.then_inc(t0_ps, 1)
                pe.wait_ge(t0_sb, half + 1)
                for c in range(2):
                    mm(ps[0:EMB, Y0_BANK + c, :], lhsT=w0[:, :], rhs=t0[:, half, 4 * c:4 * c + 4, :],
                       start=True, stop=True).then_inc(y0_ps, 1)

            def fused(half):
                pe.wait_ge(y0_sb, 2 * half + 2)
                for c in range(4):
                    at = P * half
                    mm(ps[:, c, 0:2 * D], lhsT=interp[:, at:at + P], rhs=zt[:, 2 * c:2 * c + 2, :], start=True, stop=False)
                    for m in range(2):
                        ins = mm(ps[:, c, m * D:(m + 1) * D], lhsT=y0t[:, 2 * c + m, at:at + P], rhs=wf[:, 0, :],
                                 start=False, stop=m == 1)
                    ins.then_inc(h_ps, 1)

            level0(0)
            pe.wait_ge(edge_zero, 1)
            fused(0)
            pe.wait_ge(h_sb, 4)
            level0(1)
            fused(1)
            pe.wait_ge(h_sb, 5)
            mm(ps[0:B, 0, 0:D], lhsT=y0t[:, :, NT], rhs=wf[:, 0, :], start=True, stop=False)
            for b in range(B):
                ins = mm(ps[0:B, 0, 0:D], lhsT=last_interp[:, b, :], rhs=zt[:, b, :], start=False, stop=b == B - 1)
            ins.then_inc(h_ps, 1)
            pe.wait_ge(wmax_ready, 1)
            nc.tensor.transpose(ps[0:2, 7, 0:P], wmax[:, 2 * STAT_PIECES:], ident).then_inc(wmax_ps, 1)
            pe.wait_ge(ytab_ready, 1)
            pe.wait_ge(xtab_ready, 4)
            for g in range(NG):
                ins = mm(pf[:, 2048 + g * CG * TB:2048 + (g + 1) * CG * TB],
                         lhsT=xtab[:, CG * g:CG * g + CG, :].rearrange("p c a -> p (c a)"),
                         rhs=ytab[:, 0, CG * g:CG * g + CG, :], start=True, stop=True)
            ins.then_inc(kps_ready, 1)

            def transform(c):
                pe.wait_ge(u_ready, c + 1)
                if c >= 2:
                    pe.wait_ge(prod_ready, c - 1)
                for kt in range(KT):
                    for m in range(2):
                        ins = mm(ps[:, 4 * (c % 2) + kt, 0:2 * D], lhsT=fwd[:, m, kt * P:(kt + 1) * P],
                                 rhs=u[:, m, 2 * c:2 * c + 2, :], start=m == 0, stop=m == 1)
                ins.then_inc(uhat_ps, 1)

            pe.wait_ge(diag_ready, 1)
            mm(ps[:, 7, 2 * P:2 * P + 2], lhsT=ones_row, rhs=wmax_all[:, 2:4], start=True, stop=True).then_inc(scale_ps, 1)
            pe.wait_ge(four_in, 16 * 5)
            pe.wait_ge(h_sb, 9)
            transform(0)
            pe.wait_ge(ksb_ready, 1)
            for kt in range(KT):
                dst = ps[:, 4 + kt // 2, (kt % 2) * D:(kt % 2) * D + D]
                for b in range(TB):
                    mm(dst, lhsT=fwd_k[:, b, kt * P:(kt + 1) * P], rhs=kmask[:, :, b], start=b == 0, stop=b == TB - 1)
            mm(ps[0:B, 6, 0:D], lhsT=C["half0"], rhs=ytab[:, 0, :, 0], start=True, stop=True)
            mm(ps[0:B, 6, D:2 * D], lhsT=C["ones"], rhs=sm[:, 13], start=True, stop=True)
            pe.wait_ge(scale_ready, 1)
            mm(ps[0:B, 7, 0:D], lhsT=C["row0"], rhs=u[:, 0, 0, :], start=True, stop=True).then_inc(khat_ps, 1)
            pe.wait_ge(khat_ready, 1)
            for c in range(1, B // 2):
                transform(c)

            def turn_x(c):
                pe.wait_ge(x_ready, 4 * c + 4 if c < B // 2 else TILES)
                if c:
                    pe.wait_ge(xt_sb, c)
                w = P if c < B // 2 else B
                for m in range(4 if c < B // 2 else 1):
                    j = TILE_ORDER[4 * c + m]
                    nc.tensor.transpose(ps[:, 4, m * P:m * P + w], xg[0:w, j, 0:P], ident[0:w, 0:w])
                    ins = nc.tensor.transpose(ps[0:D2, 5, m * P:m * P + w], xg[0:w, j, P:D], ident[0:w, 0:w])
                ins.then_inc(xt_ps, 1)

            def logits(c):
                pe.wait_ge(xt_sb, c + 1)
                w = P if c < B // 2 else B
                for m in range(4 if c < B // 2 else 1):
                    j = TILE_ORDER[4 * c + m]
                    mm(ps[0:w, 6, j * NE:(j + 1) * NE], lhsT=xt[:, 4 * c + m, 0, 0:w], rhs=wga[:, :], start=True, stop=False)
                    ins = mm(ps[0:w, 6, j * NE:(j + 1) * NE], lhsT=xt[0:D2, 4 * c + m, 1, 0:w], rhs=wgb[:, :],
                             start=False, stop=True)
                return ins

            for c in range(B // 2):
                pe.wait_ge(yhat_ready, c + 1)
                if c == 0:
                    pe.wait_ge(prod_ready, 3)
                if c >= 2:
                    pe.wait_ge(h2_ready, 2 * (c - 1))
                for lt in range(2):
                    for kt in range(KT):
                        ins = mm(ps[:, 2 * (c % 2) + lt, 0:2 * D], lhsT=inv[:, kt, lt * P:(lt + 1) * P],
                                 rhs=yhat[:, kt, 2 * c:2 * c + 2, :], start=kt == 0, stop=kt == KT - 1)
                    ins.then_inc(y_ps, 1)
                if c >= 2:
                    turn_x(c - 2)
                    logits(c - 2)
            sgn = C["sgn"].rearrange("p (b c) -> p b c", b=B)
            for b in range(B):
                for f in range(2):
                    ins = mm(ps[0:B, 7, 0:D], lhsT=sgn[:, b, :], rhs=yhat[:, 2 + f, b, :],
                             start=(b, f) == (0, 0), stop=(b, f) == (B - 1, 1))
            ins.then_inc(y_ps, 1)
            for c in range(B // 2 - 2, B // 2 + 1):
                turn_x(c)
                ins = logits(c)
            ins.then_inc(logit_ps, 1)
            pe.wait_ge(oh_ready, 1)
            mm(ps[:, 7, 0:(TILES + 1) * NE], lhsT=ltri16[:, :], rhs=ohb16[:, :, :].rearrange("p k e -> p (k e)"),
               start=True, stop=False)
            for j in range(TILES):
                n = TILES - j
                ins = mm(ps[:, 7, (j + 1) * NE:(TILES + 1) * NE], lhsT=ones16[:, :], rhs=bc(ohb16[:, j], 1, n),
                         start=False, stop=j == TILES - 1)
            ins.then_inc(rank_ps, 1)
            pe.wait_ge(pick_ready, 1)
            for k in range(2 * TILES):
                ins = mm(ps[:, 0, 0:2 * NBLK], lhsT=ohs[:, k, :], rhs=mvb[:, k].rearrange("p c s -> p (c s)"),
                         start=k == 0, stop=k == 2 * TILES - 1)
            ins.then_inc(slot_ps, 1)

            def turn_rows(q, r):
                pe.wait_ge(xs_in[r], 16 * (q + 1))
                for k in range(3):
                    ins = nc.tensor.transpose(x3_ps[:, k * P:(k + 1) * P], xs16[:, r, k * P:(k + 1) * P], ident16[:, :])
                ins.then_inc(bt_ps, 1)

            def up(i, e, par):
                pe.wait_ge(bt_sb, i + 1)
                for half in range(2):
                    for n, (x, w) in enumerate(((0, 0), (2, 0), (0, 1), (1, 2), (1, 3))):
                        ins = mm(ps[:, half, 0:H // 2], lhsT=x3[:, par, x * P:(x + 1) * P],
                                 rhs=fc16[:, bass.ds(e * H + (w * N_FC + half * (H // 2)), H // 2)],
                                 start=n == 0, stop=n == 4)
                ins.then_inc(fc_ps, 1)

            def down(i, e, par, first):
                pe.wait_ge(hh_ready, i + 1)
                if not first:
                    pe.wait_ge(o_ready, i - 1)
                for k in range(HT):
                    for w in range(2):
                        mm(ps[:, 5 + par, 0:D], lhsT=hh[:, par, k * P:(k + 1) * P],
                           rhs=pj16[:, bass.ds(e * HT * D + (w * N_PJ + k * D), D)], start=(k, w) == (0, 0), stop=False)
                pe.wait_ge(hl_ready, i + 1)
                for k in range(HT):
                    ins = mm(ps[:, 5 + par, 0:D], lhsT=hl[:, par, k * P:(k + 1) * P],
                             rhs=pj16[:, bass.ds(e * HT * D + k * D, D)], start=False, stop=k == HT - 1)
                ins.then_inc(pj_ps, 1)

            def turn_hidden(i, par):
                pe.wait_ge(hs_ready, i + 1)
                for k in range(HT):
                    ins = nc.tensor.transpose(ps[:, 2 + k // 3, (k % 3) * P:(k % 3 + 1) * P],
                                              hs[:, par, k * P:(k + 1) * P], ident)
                ins.then_inc(ht_ps, 1)

            def expert(i):
                return pe.value_load(blk_ei[0:1, bass.ds(i, 1)], min_val=0, max_val=NE - 1)

            def psteps(q, count, first=0, last=False):
                e_before, e = expert(4 * q), expert(4 * q + 1)
                for r in range(count):
                    i = 4 * q + r + 1
                    up(i, e, (r + 1) % 2)
                    e_next = expert(i + 1) if r + 1 < count else None
                    if not last or r + 1 < count:
                        turn_rows(q + (r + 2) // 4, (r + 2) % 4)
                    down(i - 1, e_before, r % 2, r < first)
                    turn_hidden(i, (r + 1) % 2)
                    e_before, e = e, e_next

            pe.wait_ge(expert_ready, 1)
            pe.wait_ge(idx_ready, 1)
            pe.wait_ge(low_vec, len(VEC_PIECES))
            pe.wait_ge(low_pool, len(POOL_PIECES))
            turn_rows(0, 0)
            up(0, expert(0), 0)
            turn_rows(0, 1)
            turn_hidden(0, 0)
            psteps(0, 4, first=2)
            with pe.Fori(1, NBLK // 4 - 1) as q:
                psteps(q, 4)
            psteps(NBLK // 4 - 1, 3, last=True)
            down(NBLK - 1, expert(NBLK - 1), 1, False)



def kernel(**inputs):
    import concourse.bacc as bacc
    from concourse.bass_utils import run_bass_kernel_spmd

    a = {k: np.asarray(v) for k, v in inputs.items()}
    x = a["x"]

    def patches(p):
        n = IMG // p
        return x.reshape(B, CH, n, p, n, p).transpose(2, 4, 0, 3, 5, 1).reshape(n * n, B * p * p * CH)

    arrays = {
        "px0": patches(1), "px1": patches(2), "px2": patches(4),
        "id0": a["L0_tok_idx0"].reshape(2, P, GP).transpose(1, 0, 2).reshape(P, 2 * GP),
        "id1": a["L0_tok_idx1"].reshape(64, 2, 8).transpose(1, 0, 2).reshape(P, 8),
        "id2": a["L0_tok_idx2"].reshape(16, 2, 8).transpose(2, 0, 1).reshape(P, 2),
        "w0": a["L0_tok_W0"].T,
        "w1": a["L0_tok_W1"].T.reshape(2, 96, EMB).transpose(1, 0, 2),
        "w2": a["L0_tok_W2"].T.reshape(GP, 48, EMB).transpose(1, 0, 2),
        "tb": np.stack([a["L0_tok_b0"], a["L0_tok_b1"], a["L0_tok_b2"]], 1),
        "wf": a["L0_tok_Wf"].T.reshape(3, EMB, D).transpose(1, 0, 2),
        "bf": a["L0_tok_bf"].reshape(1, D),
        "cls": a["cls_tok"].reshape(1, D),
        "a_real": a["L0_attn_A_real"].T, "a_imag": a["L0_attn_A_imag"].T,
        "b_mat": a["L0_attn_B_mat"].T, "c_mat": a["L0_attn_C_mat"].T,
        "log_delta": a["L0_attn_log_delta"],
        "w_gate": a["L0_ffn_w_gate"],
        "w_fc": a["L0_ffn_w_fc"].reshape(D, H, NE).transpose(0, 2, 1).reshape(D, NE * H),
        "w_proj": a["L0_ffn_w_proj"].reshape(HT, P, D, NE).transpose(1, 3, 0, 2).reshape(P, NE * HT * D),
        **shape_constants(),
    }
    arrays = {k: np.ascontiguousarray(v) for k, v in arrays.items()}
    nc = bacc.Bacc("TRN2", target_bir_lowering=False, num_devices=1)
    t = {k: nc.dram_tensor(k, v.shape, mybir.dt.from_np(v.dtype), kind="ExternalInput").ap() for k, v in arrays.items()}
    out = nc.dram_tensor("out", (B, L, D), F32, kind="ExternalOutput").ap()
    vit_layer(nc, t, out)
    r = run_bass_kernel_spmd(nc, [arrays], core_ids=[0])
    return r.results[0]["out"]
```

```python
import numpy as np
from contextlib import ExitStack

import concourse.bass as bass
from concourse import mybir

F32 = mybir.dt.float32
BF16 = mybir.dt.bfloat16
F16 = mybir.dt.float16
I32 = mybir.dt.int32
U32 = mybir.dt.uint32
ALU = mybir.AluOpType
ACT = mybir.ActivationFunctionType
AX = mybir.AxisListType

P = 128
B, CH, IMG = 8, 3, 64
D = 192
EMB = 64
GP = 16
NT = 256
L = NT + 1
D2 = D - P
NS = 64
TA, TB = 32, 8
CG = P // TA
NG = D // CG
XP = 8
F0 = 48
ROW0, ROW2 = 64, 64 + F0
assert ROW2 + 16 == P
NF = 256
NFFT = 2 * NF
KT = 4
H, NE = 768, 8
HT = H // P
TILES = 2 * B + 1
ROWS = B * L
NBLK = (2 * ROWS + NE * (P - 1)) // P
XW = D + NE
WC = 1024
N_FC, N_PJ = NE * H, NE * HT * D
FC_PIECES, PIECES = 2 * N_FC // WC, (2 * N_FC + N_PJ) // WC
STAT_PIECES = D * N_FC // P // WC
PIECE_BUFFER = [n if n < 5 else (0, 1, 5, 6, 7)[n % 5] for n in range(PIECES)]
VEC_PIECES = [0, 1, 2, 3, 4, 7, 8, 10, 11, 13, 14]
POOL_PIECES = [n for n in range(PIECES) if n not in VEC_PIECES]
assert N_FC % WC == 0 and N_PJ % WC == 0 and D * N_FC // P == N_PJ == STAT_PIECES * WC
EPS = 1e-5
MAGIC = 1.5 * 2.0 ** 23
TWO_PI = 6.2831845
LOWEST = -3.0e38
assert NBLK == 40 and NBLK % 8 == 0

_WIDTHS = [("ident", P), ("ltri", P), ("iota_s", P), ("iota_b", NBLK), ("off", 6), ("ids", 2 * TILES * 2),
           ("valid", TILES), ("ew", NE), ("eidx", NE), ("sgn", B * B), ("cmask", CG), ("row0", B), ("half0", B), ("ones", B)]
COL = {}
_at = 0
for _name, _w in _WIDTHS:
    COL[_name] = (_at, _at + _w)
    _at += _w
NCONST = _at


def shape_constants():
    c = np.zeros((P, NCONST), np.float32)

    def put(name, a):
        c[:, COL[name][0]:COL[name][1]] = a

    p = np.arange(P)
    put("ident", np.eye(P))
    put("ltri", p[:, None] < p[None, :])
    put("iota_s", p[None, :])
    put("iota_b", np.arange(NBLK)[None, :])
    low = (p < NS)[:, None]
    put("off", np.where(low, [[0.25, 0.25, 0.5, 0.25, 0.0, 0.25]], [[0.0, 0.5, 0.75, 0.25, 0.0, 0.0]]))
    rows = np.zeros((P, TILES), np.int64)
    valid = np.ones((P, TILES))
    for j in range(2 * B):
        rows[:, j] = (j % B) * L + P * (j // B) + p
    rows[:B, 2 * B] = p[:B] * L + NT
    valid[B:, 2 * B] = 0
    ids = np.stack([(rows + 1) % 256, (rows + 1) // 256], -1) * valid[:, :, None]
    put("ids", np.concatenate([ids, ids], 1).reshape(P, -1))
    put("valid", valid)
    put("ew", NE - np.arange(NE)[None, :])
    put("eidx", np.arange(NE)[None, :])
    sgn = np.zeros((P, B, B))
    for b in range(B):
        sgn[:, b, b] = -(2.0 / NFFT) * (-1.0) ** p
    put("sgn", sgn.reshape(P, -1))
    put("cmask", (p // TA)[:, None] == np.arange(CG)[None, :])
    put("row0", (p == 0)[:, None] * np.ones((1, B)))
    put("half0", (p < NS)[:, None] * np.ones((1, B)))
    put("ones", np.ones((1, B)))

    k = np.arange(NF)

    def angle(l):
        return np.pi * (((2 * k[None, :] + 1) * l[:, None]) % (2 * NFFT)) / NFFT

    def forward(l):
        return np.concatenate([np.cos(angle(l)), -np.sin(angle(l))], 1)

    fwd = forward(np.arange(NT)).reshape(2, P, NFFT).transpose(1, 0, 2)
    lk = TB * np.arange(TA)[:, None] + np.arange(TB)[None, :]
    fk = np.tile(forward(lk.reshape(-1)).reshape(TA, TB, NFFT), (CG, 1, 1))
    inv = (2.0 / NFFT) * forward(np.arange(NT)).T.reshape(KT, P, NT).transpose(1, 0, 2)
    interp = np.zeros((P, L))
    for at, n in ((0, 64), (ROW2, 16)):
        where = np.clip((np.arange(NT) + 0.5) * (n / NT) - 0.5, 0.0, n - 1)
        i0 = np.floor(where).astype(int)
        i1 = np.minimum(i0 + 1, n - 1)
        np.add.at(interp, (at + i0, 1 + np.arange(NT)), 1.0 - (where - i0))
        np.add.at(interp, (at + i1, 1 + np.arange(NT)), where - i0)
    f = lambda a: np.ascontiguousarray(a, np.float32)
    return {"consts": c, "fwd": f(fwd), "fwd_k": f(fk), "inv": f(inv), "interp": f(interp),
            "last_interp": f(interp[:, L - 1, None, None] * np.eye(B)[None])}


class Chain:

    def __init__(self, eng, s):
        self.eng, self.s, self.n = eng, s, 0

    def inc(self, ins):
        ins.then_inc(self.s, 1)
        self.n += 1

    def sync(self):
        self.eng.wait_ge(self.s, self.n)

    def link(self, ins):
        self.inc(ins)
        self.sync()


def bc(ap, axis, n):
    v = ap.unsqueeze(axis)
    shape = list(v.shape)
    shape[axis] = n
    return v.broadcast_to(shape)


def vit_layer(nc, t, out):
    with ExitStack() as ctx:
        def sb(name, shape, dt=F32):
            return ctx.enter_context(nc.sbuf_tensor(name, shape, dt))

        def sem(name):
            return ctx.enter_context(nc.semaphore(name))

        x_rows = nc.dram_tensor("x_rows", [ROWS, XW], F32, kind="Internal").ap()
        wmax_rows = nc.dram_tensor("wmax_rows", [P, 2], F32, kind="Internal").ap()
        out_rows = out.rearrange("b l d -> (b l) d")

        cst = sb("cst", [P, NCONST])
        C = {n: cst[:, a:b] for n, (a, b) in COL.items()}
        ident = C["ident"]
        fwd = sb("fwd_sb", [P, 2, NFFT])
        inv = sb("inv_sb", [P, KT, NT])
        id0 = sb("id0_sb", [P, 2 * GP], I32)
        id1 = sb("id1_sb", [P, 8], I32)
        id2 = sb("id2_sb", [P, 2], I32)
        w0 = sb("w0_sb", [EMB + 1, P - ROW0])
        w1 = sb("w1_sb", [96, 2, EMB])
        tb = sb("tb_sb", [EMB, 2])
        wf = sb("wf_sb", [EMB, 2, D])
        last_col = sb("last_col", [P, B, B])
        wga = sb("wga", [P, NE])
        wgb = sb("wgb", [D2, NE])
        khat = sb("khat", [P, KT, D])
        k0 = sb("k0", [B, 2, D])
        hroom = sb("hroom", [P, 2 * B * D])
        h_last = sb("h_last", [B, D])
        uroom = sb("uroom", [P, 2 * B * D])
        u_last = sb("u_last", [B, D])
        stats = sb("stats", [P, TILES, 6])
        mv = sb("mv", [P, TILES, 2])
        rstd = sb("rstd", [P, TILES])
        veps = sb("veps", [P, TILES])
        mhalf = sb("mhalf", [P, TILES])
        lg = sb("lg", [P, TILES, NE])
        oh1 = sb("oh1", [P, TILES, NE])
        oh2 = sb("oh2", [P, TILES, NE])
        rt = sb("rt", [P, 3, TILES, NE])
        rs = sb("rs", [P, 9, TILES])
        wmax = sb("wmax", [P, 2 * STAT_PIECES + 2])
        wsc = sb("wsc", [P, 16])
        stage = sb("stage", [P, 2, WC])
        ident16 = sb("ident16", [P, P], F16)
        ohb16 = sb("ohb16", [P, TILES + 1, NE], BF16)
        ltri16 = sb("ltri16", [P, P], BF16)
        ones16 = sb("ones16", [P, P], BF16)
        cnt = sb("cnt", [P, 6, NE])
        cnt_i = sb("cnt_i", [P, NE], I32)
        pos = sb("pos", [P, 2, TILES])
        pos_i = sb("pos_i", [P, 2, TILES], I32)
        blk_i = sb("blk_i", [P, 2, TILES], I32)
        slt_i = sb("slt_i", [P, 2, TILES], I32)
        blk_f = sb("blk_f", [P, 2 * TILES], BF16)
        slt_f = sb("slt_f", [P, 2 * TILES], BF16)
        blk_e = sb("blk_e", [P, NBLK])
        blk_ei = sb("blk_ei", [P, NBLK], I32)
        idx_f = sb("idx_f", [P, NBLK])
        idx = sb("idx", [P, NBLK], I32)
        gcol = sb("gcol", [P, 4], I32)
        scol = sb("scol", [P, 4], I32)
        slotv = sb("slotv", [P, 2 * NBLK])
        gsel = sb("gsel", [P, 2, NE])
        gate = sb("gate", [P, 2])
        pick_consts = stats[:, :, :].rearrange("p k n -> p (k n)").bitcast(BF16)
        iota16, ids16 = pick_consts[:, 0:P], pick_consts[:, P:P + 4 * TILES]
        wsc_i = wsc[:, :].bitcast(I32)
        w_scale, fc_back, h_scale, out_back = wsc[:, 9:11], wsc[:, 11:12], wsc[:, 12:13], wsc[:, 13:14]

        def view(base, at, shape):
            n = int(np.prod(shape[1:]))
            v = base[0:shape[0], at:at + n]
            names = "abcd"[:len(shape) - 1]
            if len(names) > 1:
                v = v.rearrange(f"p ({' '.join(names)}) -> p {' '.join(names)}",
                                **{c: s for c, s in zip(names[1:], shape[2:])})
            return v, at + n

        u, _ = view(uroom, 0, [P, 2, B, D])
        h, _ = view(hroom, 0, [P, 2, B, D])
        byb1, at = view(hroom, B * D, [P, B, 8, 12])
        byb0, at = view(hroom, at, [P, 2, B, GP * CH])
        assert at <= 2 * B * D
        w2, _ = view(uroom, 0, [48, GP, EMB])
        wroom = sb("wroom", [P, 2 * N_FC + N_PJ])
        fc16 = wroom[:, 0:2 * N_FC].bitcast(F16)
        pj16 = wroom[:, 2 * N_FC:].bitcast(F16)
        ytab, at = view(wroom, 0, [P, 2, D, TB])
        ye, at = view(wroom, at, [P, D, TB])
        kmask, at = view(wroom, at, [P, D, TB])
        assert at <= N_FC
        fwd_k, at = view(wroom, N_FC, [P, TB, NFFT])
        t2, at = view(wroom, at, [48, 2, B, P])
        assert at <= 2 * N_FC
        xtab, at = view(wroom, 2 * N_FC, [P, D, TA])
        xe, at = view(wroom, at, [P, 2, D, XP])
        assert at <= 2 * N_FC + NE * HT * D

        SROOM = 15936
        sroom = sb("sroom", [P, SROOM])
        sm, at = view(sroom, 0, [P, 14, D])
        ssm, at = view(sroom, at, [P, 5, D])
        trig1, at = view(sroom, at, [P, 3, D])
        scr, at = view(sroom, at, [P, D, XP])
        raw2, at = view(sroom, at, [P, 2, B * 48])
        raw1, at = view(sroom, at, [P, 8, B * 12])
        raw0, at = view(sroom, at, [P, 2, GP * B * 3])
        stat3, _ = view(sroom, at, [P, WC])
        t1, at = view(sroom, at, [96, B, P])
        y1t, at = view(sroom, at, [EMB, B, 64])
        y2t, at = view(sroom, at, [EMB, B, P - ROW0])
        zt, at = view(sroom, at, [P, B, D])
        tok, at = view(sroom, at, [P, B, L])
        wf0, at = view(sroom, at, [EMB + 1, D])
        z_shared, at = view(sroom, at, [P, D])
        cls_row, at = view(sroom, at, [1, D])
        assert at <= SROOM, at
        yhat, at = view(sroom, 0, [P, KT, B, D])
        prod_at = at
        prod, at = view(sroom, at, [P, 2, KT, 4 * D])
        xg_flat = sroom[:, at:at + 3 * WC]
        assert 3 * WC <= TILES * D
        stage_flat = stage[:, :, :].rearrange("p k n -> p (k n)")
        xg, at = view(sroom, at, [P, TILES, D])
        k0u, at = view(sroom, at, [B, 2, D])
        assert at <= SROOM, at
        xr_f, at = view(sroom, prod_at, [P, TILES * XW])
        xr = xr_f.rearrange("p (k w) -> p k w", w=XW)
        xr16 = xr_f.bitcast(F16).rearrange("p (k w) -> p k w", w=2 * XW)
        assert at <= prod_at + 2 * KT * 4 * D
        ohs_f, at = view(sroom, 0, [P, TILES * P])
        ohs = ohs_f.bitcast(BF16).rearrange("p (k s) -> p k s", s=P)
        ohb_f, at = view(sroom, at, [P, TILES * NBLK])
        ohb = ohb_f.bitcast(BF16).rearrange("p (k s) -> p k s", s=NBLK)
        mvb_f, at = view(sroom, at, [P, 2 * TILES * NBLK])
        mvb = mvb_f.bitcast(BF16).rearrange("p (k c s) -> p k c s", c=2, s=NBLK)
        picks_end = at
        xt, at = view(sroom, 0, [P, TILES, 2, P])
        assert 4 * 2 * P <= 6 * D and 8 * 2 * P <= 2 * B * D
        assert at <= prod_at
        gsel_e, at = view(sroom, picks_end, [P, NBLK, NE])
        ge_t, at = view(sroom, at, [P, NBLK, NE])
        xs_f, at = view(sroom, at, [P, 4 * XW])
        xs = xs_f.rearrange("p (k w) -> p k w", w=XW)
        xs16 = xs_f.bitcast(F16).rearrange("p (k w) -> p k w", w=2 * XW)
        assert at <= prod_at
        hs, at = view(sroom, 0, [P, 2, H])
        x3_f, at = view(sroom, at, [P, 3 * P])
        x3 = x3_f.bitcast(F16).rearrange("p (k w) -> p k w", k=2)
        hh_f, at = view(sroom, at, [P, H])
        hh = hh_f.bitcast(F16).rearrange("p (k w) -> p k w", k=2)
        hl_f, at = view(sroom, at, [P, H])
        hl = hl_f.bitcast(F16).rearrange("p (k w) -> p k w", k=2)
        o_sb, at = view(sroom, at, [P, 2, D])
        assert at <= picks_end

        def stat_buffer(n):
            return stat3 if n % 3 == 2 else stage[:, n % 3, :]

        def piece_buffer(n):
            k = PIECE_BUFFER[n]
            room, at = (stage_flat, 0) if k < 2 else (xg_flat, 2) if k < 5 else (uroom, 5)
            return room[:, (k - at) * WC:(k - at + 1) * WC]

        def piece_parts(n):
            if n < FC_PIECES:
                at = (n // (FC_PIECES // 2)) * 2 * N_FC + (n % (FC_PIECES // 2)) * WC
                return fc16[:, at:at + WC], fc16[:, at + N_FC:at + N_FC + WC], w_scale[:, 0:1]
            at = (n - FC_PIECES) * WC
            return pj16[:, at:at + WC], pj16[:, at + N_PJ:at + N_PJ + WC], w_scale[:, 1:2]

        def piece_loads(n):
            return 16 * sum(2 if FC_PIECES // 2 <= m < FC_PIECES else 1
                            for m in range(n + 1) if PIECE_BUFFER[m] == PIECE_BUFFER[n])

        def x_tiles(c):
            if c == B // 2:
                return xg[0:B, 2 * B, :], xr16[0:B, 2 * B, :]
            return tuple(a[:, 0:2 * B, :].rearrange("p (l b) w -> p l b w", l=2)[:, :, 2 * c:2 * c + 2, :] for a in (xg, xr16))

        wmax_all = rt[:, :, :, :].rearrange("p a k e -> p (a k e)")[:, 0:2 * P]
        delta, rate, turn = sm[:, 9], sm[:, 10], sm[:, 11]
        T0_BANK = 4, 0
        TOKEN_LOADS = 10
        TILE_ORDER = [8 * lt + b for c in range(B // 2) for lt in range(2) for b in (2 * c, 2 * c + 1)] + [2 * B]
        ps = ctx.enter_context(nc.psum_tensor("ps", [P, 8, 512], F32))
        pf = ps[:, :, :].rearrange("p k n -> p (k n)")
        x3_ps = ps[:, 4, 0:3 * P // 2].bitcast(F16)

        idx_in, ssm_in, const_in, tokw_in = sem("idx_in"), sem("ssm_in"), sem("const_in"), sem("tokw_in")
        four_in, wmax_taken, wmax_ready = sem("four_in"), sem("wmax_taken"), sem("wmax_ready")
        stat_in = [sem(f"stat_in{i}") for i in range(3)]
        piece_in = [sem(f"piece_in{i}") for i in range(8)]
        wmax_out, wmax_in, scale_ready = sem("wmax_out"), sem("wmax_in"), sem("scale_ready")
        piece_scaled, piece_high, low_vec, low_pool = sem("piece_scaled"), sem("piece_high"), sem("low_vec"), sem("low_pool")
        xhigh_ready, xlow_ready = sem("xhigh_ready"), sem("xlow_ready")
        raw2_in, raw1_in = sem("raw2_in"), sem("raw1_in")
        byb1_ready, byb0_ready = sem("byb1_ready"), sem("byb0_ready")
        raw0_in = [sem("raw0a_in"), sem("raw0b_in")]
        vec_own = sem("vec_own")
        edge_zero = sem("edge_zero")
        abs_ready, e_ready, w_ready, ln_ready = sem("abs_ready"), sem("e_ready"), sem("w_ready"), sem("ln_ready")
        rate_ready = sem("rate_ready")
        env1_ready, frac1_ready, sin1_ready = sem("env1_ready"), sem("frac1_ready"), sem("sin1_ready")
        yenv_ready, yfrac_ready, ysin_ready, ytab_ready = (sem("yenv_ready"), sem("yfrac_ready"), sem("ysin_ready"),
                                                           sem("ytab_ready"))
        xenv_ready, xfrac_ready, xsin_ready, xtab_ready = (sem("xenv_ready"), sem("xfrac_ready"), sem("xsin_ready"),
                                                           sem("xtab_ready"))
        kps_ready, ksb_ready, khat_ps, khat_ready = (sem("kps_ready"), sem("ksb_ready"), sem("khat_ps"),
                                                     sem("khat_ready"))
        zs_ps, zs_sb, last_ready, h_copied = sem("zs_ps"), sem("zs_sb"), sem("last_ready"), sem("h_copied")
        t2_ps, t2_sb, t1_ps, t1_sb = sem("t2_ps"), sem("t2_sb"), sem("t1_ps"), sem("t1_sb")
        y2_ps, y2_sb, y1_ps, y1_sb = sem("y2_ps"), sem("y2_sb"), sem("y1_ps"), sem("y1_sb")
        z_ps, z_sb = sem("z_ps"), sem("z_sb")
        t0_ps, t0_sb = sem("t0_ps"), sem("t0_sb")
        h_ps, h_sb, u_ready = sem("h_ps"), sem("h_sb"), sem("u_ready")
        uhat_ps, prod_ready, yhat_ready = sem("uhat_ps"), sem("prod_ready"), sem("yhat_ready")
        y_ps, h2_ready, x_ready = sem("y_ps"), sem("h2_ready"), sem("x_ready")
        ylast_ps, h2last_ready, xlast_ready = sem("ylast_ps"), sem("h2last_ready"), sem("xlast_ready")
        xt_ps, xt_sb, logit_ps = sem("xt_ps"), sem("xt_sb"), sem("logit_ps")
        gap_ready, gexp_ready, gates_ready = sem("gap_ready"), sem("gexp_ready"), sem("gates_ready")
        oh_ready, rank_ps, pick_ready, slot_ps = (sem("oh_ready"), sem("rank_ps"),
                                                              sem("pick_ready"), sem("slot_ps"))
        expert_ready, idx_ready = sem("expert_ready"), sem("idx_ready")
        base_out, x_out = sem("base_out"), sem("x_out")
        added, xs_clear = sem("added"), sem("xs_clear")
        xs_in = [sem(f"xs_in{i}") for i in range(4)]
        bt_ps, bt_sb, fc_ps = sem("bt_ps"), sem("bt_sb"), sem("fc_ps")
        ht_ps = sem("ht_ps")
        hs_ready, hh_ready, hl_ready = sem("hs_ready"), sem("hh_ready"), sem("hl_ready")
        pj_ps, o_ready = sem("pj_ps"), sem("o_ready")
        gate_seen = sem("gate_seen")

        veps_ready, rstd_ready = sem("veps_ready"), sem("rstd_ready")
        PAIR_ROOTS, LAST_ROOT = [(P, ((2 * c, 2 * c + 2), (8 + 2 * c, 10 + 2 * c))) for c in range(B // 2)], (B, ((16, 17),))
        ROOTS = PAIR_ROOTS + [LAST_ROOT] + PAIR_ROOTS[:3] + [LAST_ROOT] + PAIR_ROOTS[3:]

        block = ctx.enter_context(nc.Block())

        @block.sync
        def _(sp):
            sp.dma_start(id2[:, :], t["id2"]).then_inc(idx_in, 16)
            sp.dma_start(id1[:, :], t["id1"]).then_inc(idx_in, 16)
            sp.dma_start(id0[:, :], t["id0"]).then_inc(idx_in, 16)
            for n, name in enumerate(("a_real", "a_imag", "b_mat", "c_mat")):
                for half in range(2):
                    sp.dma_start(ssm[NS * half:NS * half + NS, n, :], t[name]).then_inc(ssm_in, 16)
            sp.dma_start(w2[:, :, :], t["w2"]).then_inc(tokw_in, 16)
            sp.dma_start(w1[:, :, :], t["w1"]).then_inc(tokw_in, 16)
            sp.dma_start(w0[:, :], t["w0"]).then_inc(tokw_in, 16)
            sp.dma_start(wf0[:, :], t["wf0"]).then_inc(tokw_in, 16)
            sp.dma_start(cls_row[:, :], t["cls"]).then_inc(tokw_in, 16)
            sp.dma_start(tb[:, :], t["tb"]).then_inc(tokw_in, 16)
            sp.dma_start(wf[:, :, :], t["wf"]).then_inc(tokw_in, 16)
            for rows in (slice(0, ROW0), slice(ROW2, P)):
                sp.dma_start(tok[rows], t["interp"][rows].unsqueeze(1).broadcast_to([rows.stop - rows.start, B, L])).then_inc(
                    tokw_in, 16)
            sp.dma_start(last_col[:, :, :], t["last_interp"]).then_inc(tokw_in, 16)
            sp.dma_start(fwd_k[:, :, :], t["fwd_k"]).then_inc(four_in, 16)
            sp.dma_start(fwd[:, :, :], t["fwd"]).then_inc(four_in, 16)
            sp.dma_start(inv[:, :, :], t["inv"]).then_inc(four_in, 16)
            sp.dma_start(wga[:, :], t["w_gate"][0:P, :]).then_inc(four_in, 16)
            sp.dma_start(wgb[:, :], t["w_gate"][P:D, :]).then_inc(four_in, 16)
            for n in range(2 * STAT_PIECES):
                if n == 2:
                    sp.wait_ge(y1_ps, 1)
                if n >= 3:
                    sp.wait_ge(wmax_taken, n - 2)
                w = t["w_fc"] if n < STAT_PIECES else t["w_proj"]
                flat = w.rearrange("a b -> (a b)").rearrange("(p n) -> p n", p=P)
                at = (n % STAT_PIECES) * WC
                sp.dma_start(stat_buffer(n), flat[:, at:at + WC]).then_inc(stat_in[n % 3], 16)
            sp.wait_ge(wmax_ready, 1)
            sp.dma_start(wmax_rows, wmax[:, 2 * STAT_PIECES:]).then_inc(wmax_out, 16)
            sp.wait_ge(wmax_out, 16)
            sp.dma_start(wmax_all, wmax_rows.rearrange("p w -> (p w)").partition_broadcast(P)).then_inc(wmax_in, 16)
            sp.wait_ge(wmax_taken, 2 * STAT_PIECES)
            sp.wait_ge(khat_ps, 1)
            for n in range(PIECES):
                if n == 7:
                    sp.wait_ge(uhat_ps, B // 2)
                before = [m for m in range(n) if PIECE_BUFFER[m] == PIECE_BUFFER[n]]
                if before:
                    m = before[-1]
                    if m in VEC_PIECES:
                        sp.wait_ge(low_vec, VEC_PIECES.index(m) + 1)
                    else:
                        sp.wait_ge(low_pool, POOL_PIECES.index(m) + 1)
                at = (n % (FC_PIECES // 2)) * WC
                if n < FC_PIECES // 2:
                    sp.dma_start(piece_buffer(n), t["w_fc"][0:P, at:at + WC]).then_inc(piece_in[PIECE_BUFFER[n]], 16)
                elif n < FC_PIECES:
                    for k in range(2):
                        sp.dma_start(piece_buffer(n)[D2 * k:D2 * k + D2], t["w_fc"][P:D, at:at + WC]).then_inc(
                            piece_in[PIECE_BUFFER[n]], 16)
                else:
                    at = (n - FC_PIECES) * WC
                    sp.dma_start(piece_buffer(n), t["w_proj"][:, at:at + WC]).then_inc(piece_in[PIECE_BUFFER[n]], 16)
            sp.wait_ge(h2_ready, B)
            sp.wait_ge(h2last_ready, 1)
            for lt in range(2):
                sp.dma_start(out[:, P * lt:P * lt + P, :].rearrange("b l d -> l b d"), h[:, lt]).then_inc(base_out, 16)
            sp.dma_start(out[:, NT, :], h_last[:, :]).then_inc(base_out, 16)
            rows = x_rows.rearrange("(b l) w -> l b w", b=B)
            sp.wait_ge(gates_ready, 1)
            sp.wait_ge(xlow_ready, B // 2 + 1)
            for lt in range(2):
                sp.dma_start(rows[P * lt:P * lt + P], xr[:, B * lt:B * lt + B, :]).then_inc(x_out, 16)
            sp.dma_start(rows[NT], xr[0:B, 2 * B, :]).then_inc(x_out, 16)
            sp.wait_ge(base_out, 48)
            sp.wait_ge(x_out, 48)

        @block.gpsimd
        def _(pool):
            nc.gpsimd.memset(y2t[:, :, :], 0.0).then_inc(edge_zero, 1)
            nc.gpsimd.memset(mhalf[:, :], -0.5).then_inc(edge_zero, 1)
            pool.wait_ge(idx_in, 48)
            for q in range(2):
                nc.gpsimd.indirect_dma_start(raw2[:, q, :], None, t["px2"], bass.IndirectOffsetOnAxis(
                    ap=id2[:, q:q + 1].bitcast(U32), axis=0)).then_inc(raw2_in, 16)
            for g in range(8):
                nc.gpsimd.indirect_dma_start(raw1[:, g, :], None, t["px1"], bass.IndirectOffsetOnAxis(
                    ap=id1[:, g:g + 1].bitcast(U32), axis=0)).then_inc(raw1_in, 16)
            for half in range(2):
                for g in range(GP):
                    nc.gpsimd.indirect_dma_start(
                        raw0[:, half, g * B * 3:(g + 1) * B * 3], None, t["px0"], bass.IndirectOffsetOnAxis(
                            ap=id0[:, half * GP + g:half * GP + g + 1].bitcast(U32), axis=0)).then_inc(raw0_in[half], 16)
            pool.wait_ge(xenv_ready, 1)
            for k in range(2):
                pool.wait_ge(xsin_ready, k + 1)
                part = xtab[:, :, k * XP:(k + 1) * XP]
                nc.gpsimd.tensor_tensor(part, part, xe[:, k], ALU.mult).then_inc(xtab_ready, 1)

            def root(n):
                np_, tiles = ROOTS[n]
                pool.wait_ge(veps_ready, n + 1)
                for j0, j1 in tiles:
                    ins = nc.gpsimd.tensor_tensor(rstd[0:np_, j0:j1], veps[0:np_, j0:j1], mhalf[0:np_, j0:j1], ALU.pow)
                ins.then_inc(rstd_ready, 1)

            pool.wait_ge(edge_zero, 3)
            for n in range(5):
                root(n)
            for c in range(B // 2):
                pool.wait_ge(prod_ready, c + 1)
                pr = prod[:, c % 2].rearrange("p k (f n) -> p k f n", f=2)
                for part, op in ((0, ALU.subtract), (1, ALU.add)):
                    dst = yhat[:, 2 * part:2 * part + 2, 2 * c:2 * c + 2, :].rearrange("p f b d -> p f (b d)")
                    last = nc.gpsimd.tensor_tensor(dst, pr[:, 2 * part], pr[:, 2 * part + 1], op)
                last.then_inc(yhat_ready, 1)

            def x_low(c):
                pool.wait_ge(xhigh_ready, c + 1)
                whole, parts = x_tiles(c)
                nc.gpsimd.tensor_tensor(parts[..., D:D + D2], whole[..., P:D], parts[..., P:D], ALU.subtract)
                nc.gpsimd.tensor_tensor(parts[..., D + D2:D + D2 + P], whole[..., 0:P], parts[..., 0:P],
                                        ALU.subtract).then_inc(xlow_ready, 1)

            def low_parts(*pieces):
                for n in pieces:
                    assert n in POOL_PIECES
                    pool.wait_ge(piece_high, n + 1)
                    high, low, _ = piece_parts(n)
                    nc.gpsimd.tensor_tensor(low, piece_buffer(n), high, ALU.subtract).then_inc(low_pool, 1)

            root(5)
            low_parts(*POOL_PIECES[0:2])
            root(6)
            x_low(0)
            low_parts(POOL_PIECES[2])
            root(7)
            x_low(1)
            root(8)
            low_parts(POOL_PIECES[3])
            root(9)
            for c in (2, 3, 4):
                x_low(c)
            low_parts(*POOL_PIECES[4:])

            def gather(q, r):
                nc.gpsimd.indirect_dma_start(xs[:, r, :], None, x_rows, bass.IndirectOffsetOnAxis(
                    ap=gcol[:, r:r + 1].bitcast(U32), axis=0), bounds_check=ROWS - 1,
                    oob_is_err=False).then_inc(xs_in[r], 16)

            def step(q, r, more=True, first=False):
                i = 4 * q + r + 1
                if not isinstance(i, int):
                    i, blocks_out, rows_added = pool.to_reg(i), pool.to_reg(i + 1), pool.to_reg(16 * i)
                else:
                    blocks_out, rows_added = i + 1, 16 * i
                if more:
                    pool.wait_ge(idx_ready, 1)
                    pool.wait_ge(o_ready, i)
                    gather(q + 1, r)
                pool.wait_ge(idx_ready, 1)
                pool.wait_ge(o_ready, blocks_out)
                pool.wait_ge(added, rows_added)
                scatter((r + 1) % 4, (r + 1) % 2)

            def scatter(r, par):
                nc.gpsimd.indirect_dma_start(out_rows, bass.IndirectOffsetOnAxis(
                    ap=scol[:, r:r + 1].bitcast(U32), axis=0), o_sb[:, par, :], None, bounds_check=ROWS - 1,
                    oob_is_err=False, compute_op=ALU.add).then_inc(added, 16)

            pool.wait_ge(idx_ready, 1)
            pool.wait_ge(xs_clear, 1)
            pool.wait_ge(x_out, 48)
            for r in range(4):
                gather(0, r)
            pool.wait_ge(base_out, 48)
            pool.wait_ge(o_ready, 1)
            scatter(0, 0)
            with pool.Fori(0, NBLK // 4 - 1) as q:
                for r in range(4):
                    step(q, r)
            for r in range(3):
                step(NBLK // 4 - 1, r, more=False)
            pool.wait_ge(added, 16 * NBLK)

        @block.scalar
        def _(act):
            act.dma_start(ssm[:, 4, :], t["log_delta"].partition_broadcast(P)).then_inc(ssm_in, 16)
            act.dma_start(cst[:, :], t["consts"]).then_inc(const_in, 16)

            act.wait_ge(abs_ready, 1)
            nc.scalar.activation(sm[:, 1], sm[:, 0], ACT.Exp, scale=-1.0).then_inc(e_ready, 1)
            act.wait_ge(w_ready, 1)
            nc.scalar.activation(sm[:, 3], sm[:, 2], ACT.Ln).then_inc(ln_ready, 1)
            act.wait_ge(rate_ready, 1)
            nc.scalar.activation(sm[:, 8], rate, ACT.Exp)
            nc.scalar.activation(sm[:, 12], rate, ACT.Exp, scale=float(NT)).then_inc(env1_ready, 1)
            for b in range(TB):
                ins = nc.scalar.activation(ye[:, :, b], rate, ACT.Exp, scale=float(b))
            ins.then_inc(yenv_ready, 1)
            for a in range(TA):
                ins = nc.scalar.activation(xtab[:, :, a], rate, ACT.Exp, scale=float(TB * a))
            ins.then_inc(xenv_ready, 1)

            def xsines(k):
                act.wait_ge(xfrac_ready, k + 1)
                nc.scalar.activation(xe[:, k % 2], xe[:, k % 2], ACT.Sin, scale=TWO_PI).then_inc(xsin_ready, 1)

            def level12_patches():
                act.wait_ge(raw1_in, 16 * 8)
                nc.scalar.activation(byb1, raw1.rearrange("p g (b c) -> p b g c", b=B),
                                     ACT.Copy).then_inc(byb1_ready, 1)
                act.wait_ge(t1_ps, 1)
                nc.scalar.activation(t1.rearrange("p b s -> p (b s)"), pf[0:96, 2048:3072], ACT.Copy).then_inc(t1_sb, 1)

            def level12():
                act.wait_ge(tokw_in, 16 * TOKEN_LOADS)
                act.wait_ge(y2_ps, 1)
                act.wait_ge(edge_zero, 3)
                nc.scalar.activation(y2t[:, :, F0:], ps[0:EMB, 7, 0:B * 16].rearrange("p (b s) -> p b s", b=B),
                                     ACT.Identity, bias=tb[:, 1:2]).then_inc(y2_sb, 1)
                act.wait_ge(y1_ps, 1)
                nc.scalar.activation(y1t.rearrange("p b s -> p (b s)"), ps[0:EMB, 6, 0:512],
                                     ACT.Identity, bias=tb[:, 0:1]).then_inc(y1_sb, 1)

            def level12_fused():
                act.wait_ge(z_ps, 1)
                nc.scalar.activation(zt[0:ROW0].rearrange("p (g b) d -> p g (b d)", b=2), ps[0:ROW0, 0:4, 0:2 * D],
                                     ACT.Copy).then_inc(z_sb, 1)

            def by_image(half):
                act.wait_ge(raw0_in[half], 16 * GP)
                nc.scalar.activation(byb0[:, half].rearrange("p b (g c) -> p b g c", g=GP),
                                     raw0[:, half].rearrange("p (g b c) -> p b g c", g=GP, b=B),
                                     ACT.Copy).then_inc(byb0_ready, 1)

            def turned(half):
                act.wait_ge(t0_ps, half + 1)
                nc.scalar.activation(tok[ROW0:ROW2, :, 1 + P * half:1 + P * half + P],
                                     pf[ROW0:ROW2, T0_BANK[half] * 512:T0_BANK[half] * 512 + 1024].rearrange(
                                         "p (b s) -> p b s", b=B), ACT.Copy).then_inc(t0_sb, 1)

            def fused(half):
                for c in range(4):
                    act.wait_ge(h_ps, 4 * half + c + 1)
                    ins = nc.scalar.activation(h[:, half, 2 * c:2 * c + 2, :].rearrange("p b d -> p (b d)"),
                                               ps[:, 4 - 4 * half + c, 0:2 * D], ACT.Copy)
                    ins.then_inc(h_sb if half else h_copied, 1)
                if half == 0:
                    act.wait_ge(h_copied, B // 2)
                    nc.scalar.activation(h[0:1, 0], bc(cls_row[:, :], 1, B), ACT.Copy).then_inc(h_sb, 4)

            level12_patches()
            act.wait_ge(frac1_ready, 1)
            nc.scalar.activation(trig1[:, :], trig1[:, :], ACT.Sin, scale=TWO_PI).then_inc(sin1_ready, 1)
            for k in range(2):
                act.wait_ge(yfrac_ready, k + 1)
                nc.scalar.activation(ytab[:, k], ytab[:, k], ACT.Sin, scale=TWO_PI).then_inc(ysin_ready, 1)
            by_image(0)
            level12()
            turned(0)
            xsines(0)
            by_image(1)
            level12_fused()
            turned(1)
            act.wait_ge(t0_sb, 2)
            nc.scalar.activation(last_col[ROW0:ROW2, :, :].rearrange("p b c -> p (b c)")[:, 0:B * B:B + 1],
                                 tok[ROW0:ROW2, :, NT], ACT.Copy).then_inc(last_ready, 1)
            xsines(1)
            fused(0)
            xsines(2)
            fused(1)
            xsines(3)
            act.wait_ge(h_ps, B + 1)
            nc.scalar.activation(h_last[:, :], ps[0:B, 0, 0:D], ACT.Copy).then_inc(h_sb, 1)
            act.wait_ge(khat_ps, 1)
            nc.scalar.activation(khat[:, :, :].rearrange("p (x y) d -> p x (y d)", x=2), ps[:, 4:6, 0:2 * D], ACT.Copy)
            nc.scalar.activation(k0[:, :, :].rearrange("p k d -> p (k d)"), ps[0:B, 6, 0:2 * D],
                                 ACT.Copy)
            nc.scalar.activation(k0u[:, 1], ps[0:B, 7, 0:D], ACT.Copy).then_inc(khat_ready, 1)

            def high_parts(*pieces):
                for n in pieces:
                    act.wait_ge(piece_in[PIECE_BUFFER[n]], piece_loads(n))
                    high, _, scale = piece_parts(n)
                    if n in POOL_PIECES:
                        nc.scalar.activation(piece_buffer(n), piece_buffer(n), ACT.Copy, scale=scale).then_inc(
                            piece_scaled, 1)
                        act.wait_ge(piece_scaled, POOL_PIECES.index(n) + 1)
                        scale = 1.0
                    nc.scalar.activation(high, piece_buffer(n), ACT.Copy, scale=scale).then_inc(piece_high, 1)

            act.wait_ge(scale_ready, 1)
            high_parts(*range(9))
            act.wait_ge(yhat_ready, B // 2)
            for c, (before, after) in enumerate((((9,), (10, 11, 12)), ((), (13,)), ((), (14,)), ((), ()), ((), (15,)))):
                if c < B // 2:
                    act.wait_ge(x_ready, 4 * c + 4)
                else:
                    act.wait_ge(xlast_ready, 1)
                whole, parts = x_tiles(c)
                nc.scalar.activation(parts[..., 0:D], whole, ACT.Copy).then_inc(xhigh_ready, 1)
                high_parts(*before)
                act.wait_ge(xt_ps, c + 1)
                for k, bank, rows in ((0, 4, P), (1, 5, D2)):
                    if c < B // 2:
                        ins = nc.scalar.activation(xt[0:rows, 4 * c:4 * c + 4, k, :],
                                                   ps[0:rows, bank, :].rearrange("p (k s) -> p k s", k=4), ACT.Copy)
                    else:
                        ins = nc.scalar.activation(xt[0:rows, 2 * B, k, 0:B], ps[0:rows, bank, 0:B], ACT.Copy)
                ins.then_inc(xt_sb, 1)
                high_parts(*after)
            act.wait_ge(gap_ready, 1)
            nc.scalar.activation(rs[:, 5], rs[:, 4], ACT.Exp).then_inc(gexp_ready, 1)

            high_parts(16, 17, 18, 19, 20)

            def gelu(i, par):
                act.wait_ge(fc_ps, i + 1)
                nc.scalar.activation(hs[:, par].rearrange("p (k n) -> p k n", k=2), ps[:, 0:2, 0:H // 2],
                                     ACT.Gelu_apprx_tanh, scale=fc_back).then_inc(hs_ready, 1)
                act.wait_ge(ht_ps, i + 1)
                nc.scalar.activation(hh[:, par].rearrange("p (k n) -> p k n", k=2), ps[:, 2:4, 0:H // 2], ACT.Copy, scale=h_scale).then_inc(hh_ready, 1)

            with act.Fori(0, NBLK // 8) as q:
                for k in range(8):
                    gelu(8 * q + k, k % 2)

        @block.vector
        def _(dve):
            own = Chain(dve, vec_own)
            v = nc.vector
            AR, AI, BM, CM, LD = (ssm[:, n] for n in range(5))

            v.memset(tok[ROW0:ROW2, :, 0:1], 0.0).then_inc(edge_zero, 1)
            dve.wait_ge(const_in, 16)
            dve.wait_ge(ssm_in, 16 * 9)
            v.scalar_tensor_tensor(out=sm[:, 0], in0=LD, scalar=-1.0, in1=LD, op0=ALU.mult,
                                   op1=ALU.max).then_inc(abs_ready, 1)
            dve.wait_ge(e_ready, 1)
            v.tensor_scalar(sm[:, 2], sm[:, 1], 1.0, None, ALU.add).then_inc(w_ready, 1)
            dve.wait_ge(w_ready, 1)
            own.inc(v.scalar_tensor_tensor(out=sm[:, 4], in0=sm[:, 2], scalar=-1.0, in1=sm[:, 1], op0=ALU.add,
                                           op1=ALU.subtract))
            own.link(v.reciprocal(sm[:, 5], sm[:, 2]))
            own.link(v.tensor_tensor(sm[:, 4], sm[:, 4], sm[:, 5], ALU.mult))
            dve.wait_ge(ln_ready, 1)
            own.link(v.scalar_tensor_tensor(out=sm[:, 5], in0=LD, scalar=0.0, in1=sm[:, 3], op0=ALU.max, op1=ALU.add))
            own.link(v.tensor_tensor(delta, sm[:, 5], sm[:, 4], ALU.subtract))
            v.tensor_tensor(rate, AR, delta, ALU.mult)
            v.scalar_tensor_tensor(out=turn, in0=AI, scalar=1.0 / (2.0 * np.pi), in1=delta, op0=ALU.mult,
                                   op1=ALU.mult).then_inc(rate_ready, 1)
            dve.wait_ge(rate_ready, 1)
            own.inc(v.tensor_tensor(sm[:, 0], AR, AR, ALU.mult))
            own.link(v.tensor_tensor(sm[:, 1], AI, AI, ALU.mult))
            own.link(v.tensor_tensor(sm[:, 0], sm[:, 0], sm[:, 1], ALU.add))
            own.link(v.reciprocal(sm[:, 1], sm[:, 0]))
            own.link(v.tensor_tensor(sm[:, 2], BM, CM, ALU.mult))
            own.link(v.tensor_tensor(sm[:, 0], sm[:, 1], sm[:, 2], ALU.mult))

            def fraction(dst, tmp, done, n):
                own.link(v.tensor_scalar(tmp, dst, MAGIC, -MAGIC, ALU.add, ALU.add))
                v.tensor_tensor(dst, dst, tmp, ALU.subtract).then_inc(done, 1)
                dve.wait_ge(done, n)

            taken = [0]

            def weight_max(count):
                for n in range(taken[0], taken[0] + count):
                    dve.wait_ge(stat_in[n % 3], 16 * (n // 3 + 1))
                    v.tensor_reduce(wmax[:, n:n + 1], stat_buffer(n), AX.X, ALU.max,
                                    apply_absolute_value=True).then_inc(wmax_taken, 1)
                taken[0] += count

            def turns(dst, steps, offset):
                return own.inc(v.tensor_scalar(dst, turn, float(steps), C["off"][:, offset:offset + 1], ALU.mult, ALU.add))

            for k, steps in enumerate((1, 1, NT)):
                turns(trig1[:, k], steps, 3 + k)
            own.sync()
            fraction(trig1, scr.rearrange("p d b -> p (d b)")[:, 0:3 * D].rearrange("p (k d) -> p k d", k=3),
                     frac1_ready, 1)
            for k in range(2):
                for b in range(TB):
                    turns(ytab[:, k, :, b], b, 1 + k)
                own.sync()
                fraction(ytab[:, k], scr, yfrac_ready, k + 1)
            dve.wait_ge(t2_ps, 1)
            v.tensor_copy(t2.rearrange("p q b s -> p (q b s)"), pf[0:48, 0:2048]).then_inc(t2_sb, 1)
            dve.wait_ge(sin1_ready, 1)
            dve.wait_ge(env1_ready, 1)
            own.inc(v.tensor_tensor(sm[:, 12], sm[:, 12], trig1[:, 2], ALU.mult))
            own.inc(v.tensor_tensor(sm[:, 1], sm[:, 8], trig1[:, 0], ALU.mult))
            own.link(v.tensor_tensor(sm[:, 2], sm[:, 8], trig1[:, 1], ALU.mult))
            own.link(v.tensor_scalar(sm[:, 1], sm[:, 1], -1.0, None, ALU.add))
            for n, (x, y) in enumerate(((sm[:, 1], AR), (sm[:, 2], AI), (sm[:, 2], AR), (sm[:, 1], AI))):
                own.inc(v.tensor_tensor(sm[:, 4 + n], x, y, ALU.mult))
            own.sync()
            own.inc(v.tensor_tensor(sm[:, 3], sm[:, 4], sm[:, 5], ALU.add))
            own.link(v.tensor_tensor(sm[:, 7], sm[:, 6], sm[:, 7], ALU.subtract))
            own.inc(v.tensor_tensor(sm[:, 3], sm[:, 3], sm[:, 0], ALU.mult))
            own.link(v.tensor_tensor(sm[:, 4], sm[:, 7], sm[:, 0], ALU.mult))
            dve.wait_ge(ysin_ready, 2)
            dve.wait_ge(yenv_ready, 1)
            for k in range(2):
                own.inc(v.tensor_tensor(ytab[:, k], ytab[:, k], bc(sm[:, 3 + k], 2, TB), ALU.mult))
            own.sync()
            own.link(v.tensor_tensor(ytab[:, 0], ytab[:, 0], ytab[:, 1], ALU.add))
            own.link(v.tensor_tensor(ytab[:, 0], ytab[:, 0], ye, ALU.mult))
            v.tensor_tensor(sm[:, 13], sm[:, 12], ytab[:, 0, :, 0], ALU.mult).then_inc(ytab_ready, 1)

            def part(k):
                if k >= 2:
                    dve.wait_ge(xtab_ready, k - 1)
                for a in range(XP):
                    turns(xe[:, k % 2, :, a], TB * (k * XP + a), 0)
                own.sync()
                fraction(xe[:, k % 2], scr, xfrac_ready, k + 1)

            def part_done(k):
                dve.wait_ge(xsin_ready, k + 1)
                dve.wait_ge(xtab_ready, k)
                v.tensor_tensor(xtab[:, :, k * XP:(k + 1) * XP], xtab[:, :, k * XP:(k + 1) * XP], xe[:, k % 2],
                                ALU.mult).then_inc(xtab_ready, 1)

            def norm(j, np_, src, dst):
                return v.tensor_scalar(dst, src, mv[0:np_, j, 0:1], rstd[0:np_, j:j + 1], ALU.subtract, ALU.mult)

            roots = [0]

            def root(np_, *tiles, meanwhile=None):
                assert (np_, tiles) == ROOTS[roots[0]]
                for j0, j1 in tiles:
                    ins = v.tensor_scalar(veps[0:np_, j0:j1], mv[0:np_, j0:j1, 1], EPS, None, ALU.add)
                roots[0] += 1
                ins.then_inc(veps_ready, 1)
                if meanwhile:
                    meanwhile()
                dve.wait_ge(rstd_ready, roots[0])

            dve.wait_ge(zs_ps, 1)
            v.tensor_copy(z_shared[ROW0:P, :], ps[ROW0:P, 6, 0:D]).then_inc(zs_sb, 1)
            part(0)
            dve.wait_ge(zs_sb, 1)
            dve.wait_ge(z_ps, 1)
            dve.wait_ge(z_sb, 1)
            v.tensor_tensor(zt[ROW0:P].rearrange("p (g b) d -> p g b d", b=2),
                            ps[ROW0:P, 0:4, 0:2 * D].rearrange("p g (b d) -> p g b d", b=2),
                            bc(bc(z_shared[ROW0:P, :], 1, 2), 1, 4), ALU.add).then_inc(z_sb, 1)
            part(1)
            part(2)
            part(3)
            part_done(2)
            part_done(3)
            for b in range(B):
                dve.wait_ge(h_sb, b // 2 + 1)
                own.inc(v.bn_stats(stats[:, b], h[:, 0, b]))
            own.sync()
            for b in range(B):
                own.inc(v.bn_aggr(mv[:, b], stats[:, b]))
            own.sync()
            for c in range(B // 2):
                dve.wait_ge(h_sb, 4 + c + 1)
                for b in (2 * c, 2 * c + 1):
                    own.inc(v.bn_stats(stats[:, 8 + b], h[:, 1, b]))
                own.sync()
                for b in (2 * c, 2 * c + 1):
                    own.inc(v.bn_aggr(mv[:, 8 + b], stats[:, 8 + b]))
                own.sync()
                root(P, (2 * c, 2 * c + 2), (8 + 2 * c, 10 + 2 * c), meanwhile=lambda: weight_max(1))
                for half in range(2):
                    for b in (2 * c, 2 * c + 1):
                        ins = norm(8 * half + b, P, h[:, half, b], u[:, half, b])
                ins.then_inc(u_ready, 1)
            dve.wait_ge(h_sb, 9)
            own.link(v.bn_stats(stats[0:B, 16], h_last[:, :]))
            own.link(v.bn_aggr(mv[0:B, 16], stats[0:B, 16]))
            root(B, (16, 17), meanwhile=lambda: weight_max(1))
            own.link(norm(16, B, h_last[:, :], u_last[:, :]))
            weight_max(2)
            dve.wait_ge(kps_ready, 1)
            v.tensor_tensor(kmask.rearrange("p (g c) b -> p g c b", c=CG),
                            pf[:, 2048:2048 + D * TB].rearrange("p (g c b) -> p g c b", c=CG, b=TB),
                            bc(bc(C["cmask"], 1, NG), 3, TB), ALU.mult).then_inc(ksb_ready, 1)
            weight_max(2 * STAT_PIECES - taken[0])
            assert taken[0] == 2 * STAT_PIECES
            dve.wait_ge(wmax_taken, 2 * STAT_PIECES)
            v.tensor_reduce(wmax[:, 2 * STAT_PIECES:], wmax[:, 0:2 * STAT_PIECES].rearrange("p (w n) -> p w n", w=2), AX.X,
                            ALU.max).then_inc(wmax_ready, 1)
            own.inc(v.tensor_copy(ident16[:, :], ident))
            dve.wait_ge(khat_ready, 1)
            own.inc(v.tensor_tensor(k0u[:, 1], k0u[:, 1], k0[:, 1], ALU.mult))
            own.inc(v.tensor_tensor(k0u[:, 0], u_last[:, :], k0[:, 0], ALU.mult))

            def low_parts(*pieces):
                for n in pieces:
                    assert n in VEC_PIECES
                    dve.wait_ge(piece_high, n + 1)
                    high, low, scale = piece_parts(n)
                    v.scalar_tensor_tensor(out=low, in0=piece_buffer(n), scalar=scale, in1=high, op0=ALU.mult,
                                           op1=ALU.subtract).then_inc(low_vec, 1)

            def scales():
                dve.wait_ge(wmax_in, 16)
                own.link(v.tensor_reduce(wsc[:, 0:2], wmax_all.rearrange("p (q w) -> p w q", w=2), AX.X, ALU.max))
                own.link(v.tensor_scalar(wsc_i[:, 0:2], wsc_i[:, 0:2], 23, None, ALU.arith_shift_right))
                own.link(v.tensor_scalar(wsc_i[:, 0:2], wsc_i[:, 0:2], 72, 198, ALU.max, ALU.min))
                own.inc(v.tensor_scalar(wsc_i[:, 2:4], wsc_i[:, 0:2], -1, 262, ALU.mult, ALU.add))
                own.inc(v.tensor_scalar(wsc_i[:, 4:5], wsc_i[:, 0:1], -8, None, ALU.add))
                own.inc(v.tensor_scalar(wsc_i[:, 5:6], wsc_i[:, 0:1], -1, 261, ALU.mult, ALU.add))
                own.inc(v.tensor_tensor(wsc_i[:, 6:7], wsc_i[:, 0:1], wsc_i[:, 1:2], ALU.add))
                own.sync()
                own.link(v.tensor_scalar(wsc_i[:, 6:7], wsc_i[:, 6:7], -142, None, ALU.add))
                v.tensor_scalar(wsc_i[:, 9:14], wsc_i[:, 2:7], 23, None, ALU.arith_shift_left).then_inc(scale_ready, 1)

            for c in range(B // 2):
                dve.wait_ge(uhat_ps, c + 1)
                if c >= 2:
                    dve.wait_ge(yhat_ready, c - 1)
                base = 4 * (c % 2)
                for n, (x, y) in enumerate(((0, 0), (1, 1), (0, 1), (1, 0))):
                    src = ps[:, base + 2 * x:base + 2 * x + 2, 0:2 * D].rearrange("p f (b d) -> p f b d", b=2)
                    dst = prod[:, c % 2, n].rearrange("p (f b d) -> p f b d", f=2, b=2)
                    ins = v.tensor_tensor(dst, src, bc(khat[:, 2 * y:2 * y + 2, :], 2, 2), ALU.mult)
                ins.then_inc(prod_ready, 1)
                if c == 0:
                    scales()
                    dve.wait_ge(scale_ready, 1)
                low_parts(*((0,), (1,), (2,), (3, 4))[c])

            own.inc(v.memset(lg[:, 2 * B], 0.0))

            def last_positions():
                dve.wait_ge(ylast_ps, 1)
                own.link(v.tensor_tensor(h_last[:, :], h_last[:, :], ps[0:B, 7, 0:D], ALU.add))
                own.link(v.tensor_tensor(k0u[:, 0], k0u[:, 0], k0u[:, 1], ALU.add))
                v.tensor_tensor(h_last[:, :], h_last[:, :], k0u[:, 0], ALU.add).then_inc(h2last_ready, 1)
                dve.wait_ge(h2last_ready, 1)
                own.link(v.bn_stats(stats[0:B, 16], h_last[:, :]))
                own.link(v.bn_aggr(mv[0:B, 16], stats[0:B, 16]))
                root(B, (16, 17))
                norm(16, B, h_last[:, :], xg[0:B, 16, :]).then_inc(xlast_ready, 1)

            for c in range(B // 2):
                if c == 3:
                    last_positions()
                dve.wait_ge(y_ps, 2 * c + 2)
                for lt in range(2):
                    hv = h[:, lt, 2 * c:2 * c + 2, :].rearrange("p b d -> p (b d)")
                    v.tensor_tensor(hv, hv, ps[:, 2 * (c % 2) + lt, 0:2 * D], ALU.add).then_inc(h2_ready, 1)
                dve.wait_ge(h2_ready, 2 * c + 2)
                for lt in range(2):
                    for b in (2 * c, 2 * c + 1):
                        own.inc(v.bn_stats(stats[:, 8 * lt + b], h[:, lt, b]))
                own.sync()
                for lt in range(2):
                    for b in (2 * c, 2 * c + 1):
                        own.inc(v.bn_aggr(mv[:, 8 * lt + b], stats[:, 8 * lt + b]))
                own.sync()
                root(P, (2 * c, 2 * c + 2), (8 + 2 * c, 10 + 2 * c),
                     meanwhile=lambda: low_parts(*((7,), (10,), (11,), (13,))[c]))
                if c == 0:
                    dve.wait_ge(low_vec, 5)
                for lt in range(2):
                    for b in (2 * c, 2 * c + 1):
                        norm(8 * lt + b, P, h[:, lt, b], xg[:, 8 * lt + b, :]).then_inc(x_ready, 1)
                low_parts(*((8,), (), (), (14,))[c])
            v.memset(xs, 0.0).then_inc(xs_clear, 1)
            own.inc(v.tensor_copy(iota16, C["iota_s"]))
            own.inc(v.tensor_copy(ids16, C["ids"]))

            own.inc(v.tensor_copy(ltri16[:, :], C["ltri"]))
            own.inc(v.memset(ones16[:, :], 1.0))
            own.inc(v.memset(ohb16[:, TILES], 0.0))
            dve.wait_ge(logit_ps, 1)
            own.inc(v.tensor_copy(lg[:, 0:2 * B].rearrange("p k e -> p (k e)"), ps[:, 6, 0:2 * B * NE]))
            own.link(v.tensor_copy(lg[0:B, 2 * B], ps[0:B, 6, 2 * B * NE:TILES * NE]))
            ew = bc(C["ew"], 1, TILES)

            def pick(src, top, oh):
                own.link(v.tensor_reduce(top, src, AX.X, ALU.max))
                own.link(v.tensor_tensor(rt[:, 0], src, bc(top, 2, NE), ALU.is_equal))
                own.link(v.tensor_tensor(rt[:, 0], rt[:, 0], ew, ALU.mult))
                own.link(v.tensor_reduce(rs[:, 3], rt[:, 0], AX.X, ALU.max))
                own.link(v.tensor_tensor(oh, ew, bc(rs[:, 3], 2, NE), ALU.is_equal))

            pick(lg[:, :, :], rs[:, 0], oh1[:, :, :])
            own.link(v.scalar_tensor_tensor(out=rt[:, 1], in0=oh1[:, :, :], scalar=LOWEST, in1=lg[:, :, :],
                                            op0=ALU.mult, op1=ALU.add))
            pick(rt[:, 1], rs[:, 1], oh2[:, :, :])
            v.tensor_tensor(rs[:, 4], rs[:, 1], rs[:, 0], ALU.subtract).then_inc(gap_ready, 1)
            own.link(v.tensor_tensor(rt[:, 0], oh1[:, :, :], oh2[:, :, :], ALU.add))
            v.tensor_tensor(ohb16[:, 0:TILES], rt[:, 0], bc(C["valid"], 2, NE), ALU.mult).then_inc(oh_ready, 1)
            dve.wait_ge(gexp_ready, 1)
            own.link(v.tensor_scalar(rs[:, 6], rs[:, 5], 1.0, None, ALU.add))
            own.link(v.reciprocal(rs[:, 7], rs[:, 6]))
            own.link(v.tensor_scalar(rs[:, 7], rs[:, 7], out_back, None, ALU.mult))
            own.link(v.tensor_tensor(rs[:, 8], rs[:, 5], rs[:, 7], ALU.mult))
            own.inc(v.tensor_tensor(rt[:, 1], oh1[:, :, :], bc(rs[:, 7], 2, NE), ALU.mult))
            own.link(v.tensor_tensor(rt[:, 2], oh2[:, :, :], bc(rs[:, 8], 2, NE), ALU.mult))
            v.tensor_tensor(xr[:, :, D:XW], rt[:, 1], rt[:, 2], ALU.add).then_inc(gates_ready, 1)
            dve.wait_ge(rank_ps, 1)
            rank = ps[:, 7, 0:(TILES + 1) * NE].rearrange("p (k e) -> p k e", e=NE)
            own.link(v.tensor_scalar(cnt_i[:, :], rank[:, TILES], float(P - 1), None, ALU.add))
            own.link(v.tensor_scalar(cnt_i[:, :], cnt_i[:, :], 7, None, ALU.arith_shift_right))
            own.inc(v.memset(cnt[:, 0], 1.0))
            own.link(v.tensor_copy(cnt[:, 1], cnt_i[:, :]))
            own.link(v.tensor_tensor_scan(cnt[:, 2], cnt[:, 0], cnt[:, 1], 0.0, ALU.mult, ALU.add))
            own.link(v.tensor_tensor(cnt[:, 3], cnt[:, 2], cnt[:, 1], ALU.subtract))
            own.link(v.tensor_scalar(cnt[:, 3], cnt[:, 3], float(P), None, ALU.mult))
            own.link(v.tensor_tensor(rt[:, 0], rank[:, 0:TILES], bc(cnt[:, 3], 1, TILES), ALU.add))
            own.inc(v.tensor_tensor(rt[:, 1], rt[:, 0], oh1[:, :, :], ALU.mult))
            own.link(v.tensor_tensor(rt[:, 2], rt[:, 0], oh2[:, :, :], ALU.mult))
            for n in range(2):
                own.inc(v.tensor_reduce(pos[:, n], rt[:, 1 + n], AX.X, ALU.add))
            own.sync()
            own.link(v.tensor_copy(pos_i[:, :, :], pos[:, :, :]))
            own.inc(v.tensor_scalar(blk_i[:, :, :], pos_i[:, :, :], 7, None, ALU.arith_shift_right))
            own.link(v.tensor_scalar(slt_i[:, :, :], pos_i[:, :, :], P - 1, None, ALU.bitwise_and))
            own.inc(v.tensor_copy(blk_f[:, :], blk_i[:, :, :].rearrange("p k j -> p (k j)")))
            own.link(v.tensor_copy(slt_f[:, :], slt_i[:, :, :].rearrange("p k j -> p (k j)")))
            own.link(v.tensor_tensor(ohb, bc(iota16[:, 0:NBLK], 1, 2 * TILES), bc(blk_f[:, :], 2, NBLK), ALU.is_equal))
            own.inc(v.tensor_tensor(mvb, bc(ohb, 2, 2), bc(ids16.rearrange("p (k c) -> p k c", c=2), 3, NBLK), ALU.mult))
            for n in range(2):
                picks = slice(n * TILES, (n + 1) * TILES)
                v.tensor_tensor(ohs[:, picks], bc(iota16, 1, TILES), bc(slt_f[:, picks], 2, P),
                                ALU.is_equal).then_inc(pick_ready, 1)
            own.link(v.tensor_tensor(ge_t, bc(C["iota_b"], 2, NE), bc(cnt[:, 2], 1, NBLK), ALU.is_ge))
            own.link(v.tensor_reduce(blk_e[:, :], ge_t, AX.X, ALU.add))
            own.link(v.tensor_scalar(blk_e[:, :], blk_e[:, :], float(NE - 1), None, ALU.min))
            v.tensor_copy(blk_ei[:, :], blk_e[:, :]).then_inc(expert_ready, 1)
            own.inc(v.tensor_tensor(gsel_e, bc(C["eidx"], 1, NBLK), bc(blk_e[:, :], 2, NE), ALU.is_equal))
            dve.wait_ge(slot_ps, 1)
            own.link(v.tensor_copy(slotv[:, :], ps[:, 0, 0:2 * NBLK]))
            sv = slotv[:, :].rearrange("p (c s) -> p c s", c=2)
            own.link(v.scalar_tensor_tensor(out=idx_f[:, :], in0=sv[:, 1], scalar=256.0, in1=sv[:, 0], op0=ALU.mult,
                                            op1=ALU.add))
            own.link(v.tensor_scalar(idx_f[:, :], idx_f[:, :], -1.0, None, ALU.add))
            own.link(v.tensor_copy(idx[:, :], idx_f[:, :]))
            v.tensor_copy(gcol[:, :], idx[:, 0:4]).then_inc(idx_ready, 1)

            def turned(i, par):
                dve.wait_ge(bt_ps, i + 1)
                v.tensor_copy(x3[:, par], x3_ps).then_inc(bt_sb, 1)

            def output(i, r, first, more=True):
                v.tensor_tensor(gsel[:, r % 2], xs[:, r, D:XW], gsel_e[:, bass.ds(i, 1), :].rearrange("p o e -> p (o e)"),
                                ALU.mult).then_inc(gate_seen, 1)
                dve.wait_ge(gate_seen, 2 * i + 1)
                v.tensor_reduce(gate[:, r % 2:r % 2 + 1], gsel[:, r % 2], AX.X, ALU.add).then_inc(gate_seen, 1)
                dve.wait_ge(gate_seen, 2 * i + 2)
                dve.wait_ge(pj_ps, i + 1)
                if not first:
                    dve.wait_ge(added, 16 * (i - 1))
                v.tensor_copy(scol[:, r:r + 1], idx[:, bass.ds(i, 1)])
                if more:
                    v.tensor_copy(gcol[:, r:r + 1], idx[:, bass.ds(i + 4, 1)])
                v.tensor_scalar(o_sb[:, r % 2], ps[:, 5 + r % 2, 0:D], gate[:, r % 2:r % 2 + 1], None,
                                ALU.mult).then_inc(o_ready, 1)

            def hidden(i, par):
                dve.wait_ge(hh_ready, i + 1)
                v.scalar_tensor_tensor(out=hl[:, par].rearrange("p (k n) -> p k n", k=2), in0=ps[:, 2:4, 0:H // 2],
                                       scalar=h_scale, in1=hh[:, par].rearrange("p (k n) -> p k n", k=2),
                                       op0=ALU.mult, op1=ALU.subtract).then_inc(hl_ready, 1)

            def vstep(q, r, more=True, first=False, gather_more=True):
                i = 4 * q + r + 1
                if more:
                    turned(i + 1, r % 2)
                output(i - 1, r, first, gather_more)
                hidden(i, (r + 1) % 2)

            turned(0, 0)
            turned(1, 1)
            hidden(0, 0)
            for r in range(2):
                vstep(0, r, first=True)
            for r in range(2, 4):
                vstep(0, r)
            with dve.Fori(1, NBLK // 4 - 1) as q:
                for r in range(4):
                    vstep(q, r)
            for r in range(3):
                vstep(NBLK // 4 - 1, r, more=r < 2, gather_more=False)
            output(NBLK - 1, 3, False, False)

        @block.tensor
        def _(pe):
            mm = nc.tensor.matmul
            pe.wait_ge(const_in, 16)
            pe.wait_ge(raw2_in, 32)
            for q in range(2):
                for b in range(B):
                    k = (q * B + b) * P
                    ins = nc.tensor.transpose(pf[0:48, k:k + P], raw2[:, q, b * 48:(b + 1) * 48], ident)
            ins.then_inc(t2_ps, 1)
            pe.wait_ge(byb1_ready, 1)
            for b in range(B):
                k = 2048 + b * P
                ins = nc.tensor.transpose(pf[0:96, k:k + P], byb1[:, b].rearrange("p g c -> p (g c)"), ident)
            ins.then_inc(t1_ps, 1)
            pe.wait_ge(tokw_in, 16 * TOKEN_LOADS)
            pe.wait_ge(t2_sb, 1)
            for g in range(GP):
                q, gg = g // 8, g % 8
                ins = mm(ps[0:EMB, 7, 0:B * 16], lhsT=w2[:, g, :],
                         rhs=t2[:, q, :, gg * 16:(gg + 1) * 16], start=g == 0, stop=g == GP - 1)
            ins.then_inc(y2_ps, 1)
            pe.wait_ge(t1_sb, 1)
            for k in range(2):
                ins = mm(ps[0:EMB, 6, :], lhsT=w1[:, k, :], rhs=t1[:, :, k * 64:(k + 1) * 64], start=k == 0, stop=k == 1)
            ins.then_inc(y1_ps, 1)
            def turn_level0(half):
                pe.wait_ge(byb0_ready, half + 1)
                for b in range(B):
                    k = T0_BANK[half] * 512 + b * P
                    ins = mm(pf[ROW0:ROW2, k:k + P], lhsT=byb0[:, half, b], rhs=ident, start=True, stop=True)
                ins.then_inc(t0_ps, 1)

            pe.wait_ge(y1_sb, 1)
            pe.wait_ge(y2_sb, 1)
            mm(ps[ROW0:P, 6, 0:D], lhsT=w0[:, :], rhs=wf0[:, :], start=True, stop=True).then_inc(zs_ps, 1)
            turn_level0(0)
            for b in range(B):
                mm(ps[0:ROW0, b // 2, (b % 2) * D:(b % 2) * D + D], lhsT=y1t[:, b, :], rhs=wf[:, 0, :],
                   start=True, stop=True)
                ins = mm(ps[ROW0:P, b // 2, (b % 2) * D:(b % 2) * D + D], lhsT=y2t[:, b, :], rhs=wf[:, 1, :],
                         start=True, stop=True)
            ins.then_inc(z_ps, 1)
            pe.wait_ge(z_sb, 2)
            turn_level0(1)

            def fused(half):
                pe.wait_ge(t0_sb, half + 1)
                for c in range(4):
                    for m in range(2):
                        at = P * half
                        ins = mm(ps[:, 4 - 4 * half + c, m * D:(m + 1) * D], lhsT=tok[:, 2 * c + m, at:at + P],
                                 rhs=zt[:, 2 * c + m, :], start=True, stop=True)
                    ins.then_inc(h_ps, 1)

            pe.wait_ge(edge_zero, 3)
            fused(0)
            fused(1)
            pe.wait_ge(last_ready, 1)
            pe.wait_ge(h_sb, 5)
            for b in range(B):
                ins = mm(ps[0:B, 0, 0:D], lhsT=last_col[:, b, :], rhs=zt[:, b, :], start=b == 0, stop=b == B - 1)
            ins.then_inc(h_ps, 1)
            pe.wait_ge(ytab_ready, 1)
            pe.wait_ge(xtab_ready, 4)
            pe.wait_ge(h_sb, 8)
            for g in range(NG):
                ins = mm(pf[:, 2048 + g * CG * TB:2048 + (g + 1) * CG * TB],
                         lhsT=xtab[:, CG * g:CG * g + CG, :].rearrange("p c a -> p (c a)"),
                         rhs=ytab[:, 0, CG * g:CG * g + CG, :], start=True, stop=True)
            ins.then_inc(kps_ready, 1)

            def transform(c):
                pe.wait_ge(u_ready, c + 1)
                if c >= 2:
                    pe.wait_ge(prod_ready, c - 1)
                for kt in range(KT):
                    for m in range(2):
                        ins = mm(ps[:, 4 * (c % 2) + kt, 0:2 * D], lhsT=fwd[:, m, kt * P:(kt + 1) * P],
                                 rhs=u[:, m, 2 * c:2 * c + 2, :], start=m == 0, stop=m == 1)
                ins.then_inc(uhat_ps, 1)

            pe.wait_ge(four_in, 16 * 5)
            pe.wait_ge(h_sb, 9)
            transform(0)
            pe.wait_ge(ksb_ready, 1)

            for kt in range(KT):
                dst = ps[:, 4 + kt // 2, (kt % 2) * D:(kt % 2) * D + D]
                for b in range(TB):
                    mm(dst, lhsT=fwd_k[:, b, kt * P:(kt + 1) * P], rhs=kmask[:, :, b], start=b == 0, stop=b == TB - 1)
            mm(ps[0:B, 6, 0:D], lhsT=C["half0"], rhs=ytab[:, 0, :, 0], start=True, stop=True)
            mm(ps[0:B, 6, D:2 * D], lhsT=C["ones"], rhs=sm[:, 13], start=True, stop=True)
            mm(ps[0:B, 7, 0:D], lhsT=C["row0"], rhs=u[:, 0, 0, :], start=True, stop=True).then_inc(khat_ps, 1)
            pe.wait_ge(khat_ready, 1)
            for c in range(1, B // 2):
                transform(c)

            def turn_x(c):
                if c < B // 2:
                    pe.wait_ge(x_ready, 4 * c + 4)
                else:
                    pe.wait_ge(xlast_ready, 1)
                if c:
                    pe.wait_ge(xt_sb, c)
                w = P if c < B // 2 else B
                for m in range(4 if c < B // 2 else 1):
                    j = TILE_ORDER[4 * c + m]
                    nc.tensor.transpose(ps[:, 4, m * P:m * P + w], xg[0:w, j, 0:P], ident[0:w, 0:w])
                    ins = nc.tensor.transpose(ps[0:D2, 5, m * P:m * P + w], xg[0:w, j, P:D], ident[0:w, 0:w])
                ins.then_inc(xt_ps, 1)

            def logits(c):
                pe.wait_ge(xt_sb, c + 1)
                w = P if c < B // 2 else B
                for m in range(4 if c < B // 2 else 1):
                    j = TILE_ORDER[4 * c + m]
                    mm(ps[0:w, 6, j * NE:(j + 1) * NE], lhsT=xt[:, 4 * c + m, 0, 0:w], rhs=wga[:, :], start=True, stop=False)
                    ins = mm(ps[0:w, 6, j * NE:(j + 1) * NE], lhsT=xt[0:D2, 4 * c + m, 1, 0:w], rhs=wgb[:, :],
                             start=False, stop=True)
                return ins

            def last_positions():
                sgn = C["sgn"].rearrange("p (b c) -> p b c", b=B)
                pe.wait_ge(yhat_ready, B // 2)
                for b in range(B):
                    for f in range(2):
                        ins = mm(ps[0:B, 7, 0:D], lhsT=sgn[:, b, :], rhs=yhat[:, 2 + f, b, :],
                                 start=(b, f) == (0, 0), stop=(b, f) == (B - 1, 1))
                ins.then_inc(ylast_ps, 1)

            for c in range(B // 2):
                if c == 3:
                    last_positions()
                pe.wait_ge(yhat_ready, c + 1)
                if c == 0:
                    pe.wait_ge(prod_ready, 3)
                if c >= 2:
                    pe.wait_ge(h2_ready, 2 * (c - 1))
                for lt in range(2):
                    for kt in range(KT):
                        ins = mm(ps[:, 2 * (c % 2) + lt, 0:2 * D], lhsT=inv[:, kt, lt * P:(lt + 1) * P],
                                 rhs=yhat[:, kt, 2 * c:2 * c + 2, :], start=kt == 0, stop=kt == KT - 1)
                    ins.then_inc(y_ps, 1)
                if c >= 2:
                    turn_x(c - 2)
                    logits(c - 2)
            turn_x(B // 2 - 2)
            for c in range(B // 2 - 1, B // 2 + 1):
                turn_x(c)
                logits(c - 1)
            logits(B // 2).then_inc(logit_ps, 1)
            pe.wait_ge(oh_ready, 1)
            mm(ps[:, 7, 0:(TILES + 1) * NE], lhsT=ltri16[:, :], rhs=ohb16[:, :, :].rearrange("p k e -> p (k e)"),
               start=True, stop=False)
            for j in range(TILES):
                n = TILES - j
                ins = mm(ps[:, 7, (j + 1) * NE:(TILES + 1) * NE], lhsT=ones16[:, :], rhs=bc(ohb16[:, j], 1, n),
                         start=False, stop=j == TILES - 1)
            ins.then_inc(rank_ps, 1)
            for k in range(2 * TILES):
                if k % TILES == 0:
                    pe.wait_ge(pick_ready, k // TILES + 1)
                ins = mm(ps[:, 0, 0:2 * NBLK], lhsT=ohs[:, k, :], rhs=mvb[:, k].rearrange("p c s -> p (c s)"),
                         start=k == 0, stop=k == 2 * TILES - 1)
            ins.then_inc(slot_ps, 1)

            def turn_rows(q, r):
                pe.wait_ge(xs_in[r], 16 * (q + 1))
                for k in range(3):
                    ins = nc.tensor.transpose(x3_ps[:, k * P:(k + 1) * P], xs16[:, r, k * P:(k + 1) * P], ident16[:, :])
                ins.then_inc(bt_ps, 1)

            def up(i, e, par):
                pe.wait_ge(bt_sb, i + 1)
                for half in range(2):
                    for n, (x, w) in enumerate(((0, 0), (2, 0), (0, 1), (1, 2), (1, 3))):
                        ins = mm(ps[:, half, 0:H // 2], lhsT=x3[:, par, x * P:(x + 1) * P],
                                 rhs=fc16[:, bass.ds(e * H + (w * N_FC + half * (H // 2)), H // 2)],
                                 start=n == 0, stop=n == 4)
                ins.then_inc(fc_ps, 1)

            def down(i, e, par, first):
                pe.wait_ge(hh_ready, i + 1)
                if not first:
                    pe.wait_ge(o_ready, i - 1)
                for k in range(HT):
                    mm(ps[:, 5 + par, 0:D], lhsT=hh[:, par, k * P:(k + 1) * P],
                       rhs=pj16[:, bass.ds(e * HT * D + (N_PJ + k * D), D)], start=k == 0, stop=False)
                pe.wait_ge(hl_ready, i + 1)
                for k in range(HT):
                    for hidden in (hh, hl):
                        ins = mm(ps[:, 5 + par, 0:D], lhsT=hidden[:, par, k * P:(k + 1) * P],
                                 rhs=pj16[:, bass.ds(e * HT * D + k * D, D)], start=False,
                                 stop=k == HT - 1 and hidden is hl)
                ins.then_inc(pj_ps, 1)

            def turn_hidden(i, par):
                pe.wait_ge(hs_ready, i + 1)
                for k in range(HT):
                    ins = nc.tensor.transpose(ps[:, 2 + k // 3, (k % 3) * P:(k % 3 + 1) * P],
                                              hs[:, par, k * P:(k + 1) * P], ident)
                ins.then_inc(ht_ps, 1)

            def expert(i):
                return pe.value_load(blk_ei[0:1, bass.ds(i, 1)], min_val=0, max_val=NE - 1)

            def psteps(q, start, stop, first=False, last=False):
                e_before, e = expert(8 * q + start - 1), expert(8 * q + start)
                for r in range(start, stop):
                    i = 8 * q + r
                    up(i, e, r % 2)
                    e_next = expert(i + 1) if r + 1 < stop else None
                    if not last or r + 1 < stop:
                        turn_rows(2 * q + (r + 1) // 4, (r + 1) % 4)
                    down(i - 1, e_before, (r + 1) % 2, first and r <= 2)
                    turn_hidden(i, r % 2)
                    e_before, e = e, e_next

            pe.wait_ge(expert_ready, 1)
            pe.wait_ge(idx_ready, 1)
            pe.wait_ge(low_vec, len(VEC_PIECES))
            pe.wait_ge(low_pool, len(POOL_PIECES))
            turn_rows(0, 0)
            up(0, expert(0), 0)
            turn_rows(0, 1)
            turn_hidden(0, 0)
            psteps(0, 1, 8, first=True)
            with pe.Fori(1, NBLK // 8 - 1) as q:
                psteps(q, 0, 8)
            psteps(NBLK // 8 - 1, 0, 8, last=True)
            down(NBLK - 1, expert(NBLK - 1), 1, False)



def kernel(**inputs):
    import concourse.bacc as bacc
    from concourse.bass_utils import run_bass_kernel_spmd

    a = {k: np.asarray(v) for k, v in inputs.items()}
    x = a["x"]

    def patches(p):
        n = IMG // p
        return x.reshape(B, CH, n, p, n, p).transpose(2, 4, 0, 3, 5, 1).reshape(n * n, B * p * p * CH)

    arrays = {
        "px0": patches(1), "px1": patches(2), "px2": patches(4),
        "id0": a["L0_tok_idx0"].reshape(2, P, GP).transpose(1, 0, 2).reshape(P, 2 * GP),
        "id1": a["L0_tok_idx1"].reshape(64, 2, 8).transpose(1, 0, 2).reshape(P, 8),
        "id2": a["L0_tok_idx2"].reshape(16, 2, 8).transpose(2, 0, 1).reshape(P, 2),
        "w0": np.concatenate([np.concatenate([a["L0_tok_W0"], np.repeat(a["L0_tok_b0"][:, None], P - ROW2, 1)], 1),
                              (np.arange(P - ROW0) >= F0)[None, :].astype(np.float32)]),
        "wf0": np.concatenate([a["L0_tok_Wf"].T[0:EMB], a["L0_tok_bf"][None, :]]),
        "w1": a["L0_tok_W1"].T.reshape(2, 96, EMB).transpose(1, 0, 2),
        "w2": a["L0_tok_W2"].T.reshape(GP, 48, EMB).transpose(1, 0, 2),
        "tb": np.stack([a["L0_tok_b1"], a["L0_tok_b2"]], 1),
        "wf": a["L0_tok_Wf"].T.reshape(3, EMB, D)[1:].transpose(1, 0, 2),
        "cls": a["cls_tok"].reshape(1, D),
        "a_real": a["L0_attn_A_real"].T, "a_imag": a["L0_attn_A_imag"].T,
        "b_mat": a["L0_attn_B_mat"].T, "c_mat": a["L0_attn_C_mat"].T,
        "log_delta": a["L0_attn_log_delta"],
        "w_gate": a["L0_ffn_w_gate"],
        "w_fc": a["L0_ffn_w_fc"].reshape(D, H, NE).transpose(0, 2, 1).reshape(D, NE * H),
        "w_proj": a["L0_ffn_w_proj"].reshape(HT, P, D, NE).transpose(1, 3, 0, 2).reshape(P, NE * HT * D),
        **shape_constants(),
    }
    arrays = {k: np.ascontiguousarray(v) for k, v in arrays.items()}
    nc = bacc.Bacc("TRN2", target_bir_lowering=False, num_devices=1)
    t = {k: nc.dram_tensor(k, v.shape, mybir.dt.from_np(v.dtype), kind="ExternalInput").ap() for k, v in arrays.items()}
    out = nc.dram_tensor("out", (B, L, D), F32, kind="ExternalOutput").ap()
    vit_layer(nc, t, out)
    r = run_bass_kernel_spmd(nc, [arrays], core_ids=[0])
    return r.results[0]["out"]
```
